# Optimizing a Trainium2 kernel written in Bass

```python
import numpy as np
import jax
import jax.numpy as jnp

def _softmax(x, axis=-1):
    return jax.nn.softmax(x, axis=axis)

def _gelu(x):
    return jax.nn.gelu(x, approximate=True)

def _silu(x):
    return jax.nn.silu(x)

def _sigmoid(x):
    return jax.nn.sigmoid(x)

def _layernorm(x, axis=-1, eps=1e-05):
    m = jnp.mean(x, axis=axis, keepdims=True)
    v = jnp.var(x, axis=axis, keepdims=True)
    return (x - m) / jnp.sqrt(v + eps)

def _scatter_add(tgt, idx, src, axis=0):
    return tgt.at[idx].add(src)

def _segment_sum(src, seg, n):
    return jax.ops.segment_sum(src, seg, n)
kernel_name = 'mk_hybrid_d1_jaxref_r8_af849f'

def setup_inputs(seed: int=0):
    np.random.seed(seed)
    _w = jnp.asarray

    def _L0_attn_a_setup():
        import jax, jax.numpy as jnp
        import numpy as np
        N_HEADS, D_HEAD, D_EMBED = (16, 64, 128)
        BATCH, SEQ = (8, 128)
        WEIGHT_ALPHA = 1.0
        key = jax.random.key(seed)
        k1, k2, k3, k4, k5 = jax.random.split(key, 5)
        scale = WEIGHT_ALPHA / np.sqrt(D_EMBED)
        x = jax.random.normal(k1, (BATCH, SEQ, D_EMBED), dtype=jnp.float32)
        W_K = scale * jax.random.normal(k2, (N_HEADS, D_HEAD, D_EMBED), dtype=jnp.float32)
        W_Q = scale * jax.random.normal(k3, (N_HEADS, D_HEAD, D_EMBED), dtype=jnp.float32)
        W_V = scale * jax.random.normal(k4, (N_HEADS, D_HEAD, D_EMBED), dtype=jnp.float32)
        W_O = scale * jax.random.normal(k5, (D_EMBED, N_HEADS * D_HEAD), dtype=jnp.float32)
        return {'x': x, 'W_K': W_K, 'W_Q': W_Q, 'W_V': W_V, 'W_O': W_O}
    _L0_attn_a_in = _L0_attn_a_setup()

    def _L0_attn_b_setup():
        import jax, jax.numpy as jnp
        import numpy as np
        B, T, D = (2, 512, 128)
        H, DK, DV = (8, 128, 128)
        INTER = 512
        CHUNK = 128
        EPS = 1e-05

        def rmsnorm(x, w, eps=EPS):
            return x * jax.lax.rsqrt(jnp.mean(x * x, axis=-1, keepdims=True) + eps) * w

        def linear_attention(x, Wq, Wk, Wv, Wo, out_norm_w):
            b, t, d = x.shape
            n = t // CHUNK
            q = (x @ Wq).reshape(b, t, H, DK).transpose(0, 2, 1, 3)
            k = (x @ Wk).reshape(b, t, H, DK).transpose(0, 2, 1, 3)
            v = (x @ Wv).reshape(b, t, H, DV).transpose(0, 2, 1, 3)
            qc = q.reshape(b, H, n, CHUNK, DK).transpose(2, 0, 1, 3, 4)
            kc = k.reshape(b, H, n, CHUNK, DK).transpose(2, 0, 1, 3, 4)
            vc = v.reshape(b, H, n, CHUNK, DV).transpose(2, 0, 1, 3, 4)
            causal = jnp.tril(jnp.ones((CHUNK, CHUNK), dtype=bool))

            def step(S, qkv):
                qb, kb, vb = qkv
                attn = jnp.einsum('bhid,bhjd->bhij', qb, kb)
                attn = jnp.where(causal, attn, 0.0)
                o = jnp.einsum('bhij,bhjv->bhiv', attn, vb) + jnp.einsum('bhid,bhdv->bhiv', qb, S)
                S = S + jnp.einsum('bhid,bhiv->bhdv', kb, vb)
                return (S, o)
            S0 = jnp.zeros((b, H, DK, DV), x.dtype)
            _, o = jax.lax.scan(step, S0, (qc, kc, vc))
            o = o.transpose(1, 2, 0, 3, 4).reshape(b, H, t, DV)
            o = rmsnorm(o, out_norm_w)
            o = o.transpose(0, 2, 1, 3).reshape(b, t, H * DV)
            return o @ Wo
        key = jax.random.key(seed)
        ks = jax.random.split(key, 9)
        s = 0.02
        return {'hidden_states': jax.random.normal(ks[0], (B, T, D), jnp.float32), 'attn_norm_w': jnp.ones((D,), jnp.float32), 'Wq': jax.random.normal(ks[1], (D, H * DK), jnp.float32) * s, 'Wk': jax.random.normal(ks[2], (D, H * DK), jnp.float32) * s, 'Wv': jax.random.normal(ks[3], (D, H * DV), jnp.float32) * s, 'Wo': jax.random.normal(ks[4], (H * DV, D), jnp.float32) * s, 'attn_out_norm_w': jnp.ones((DV,), jnp.float32), 'mlp_norm_w': jnp.ones((D,), jnp.float32), 'Wgate': jax.random.normal(ks[5], (D, INTER), jnp.float32) * s, 'Wup': jax.random.normal(ks[6], (D, INTER), jnp.float32) * s, 'Wdown': jax.random.normal(ks[7], (INTER, D), jnp.float32) * s}
    _L0_attn_b_in = _L0_attn_b_setup()

    def _L0_ffn_setup():
        import jax, jax.numpy as jnp
        import numpy as np
        B, S, H, F, E, K = (4, 512, 128, 512, 8, 2)
        LN_EPS = 1e-05
        key = jax.random.key(seed)
        kx, kr, k1, k2 = jax.random.split(key, 4)
        x = jax.random.normal(kx, (B, S, H), dtype=jnp.float32)
        gamma = jnp.ones((H,), jnp.float32)
        beta = jnp.zeros((H,), jnp.float32)
        Wr = jax.random.normal(kr, (H, E), jnp.float32) * 0.02
        br = jnp.zeros((E,), jnp.float32)
        W1 = jax.random.normal(k1, (E, H, F), jnp.float32) * (1.0 / np.sqrt(H))
        b1 = jnp.zeros((E, F), jnp.float32)
        W2 = jax.random.normal(k2, (E, F, H), jnp.float32) * (1.0 / np.sqrt(F))
        b2 = jnp.zeros((E, H), jnp.float32)
        return {'x': x, 'gamma': gamma, 'beta': beta, 'Wr': Wr, 'br': br, 'W1': W1, 'b1': b1, 'W2': W2, 'b2': b2}
    _L0_ffn_in = _L0_ffn_setup()
    _d = {'L0_attn_a_x': _L0_attn_a_in['x'], 'L0_attn_a_W_K': _L0_attn_a_in['W_K'], 'L0_attn_a_W_Q': _L0_attn_a_in['W_Q'], 'L0_attn_a_W_V': _L0_attn_a_in['W_V'], 'L0_attn_a_W_O': _L0_attn_a_in['W_O'], 'L0_attn_b_attn_norm_w': _L0_attn_b_in['attn_norm_w'], 'L0_attn_b_Wq': _L0_attn_b_in['Wq'], 'L0_attn_b_Wk': _L0_attn_b_in['Wk'], 'L0_attn_b_Wv': _L0_attn_b_in['Wv'], 'L0_attn_b_Wo': _L0_attn_b_in['Wo'], 'L0_attn_b_attn_out_norm_w': _L0_attn_b_in['attn_out_norm_w'], 'L0_attn_b_mlp_norm_w': _L0_attn_b_in['mlp_norm_w'], 'L0_attn_b_Wgate': _L0_attn_b_in['Wgate'], 'L0_attn_b_Wup': _L0_attn_b_in['Wup'], 'L0_attn_b_Wdown': _L0_attn_b_in['Wdown'], 'L0_ffn_gamma': _L0_ffn_in['gamma'], 'L0_ffn_beta': _L0_ffn_in['beta'], 'L0_ffn_Wr': _L0_ffn_in['Wr'], 'L0_ffn_br': _L0_ffn_in['br'], 'L0_ffn_W1': _L0_ffn_in['W1'], 'L0_ffn_b1': _L0_ffn_in['b1'], 'L0_ffn_W2': _L0_ffn_in['W2'], 'L0_ffn_b2': _L0_ffn_in['b2']}
    _x0 = _d['L0_attn_a_x']
    _d['L0_attn_a_x'] = jax.random.normal(jax.random.fold_in(jax.random.key(seed), 1), (8, 512, 128), dtype=_x0.dtype)
    del _x0
    return _d

def reference(L0_attn_a_x, L0_attn_a_W_K, L0_attn_a_W_Q, L0_attn_a_W_V, L0_attn_a_W_O, L0_attn_b_attn_norm_w, L0_attn_b_Wq, L0_attn_b_Wk, L0_attn_b_Wv, L0_attn_b_Wo, L0_attn_b_attn_out_norm_w, L0_attn_b_mlp_norm_w, L0_attn_b_Wgate, L0_attn_b_Wup, L0_attn_b_Wdown, L0_ffn_gamma, L0_ffn_beta, L0_ffn_Wr, L0_ffn_br, L0_ffn_W1, L0_ffn_b1, L0_ffn_W2, L0_ffn_b2):

    def _L0_attn_a_ref(x, W_K, W_Q, W_V, W_O):
        import jax, jax.numpy as jnp
        import numpy as np
        N_HEADS, D_HEAD, D_EMBED = (16, 64, 128)
        BATCH, SEQ = (8, 128)
        WEIGHT_ALPHA = 1.0
        b, seq, _ = x.shape
        d_head = W_K.shape[1]
        k = jnp.einsum('ahe,bce->bach', W_K, x)
        q = jnp.einsum('ahe,bce->bach', W_Q, x)
        v = jnp.einsum('ahe,bce->bach', W_V, x)
        scores = jnp.einsum('bach,baCh->bacC', k, q)
        mask = jnp.tril(jnp.ones((seq, seq), dtype=scores.dtype))
        masked = jnp.tril(scores) - 10000000000.0 * (1.0 - mask)
        attn = jax.nn.softmax(masked / np.sqrt(d_head), axis=-1)
        z = jnp.einsum('bach,bacC->baCh', v, attn)
        z_flat = z.transpose(0, 2, 1, 3).reshape(b, seq, -1)
        out = jnp.einsum('ef,bcf->bce', W_O, z_flat)
        return out

    def _L0_attn_b_ref(hidden_states, attn_norm_w, Wq, Wk, Wv, Wo, attn_out_norm_w, mlp_norm_w, Wgate, Wup, Wdown):
        import jax, jax.numpy as jnp
        import numpy as np
        B, T, D = (2, 512, 128)
        H, DK, DV = (8, 128, 128)
        INTER = 512
        CHUNK = 128
        EPS = 1e-05

        def rmsnorm(x, w, eps=EPS):
            return x * jax.lax.rsqrt(jnp.mean(x * x, axis=-1, keepdims=True) + eps) * w

        def linear_attention(x, Wq, Wk, Wv, Wo, out_norm_w):
            b, t, d = x.shape
            n = t // CHUNK
            q = (x @ Wq).reshape(b, t, H, DK).transpose(0, 2, 1, 3)
            k = (x @ Wk).reshape(b, t, H, DK).transpose(0, 2, 1, 3)
            v = (x @ Wv).reshape(b, t, H, DV).transpose(0, 2, 1, 3)
            qc = q.reshape(b, H, n, CHUNK, DK).transpose(2, 0, 1, 3, 4)
            kc = k.reshape(b, H, n, CHUNK, DK).transpose(2, 0, 1, 3, 4)
            vc = v.reshape(b, H, n, CHUNK, DV).transpose(2, 0, 1, 3, 4)
            causal = jnp.tril(jnp.ones((CHUNK, CHUNK), dtype=bool))

            def step(S, qkv):
                qb, kb, vb = qkv
                attn = jnp.einsum('bhid,bhjd->bhij', qb, kb)
                attn = jnp.where(causal, attn, 0.0)
                o = jnp.einsum('bhij,bhjv->bhiv', attn, vb) + jnp.einsum('bhid,bhdv->bhiv', qb, S)
                S = S + jnp.einsum('bhid,bhiv->bhdv', kb, vb)
                return (S, o)
            S0 = jnp.zeros((b, H, DK, DV), x.dtype)
            _, o = jax.lax.scan(step, S0, (qc, kc, vc))
            o = o.transpose(1, 2, 0, 3, 4).reshape(b, H, t, DV)
            o = rmsnorm(o, out_norm_w)
            o = o.transpose(0, 2, 1, 3).reshape(b, t, H * DV)
            return o @ Wo
        x = hidden_states
        h = rmsnorm(x, attn_norm_w)
        x = x + linear_attention(h, Wq, Wk, Wv, Wo, attn_out_norm_w)
        h = rmsnorm(x, mlp_norm_w)
        x = x + jax.nn.silu(h @ Wgate) * (h @ Wup) @ Wdown
        return x

    def _L0_ffn_ref(x, gamma, beta, Wr, br, W1, b1, W2, b2):
        import jax, jax.numpy as jnp
        import numpy as np
        B, S, H, F, E, K = (4, 512, 128, 512, 8, 2)
        LN_EPS = 1e-05
        residual = x
        mu = jnp.mean(x, axis=-1, keepdims=True)
        var = jnp.var(x, axis=-1, keepdims=True)
        xn = (x - mu) * jax.lax.rsqrt(var + LN_EPS) * gamma + beta
        probs = jax.nn.softmax(xn @ Wr + br, axis=-1)
        scores, idx = jax.lax.top_k(probs, K)

        def expert_fn(w):
            W1_e, b1_e, W2_e, b2_e = w
            return jax.nn.relu(xn @ W1_e + b1_e) @ W2_e + b2_e
        full = jax.lax.map(expert_fn, (W1, b1, W2, b2))
        full = jnp.moveaxis(full, 0, 2)
        c = jnp.einsum('ef,efh->eh', jax.nn.relu(b1), W2) + b2
        c_total = c.sum(axis=0)
        sel_full = jnp.take_along_axis(full, idx[..., None], axis=2)
        c_sel = c[idx]
        output = jnp.sum(scores[..., None] * (sel_full - c_sel + c_total), axis=2)
        return residual + output
    x = L0_attn_a_x
    x = x + _L0_attn_a_ref(_layernorm(x, axis=-1), L0_attn_a_W_K, L0_attn_a_W_Q, L0_attn_a_W_V, L0_attn_a_W_O)
    x = x + _L0_ffn_ref(_layernorm(x, axis=-1), L0_ffn_gamma, L0_ffn_beta, L0_ffn_Wr, L0_ffn_br, L0_ffn_W1, L0_ffn_b1, L0_ffn_W2, L0_ffn_b2)
    x = x + _L0_attn_b_ref(_layernorm(x, axis=-1), L0_attn_b_attn_norm_w, L0_attn_b_Wq, L0_attn_b_Wk, L0_attn_b_Wv, L0_attn_b_Wo, L0_attn_b_attn_out_norm_w, L0_attn_b_mlp_norm_w, L0_attn_b_Wgate, L0_attn_b_Wup, L0_attn_b_Wdown)
    x = x + _L0_ffn_ref(_layernorm(x, axis=-1), L0_ffn_gamma, L0_ffn_beta, L0_ffn_Wr, L0_ffn_br, L0_ffn_W1, L0_ffn_b1, L0_ffn_W2, L0_ffn_b2)
    return x

_drawn_inputs = setup_inputs


def setup_inputs(seed=0):
    import zlib

    import numpy as np

    out = dict(_drawn_inputs(seed))
    spreads = {'L0_attn_b_attn_norm_w': (1.0, 0.2),
     'L0_attn_b_attn_out_norm_w': (1.0, 0.2),
     'L0_attn_b_mlp_norm_w': (1.0, 0.6),
     'L0_ffn_gamma': (1.0, 0.2),
     'L0_ffn_beta': (0.0, 0.1),
     'L0_ffn_br': (0.0, 0.1),
     'L0_ffn_b1': (0.0, 0.1),
     'L0_ffn_b2': (0.0, 0.1)}
    factors = {'L0_attn_b_Wgate': 8.0, 'L0_attn_b_Wup': 8.0, 'L0_attn_b_Wdown': 8.0}
    for name, (base, spread) in spreads.items():
        noise = np.random.default_rng([zlib.crc32(name.encode()), seed]).standard_normal(out[name].shape)
        drawn = base * np.exp(spread * noise) if base else spread * noise
        out[name] = jnp.asarray(drawn.astype(out[name].dtype))
    for name, factor in factors.items():
        out[name] = (out[name] * factor).astype(out[name].dtype)
    return out
```

```python
import concourse.bass as bass
from concourse import mybir
from contextlib import ExitStack

f32 = mybir.dt.float32
bf16 = mybir.dt.bfloat16
u32 = mybir.dt.uint32
ALU = mybir.AluOpType
ACT = mybir.ActivationFunctionType
AX = mybir.AxisListType

P = 128
B, T, D = 8, 512, 128
NT = T // P
EPS = 1e-5
START = 8
MASKED = -1e10

HA, DHA = 16, 64
ND = HA * NT
HB, DB = 8, 128
INTER = 512
E, F = 8, 512
FC = F // P


def build_hybrid(nc, x, W_K, W_Q, W_V, W_O, attn_norm_w, Wq, Wk, Wv, Wo, out_norm_w, mlp_norm_w,
                 Wgate, Wup, Wdown, gamma, beta, Wr, br, W1, b1, W2, b2, out):
    root = ExitStack()
    with root:
        def sb(name, shape, dt=f32, at=root):
            return at.enter_context(nc.sbuf_tensor(name, shape, dt))

        def sem(name, at=root):
            return at.enter_context(nc.semaphore(name))

        bank = [root.enter_context(nc.psum_tensor(f"bank{k}", [P, 512], f32)) for k in range(8)]

        x_sb = sb("x_sb", [P, (B + 1) * NT, D])
        z_sb = sb("z_sb", [P, (B + 1) * NT, D])
        M_sb = sb("M_sb", [P, HA, D])
        U_sb = sb("U_sb", [P, HA, D])
        A_sb = sb("A_sb", [P, HB, D])
        Wv_sb = sb("Wv_sb", [P, HB * DB])
        Wo_sb = sb("Wo_sb", [P, HB, D])
        Wgate_sb = sb("Wgate_sb", [P, INTER])
        Wup_sb = sb("Wup_sb", [P, INTER])
        Wdown_sb = sb("Wdown_sb", [P, INTER // P, D])
        W1_sb = sb("W1_sb", [P, E, F])
        W2_sb = sb("W2_sb", [P, E, FC, D])
        Wr_sb = sb("Wr_sb", [P, E])
        br_sb = sb("br_sb", [P, E])
        wn_sb = sb("wn_sb", [P, D])
        cols = sb("cols", [P, E * FC + 5])
        b1_col = cols[:, 0:E * FC]
        gamma_col, beta_col, attn_norm_col, out_norm_col, mlp_norm_col = (
            cols[:, E * FC + k:E * FC + k + 1] for k in range(5))
        moe_const = sb("moe_const", [E, D])
        ident = sb("ident", [P, P])
        ident_bf = sb("ident_bf", [P, P], bf16)
        mask_bf = sb("mask_bf", [P, P], bf16)
        keep = sb("keep", [P, P])
        expert_id = sb("expert_id", [P, E])
        half = sb("half", [P, NT])
        eps = sb("eps", [P, NT])
        per_dim = sb("per_dim", [P, NT])
        stats = sb("stats", [P, 2, NT, 6])
        moments = sb("moments", [P, 2, NT, 2])
        power = sb("power", [P, 2, 6, NT])
        xn = sb("xn", [P, 2, NT, D])
        xnT = sb("xnT", [P, 2, T])
        y_sb = sb("y_sb", [P, 2, NT, D])
        xy_sb = sb("xy_sb", [P, 2, NT, D])
        htok = sb("htok", [P, 2, NT, D])

        s_xload = sem("s_xload")
        s_store = sem("s_store")

        with ExitStack() as st:
            WK_sb = sb("WK_sb", [P, HA // 2, D], at=st)
            WQ_sb = sb("WQ_sb", [P, HA // 2, D], at=st)
            WV_sb = sb("WV_sb", [P, HA // 2, D], at=st)
            WO_sb = sb("WO_sb", [P, HA * DHA], at=st)
            WOT_sb = sb("WOT_sb", [P, HA // 2, D], at=st)
            Wq_sb = sb("Wq_sb", [P, HB * DB], at=st)
            Wk_sb = sb("Wk_sb", [P, HB * DB], at=st)
            WqT_sb = sb("WqT_sb", [P, HB, D], at=st)
            WkT_sb = sb("WkT_sb", [P, HB, D], at=st)
            Wo_raw = sb("Wo_raw", [P, HB, D], at=st)
            rows = sb("rows", [E * FC + 5, P], at=st)
            b2_sb = sb("b2_sb", [E, D], at=st)
            c_sb = sb("c_sb", [E, D], at=st)
            ones = sb("ones", [E, E], at=st)
            rb1 = sb("rb1", [P, E, FC, E], at=st)
            zero = sb("zero", [P, P], at=st)
            zero_bf = sb("zero_bf", [P, P], bf16, at=st)

            s_heads = sem("s_heads")
            s_lin = sem("s_lin")
            s_small = sem("s_small")
            s_big = sem("s_big")
            s_fill = sem("s_fill")
            s_const = sem("s_const")
            s_prod = sem("s_prod")
            s_evac = sem("s_evac")
            s_rows = sem("s_rows")
            s_cols = sem("s_cols")
            s_rb1 = sem("s_rb1")
            s_c = sem("s_c")
            s_csum = sem("s_csum")
            s_dve = sem("s_dve")

            with nc.Block() as block:
                @block.sync
                def _(sp):
                    for w_sb, w in ((WK_sb, W_K), (WQ_sb, W_Q), (WV_sb, W_V)):
                        sp.dma_start(w_sb[:, :, :], w.rearrange("(t a) d e -> (a d) t e", a=2)).then_inc(s_heads, 16)
                    sp.dma_start(WO_sb[:, :], W_O).then_inc(s_heads, 16)
                    for b in range(B):
                        sp.dma_start(x_sb[:, b * NT:(b + 1) * NT, :],
                                     x[b].rearrange("(t p) e -> p t e", p=P)).then_inc(s_xload, 16)
                    sp.dma_start(W1_sb[:, :, :], W1.rearrange("e h f -> h e f")).then_inc(s_big, 16)
                    sp.dma_start(W2_sb[:, :, :, :], W2.rearrange("e (c f) h -> f e c h", f=P)).then_inc(s_big, 16)
                    sp.dma_start(Wv_sb[:, :], Wv).then_inc(s_big, 16)
                    sp.dma_start(Wgate_sb[:, :], Wgate).then_inc(s_big, 16)
                    sp.dma_start(Wup_sb[:, :], Wup).then_inc(s_big, 16)
                    sp.dma_start(Wdown_sb[:, :, :], Wdown.rearrange("(c f) d -> f c d", f=P)).then_inc(s_big, 16)

                @block.gpsimd
                def _(pool):
                    nc.gpsimd.memset(zero[:, :], 0.0).then_inc(s_fill, 1)
                    nc.gpsimd.memset(zero_bf[:, :], 0.0).then_inc(s_fill, 1)
                    nc.gpsimd.memset(half[:, :], -0.5).then_inc(s_const, 1)
                    nc.gpsimd.memset(eps[:, :], EPS).then_inc(s_const, 1)
                    nc.gpsimd.memset(per_dim[:, :], 1.0 / DB).then_inc(s_const, 1)
                    nc.gpsimd.memset(ones[:, :], 1.0).then_inc(s_const, 1)
                    nc.gpsimd.memset(x_sb[:, B * NT:, :], 0.0).then_inc(s_const, 1)
                    nc.gpsimd.memset(z_sb[:, B * NT:, :], 0.0).then_inc(s_const, 1)
                    nc.gpsimd.iota(expert_id[:, :], pattern=[[1, E]], base=0, channel_multiplier=0,
                                   allow_small_or_imprecise_dtypes=True).then_inc(s_const, 1)
                    pool.wait_ge(s_fill, 2)
                    nc.gpsimd.affine_select(out=ident[:, :], in_=zero[:, :], compare_op=ALU.not_equal, fill=1.0,
                                            base=0, pattern=[[-1, P]], channel_multiplier=1).then_inc(s_const, 1)
                    nc.gpsimd.affine_select(out=ident_bf[:, :], in_=zero_bf[:, :], compare_op=ALU.not_equal, fill=1.0,
                                            base=0, pattern=[[-1, P]], channel_multiplier=1).then_inc(s_const, 1)
                    nc.gpsimd.affine_select(out=mask_bf[:, :], in_=zero_bf[:, :], compare_op=ALU.is_ge, fill=MASKED,
                                            base=0, pattern=[[-1, P]], channel_multiplier=1).then_inc(s_const, 1)
                    nc.gpsimd.affine_select(out=keep[:, :], in_=zero[:, :], compare_op=ALU.is_gt, fill=1.0,
                                            base=0, pattern=[[-1, P]], channel_multiplier=1).then_inc(s_const, 1)

                @block.scalar
                def _(act):
                    act.dma_start(rows[0:E * FC, :], b1.rearrange("e (c f) -> (e c) f", f=P)).then_inc(s_small, 16)
                    for k, v in enumerate((gamma, beta, attn_norm_w, out_norm_w, mlp_norm_w)):
                        act.dma_start(rows[E * FC + k:E * FC + k + 1, :],
                                      v.rearrange("(a n) -> a n", a=1)).then_inc(s_small, 16)
                    act.dma_start(b2_sb[:, :], b2).then_inc(s_small, 16)
                    act.dma_start(Wr_sb[:, :], Wr).then_inc(s_small, 16)
                    act.dma_start(br_sb[:, :], br.partition_broadcast(P)).then_inc(s_small, 16)
                    act.dma_start(wn_sb[:, :], attn_norm_w.partition_broadcast(P)).then_inc(s_small, 16)
                    act.dma_start(Wq_sb[:, :], Wq).then_inc(s_lin, 16)
                    act.dma_start(Wk_sb[:, :], Wk).then_inc(s_lin, 16)
                    act.dma_start(Wo_raw[:, :, :], Wo.rearrange("(h v) d -> v h d", v=DB)).then_inc(s_lin, 16)
                    job = 0
                    for dst, step, scale in (
                            (M_sb, 2, DHA ** -0.5), (WOT_sb, 1, 1.0), (WqT_sb, 1, 1.0), (WkT_sb, 1, 1.0),
                            (U_sb, 2, 1.0), (A_sb, 1, 1.0)):
                        for k in range(2 * step):
                            first = (k // 2) + step * 4 * (k % 2)
                            act.wait_ge(s_prod, job + 1)
                            nc.scalar.activation(dst[:, first:first + 3 * step + 1:step, :],
                                                 bank[job % 7][:, :].rearrange("p (h e) -> p h e", e=D),
                                                 ACT.Copy, scale=scale).then_inc(s_evac, 1)
                            job += 1

                @block.tensor
                def _(pe):
                    job = 0

                    def next_bank():
                        if job >= 7:
                            pe.wait_ge(s_evac, job - 6)
                        return bank[job % 7]

                    pe.wait_ge(s_heads, 64)
                    for k in range(4):
                        ps = next_bank()
                        for m in range(4):
                            h = k // 2 + 2 * (4 * (k % 2) + m)
                            r = slice(DHA * (h % 2), DHA * (h % 2) + DHA)
                            mm = nc.tensor.matmul(ps[:, m * D:(m + 1) * D], WK_sb[r, h // 2, :], WQ_sb[r, h // 2, :],
                                                  start=True, stop=True)
                        mm.then_inc(s_prod, 1)
                        job += 1
                    pe.wait_ge(s_const, 11)
                    pe.wait_ge(s_lin, 48)
                    for src in (WO_sb, Wq_sb, Wk_sb):
                        for k in range(2):
                            ps = next_bank()
                            for m in range(4):
                                c = 4 * k + m
                                mm = nc.tensor.transpose(ps[:, m * P:(m + 1) * P], src[:, c * P:(c + 1) * P],
                                                         ident[:, :])
                            mm.then_inc(s_prod, 1)
                            job += 1
                    for k in range(4):
                        ps = next_bank()
                        if k == 0:
                            pe.wait_ge(s_evac, 6)
                        for m in range(4):
                            h = k // 2 + 2 * (4 * (k % 2) + m)
                            r = slice(DHA * (h % 2), DHA * (h % 2) + DHA)
                            mm = nc.tensor.matmul(ps[:, m * D:(m + 1) * D], WV_sb[r, h // 2, :], WOT_sb[r, h // 2, :],
                                                  start=True, stop=True)
                        mm.then_inc(s_prod, 1)
                        job += 1
                    for k in range(2):
                        ps = next_bank()
                        if k == 0:
                            pe.wait_ge(s_evac, 10)
                        for m in range(4):
                            h = 4 * k + m
                            mm = nc.tensor.matmul(ps[:, m * D:(m + 1) * D], WqT_sb[:, h, :], WkT_sb[:, h, :],
                                                  start=True, stop=True)
                        mm.then_inc(s_prod, 1)
                        job += 1
                    pe.wait_ge(s_small, 160)
                    n = E * FC + 5
                    nc.tensor.transpose(bank[7][:, 0:n], rows[:, :], ident[0:n, 0:n]).then_inc(s_rows, 1)
                    pe.wait_ge(s_rb1, E)
                    pe.wait_ge(s_big, 96)
                    for e in range(E):
                        for c in range(FC):
                            mm = nc.tensor.matmul(bank[7][0:E, 0:D], rb1[:, e, c, :], W2_sb[:, e, c, :],
                                                  start=(e == 0 and c == 0), stop=(e == E - 1 and c == FC - 1))
                    mm.then_inc(s_c, 1)
                    pe.wait_ge(s_dve, 3)
                    nc.tensor.matmul(bank[7][0:E, 0:D], ones[:, :], c_sb[:, :], start=True, stop=True).then_inc(s_csum, 1)

                @block.vector
                def _(dve):
                    nc.vector.memset(rb1[:, :, :, :], 0.0).then_inc(s_dve, 1)
                    dve.wait_ge(s_rows, 1)
                    nc.vector.tensor_copy(cols[:, :], bank[7][:, 0:E * FC + 5]).then_inc(s_cols, 1)
                    dve.wait_ge(s_cols, 1)
                    dve.wait_ge(s_dve, 1)
                    for e in range(E):
                        nc.vector.tensor_scalar(rb1[:, e, :, e], b1_col[:, e * FC:(e + 1) * FC], 0.0, None,
                                                ALU.max).then_inc(s_rb1, 1)
                    nc.vector.tensor_scalar(Wo_sb[:, :, :], Wo_raw[:, :, :], out_norm_col, None,
                                            ALU.mult).then_inc(s_dve, 1)
                    dve.wait_ge(s_c, 1)
                    nc.vector.tensor_tensor(c_sb[:, :], bank[7][0:E, 0:D], b2_sb[:, :], ALU.add).then_inc(s_dve, 1)
                    dve.wait_ge(s_dve, 3)
                    nc.vector.tensor_tensor(b2_sb[:, :], b2_sb[:, :], c_sb[:, :], ALU.subtract).then_inc(s_dve, 1)
                    dve.wait_ge(s_csum, 1)
                    dve.wait_ge(s_dve, 4)
                    nc.vector.tensor_tensor(moe_const[:, :], bank[7][0:E, 0:D], b2_sb[:, :],
                                            ALU.add).then_inc(s_dve, 1)

        def uses_ago(n, ring, per_row):
            if n >= ring:
                return ring
            return min(ring, per_row + n - max(m for m in range(per_row) if m % ring == n))

        LN, LN_LN, RMS = range(3)

        class Ahead:

            def __init__(self, name, at, kind, src, scale, bias, want_y=False, want_sum=False, want_htok=False):
                self.kind, self.src, self.scale, self.bias = kind, src, scale, bias
                self.want_y, self.want_sum, self.want_htok = want_y, want_sum, want_htok
                self.stats = sem(name + "_stats_ready", at)
                self.counted = sem(name + "_stats_counted", at)
                self.moments = sem(name + "_moments_ready", at)
                self.pool_step = sem(name + "_pool_step", at)
                self.rstd = sem(name + "_rstd_ready", at)
                self.xn = sem(name + "_xn_ready", at)
                self.y = sem(name + "_y_ready", at)
                self.sum = sem(name + "_sum_ready", at)
                self.htok = sem(name + "_htok_ready", at)
                self.tr = sem(name + "_transposed", at)
                self.of_dve = (self.stats, self.moments, self.xn, self.y)
                self.of_pool = (self.pool_step, self.rstd, self.sum, self.htok)

            def tiles(self, b, where=None):
                return (self.src if where is None else where)[:, bass.ds(b * NT, NT), :]

            def dve_stats(self, dve, b, u):
                for t in range(NT):
                    nc.vector.bn_stats(stats[:, u, t, :],
                                       self.src[:, bass.ds(b * NT + t, 1), :]).then_inc(self.stats, 1)
                dve.wait_ge(self.stats, START + b * NT + NT)
                dve.sem_inc(self.counted, 1)
                for t in range(NT):
                    nc.vector.bn_aggr(moments[:, u, t, :], stats[:, u, t, :]).then_inc(self.moments, 1)

            def pool_rstd(self, pool, b, u):
                pw = [power[:, u, k, :] for k in range(6)]
                mean, var = moments[:, u, :, 0], moments[:, u, :, 1]
                TT = nc.gpsimd.tensor_tensor
                per_row = {LN: 1, LN_LN: 5, RMS: 3}[self.kind]
                done = [0]

                def then_next(ins):
                    done[0] += 1
                    ins.then_inc(self.pool_step, 1)
                    pool.wait_ge(self.pool_step, START + b * per_row + done[0])

                pool.wait_ge(self.moments, START + b * NT + NT)
                if self.kind == RMS:
                    then_next(TT(pw[1], mean, mean, ALU.mult))
                    then_next(TT(pw[2], pw[1], var, ALU.add))
                    then_next(TT(pw[3], pw[2], eps[:, :], ALU.add))
                    TT(pw[5], pw[3], half[:, :], ALU.pow).then_inc(self.rstd, 1)
                    return
                then_next(TT(pw[1], var, eps[:, :], ALU.add))
                if self.kind == LN:
                    TT(pw[5], pw[1], half[:, :], ALU.pow).then_inc(self.rstd, 1)
                    return
                then_next(TT(pw[0], pw[1], half[:, :], ALU.pow))
                then_next(TT(pw[2], pw[0], pw[0], ALU.mult))
                then_next(TT(pw[3], pw[2], var, ALU.mult))
                then_next(TT(pw[4], pw[3], eps[:, :], ALU.add))
                TT(pw[2], pw[4], half[:, :], ALU.pow).then_inc(self.rstd, 1)
                pool.wait_ge(self.rstd, START + 2 * b + 1)
                TT(pw[5], pw[0], pw[2], ALU.mult).then_inc(self.rstd, 1)

            def dve_normalise(self, dve, b, u):
                dve.wait_ge(self.rstd, START + ((2 * b + 2) if self.kind == LN_LN else (b + 1)))
                for t in range(NT):
                    tile = self.src[:, bass.ds(b * NT + t, 1), :]
                    if self.kind == RMS:
                        nc.vector.tensor_scalar(xn[:, u, t:t + 1, :], tile, power[:, u, 5, t:t + 1], None,
                                                ALU.mult).then_inc(self.xn, 1)
                        continue
                    mean = moments[:, u, t, 0:1]
                    nc.vector.tensor_scalar(xn[:, u, t:t + 1, :], tile, mean, power[:, u, 5, t:t + 1],
                                            ALU.subtract, ALU.mult).then_inc(self.xn, 1)
                    if self.want_y:
                        nc.vector.tensor_scalar(y_sb[:, u, t:t + 1, :], tile, mean, power[:, u, 0, t:t + 1],
                                                ALU.subtract, ALU.mult).then_inc(self.y, 1)

            def pool_finish(self, pool, b, u):
                if self.want_sum:
                    pool.wait_ge(self.xn, START + b * NT + NT)
                    if self.want_y:
                        pool.wait_ge(self.y, START + b * NT + NT)
                    nc.gpsimd.tensor_tensor(xy_sb[:, u, :, :], self.tiles(b, x_sb),
                                            y_sb[:, u, :, :] if self.want_y else self.tiles(b),
                                            ALU.add).then_inc(self.sum, 1)
                if self.want_htok:
                    pool.wait_ge(self.xn, START + b * NT + NT)
                    nc.gpsimd.tensor_tensor(htok[:, u, :, :], xn[:, u, :, :],
                                            wn_sb[:, :].unsqueeze(1).to_broadcast([P, NT, D]),
                                            ALU.mult).then_inc(self.htok, 1)

            def pe_transpose(self, pe, b, u):
                pe.wait_ge(self.xn, START + b * NT + NT)
                for t in range(NT):
                    mm = nc.tensor.transpose(bank[0][:, t * P:(t + 1) * P], xn[:, u, t, :], ident[:, :])
                mm.then_inc(self.tr, 1)

            def act_evacuate(self, act, b, u, done):
                act.wait_ge(self.tr, START + b + 1)
                if self.bias is not None:
                    nc.scalar.activation(xnT[:, u, :], bank[0][:, :], ACT.Identity, bias=self.bias,
                                         scale=self.scale).then_inc(done, 1)
                else:
                    nc.scalar.activation(xnT[:, u, :], bank[0][:, :], ACT.Copy, scale=self.scale).then_inc(done, 1)

        def begin(eng, *semaphores):
            for s in semaphores:
                eng.sem_inc(s, START)

        with ExitStack() as st:
            ahead = Ahead("a", st, LN, x_sb, 1.0, None)
            width = [P * (i + 1) for i in range(NT)]
            start = [sum(width[:i]) for i in range(NT)]
            G_sb = sb("G_sb", [P, 2, T], at=st)
            Vraw = sb("Vraw", [P, 2, NT, 4, D], at=st)
            Vs = sb("Vs", [P, 8, D], at=st)
            prob = sb("prob", [P, 2, sum(width)], at=st)
            negmax = sb("negmax", [P, 8], at=st)
            rowsum = sb("rowsum", [P, 8], at=st)
            rinv = sb("rinv", [P, 8], at=st)
            warm = sb("warm", [P, NT], at=st)
            bankT, bankO, bankG, bankV, bankS = bank[0], bank[1], bank[2], bank[3:5], bank[5:8]

            xnT_ready = sem("a_xnT_ready", st)
            G_done, G_ready = sem("a_G_done", st), sem("a_G_ready", st)
            V_done, V_ready = sem("a_V_done", st), sem("a_V_ready", st)
            scores_ready = sem("a_scores_ready", st)
            negmax_ready = sem("a_negmax_ready", st)
            prob_ready = sem("a_prob_ready", st)
            rinv_ready = sem("a_rinv_ready", st)
            Vs_ready = sem("a_Vs_ready", st)
            row_done = sem("a_row_done", st)
            x_done = sem("a_x_done", st)
            STATS_AT, NORM_AT, TR_AT, EVAC_AT = 20, 36, 46, 48

            def step(n):
                return n // NT, NT - 1 - n % NT

            with nc.Block() as block:
                @block.tensor
                def _(pe):
                    begin(pe, G_done, V_done, scores_ready, row_done, ahead.tr)
                    pe.wait_ge(s_const, 11)
                    ahead.pe_transpose(pe, 0, 0)

                    def G(b, u, h):
                        pe.wait_ge(G_ready, START + b * HA + h)
                        nc.tensor.matmul(bankG[:, :], M_sb[:, h, :], xnT[:, u, :], start=True,
                                         stop=True).then_inc(G_done, 1)

                    def V(b, u, g, i):
                        n = g * NT + i
                        pe.wait_ge(V_ready, START + b * (NT * 4) + n - 1)
                        nc.tensor.matmul(bankV[n % 2][:, :], xnT[:, u, i * P:(i + 1) * P],
                                         U_sb[:, 4 * g:4 * g + 4, :], start=True, stop=True).then_inc(V_done, 1)

                    def S(b, u, n):
                        h, i = step(n)
                        pe.wait_ge(G_ready, START + b * HA + h + 1)
                        pe.wait_ge(prob_ready, START + b * ND + n + 1 - uses_ago(n, len(bankS), ND))
                        ps = bankS[n % 3]
                        nc.tensor.matmul(ps[:, 0:width[i]], G_sb[:, h % 2, i * P:(i + 1) * P],
                                         xnT[:, u, 0:width[i]], start=True, stop=False)
                        nc.tensor.matmul(ps[:, i * P:(i + 1) * P], ident_bf[:, :], mask_bf[:, :], start=False,
                                         stop=True).then_inc(scores_ready, 1)

                    def PV(b, u, n):
                        h, i = step(n)
                        if n == 0:
                            pe.wait_ge(x_done, START + b)
                        pe.wait_ge(prob_ready, START + b * ND + n + 1)
                        pe.wait_ge(Vs_ready, START + b * ND + n + 1)
                        for j in range(i + 1):
                            mm = nc.tensor.matmul(bankO[:, j * D:(j + 1) * D],
                                                  prob[:, h % 2, start[i] + j * P:start[i] + (j + 1) * P],
                                                  Vs[:, n % 8, :], start=(n == 0 and j == 0),
                                                  stop=(h == HA - 1), skip_group_check=True)
                        if n == ND - 1:
                            mm.then_inc(row_done, 1)

                    with pe.Fori(0, B // 2) as pair:
                        for u in range(2):
                            b = pair * 2 + u
                            pe.wait_ge(xnT_ready, START + b + 1)
                            for n in range(ND + NT):
                                if n == 0:
                                    G(b, u, 0)
                                    for i in range(NT):
                                        V(b, u, 0, i)
                                    G(b, u, 1)
                                elif n < ND and n % NT == 0 and n // NT + 1 < HA:
                                    G(b, u, n // NT + 1)
                                if n % NT == 2 and n // NT < HA - 4:
                                    V(b, u, n // NT // 4 + 1, n // NT % 4)
                                if n < ND:
                                    S(b, u, n)
                                if n >= NT:
                                    PV(b, u, n - NT)
                                if n == TR_AT:
                                    ahead.pe_transpose(pe, b + 1, 1 - u)

                @block.scalar
                def _(act):
                    begin(act, G_ready, V_ready, prob_ready, xnT_ready)
                    act.wait_ge(s_const, 11)
                    nc.scalar.activation(warm[:, :], half[:, :], ACT.Exp)
                    ahead.act_evacuate(act, 0, 0, xnT_ready)

                    def evac_G(b, u, h):
                        act.wait_ge(G_done, START + b * HA + h + 1)
                        act.wait_ge(scores_ready, START + b * ND + NT * (h - 1))
                        nc.scalar.activation(G_sb[:, h % 2, :], bankG[:, :], ACT.Copy).then_inc(G_ready, 1)

                    def evac_V(b, u, g, i):
                        n = g * NT + i
                        act.wait_ge(V_done, START + b * (NT * 4) + n + 1)
                        act.wait_ge(Vs_ready, START + b * ND + 4 * NT * max(g - 1, 0))
                        nc.scalar.activation(Vraw[:, g % 2, i, :, :],
                                             bankV[n % 2][:, :].rearrange("p (h e) -> p h e", e=D),
                                             ACT.Copy).then_inc(V_ready, 1)

                    with act.Fori(0, B // 2) as pair:
                        for u in range(2):
                            b = pair * 2 + u
                            for n in range(ND):
                                if n == 0:
                                    evac_G(b, u, 0)
                                    for i in range(NT):
                                        evac_V(b, u, 0, i)
                                    evac_G(b, u, 1)
                                elif n % NT == 0 and n // NT + 1 < HA:
                                    evac_G(b, u, n // NT + 1)
                                if n % NT == 2 and n // NT < HA - 4:
                                    evac_V(b, u, n // NT // 4 + 1, n // NT % 4)
                                h, i = step(n)
                                act.wait_ge(negmax_ready, START + b * ND + n + 1)
                                nc.scalar.activation(prob[:, h % 2, start[i]:start[i] + width[i]],
                                                     bankS[n % 3][:, 0:width[i]], ACT.Exp,
                                                     bias=negmax[:, n % 8:n % 8 + 1],
                                                     accum_out=rowsum[:, n % 8:n % 8 + 1]).then_inc(prob_ready, 1)
                                if n == EVAC_AT:
                                    ahead.act_evacuate(act, b + 1, 1 - u, xnT_ready)

                @block.vector
                def _(dve):
                    begin(dve, negmax_ready, rinv_ready, Vs_ready, x_done, *ahead.of_dve)
                    dve.wait_ge(s_xload, 16 * B)
                    ahead.dve_stats(dve, 0, 0)
                    ahead.dve_normalise(dve, 0, 0)
                    with dve.Fori(0, B // 2) as pair:
                        for u in range(2):
                            b = pair * 2 + u
                            for n in range(ND + 2):
                                if n < ND:
                                    h, i = step(n)
                                    dve.wait_ge(scores_ready, START + b * ND + n + 1)
                                    nc.vector.tensor_reduce(negmax[:, n % 8:n % 8 + 1],
                                                            bankS[n % 3][:, 0:width[i]], AX.X, ALU.max,
                                                            negate=True).then_inc(negmax_ready, 1)
                                if 1 <= n <= ND:
                                    m = n - 1
                                    dve.wait_ge(prob_ready, START + b * ND + m + 1)
                                    nc.vector.reciprocal(rinv[:, m % 8:m % 8 + 1],
                                                         rowsum[:, m % 8:m % 8 + 1]).then_inc(rinv_ready, 1)
                                if n >= 2:
                                    m = n - 2
                                    h, i = step(m)
                                    dve.wait_ge(rinv_ready, START + b * ND + m + 1)
                                    dve.wait_ge(V_ready, START + b * (NT * 4) + (h // 4) * NT + i + 1)
                                    nc.vector.tensor_scalar(Vs[:, m % 8, :], Vraw[:, h // 4 % 2, i, h % 4, :],
                                                            rinv[:, m % 8:m % 8 + 1], None,
                                                            ALU.mult).then_inc(Vs_ready, 1)
                                if n == STATS_AT:
                                    ahead.dve_stats(dve, b + 1, 1 - u)
                                if n == NORM_AT:
                                    dve.wait_ge(row_done, START + b)
                                    ahead.dve_normalise(dve, b + 1, 1 - u)
                            dve.wait_ge(row_done, START + b + 1)
                            tiles = x_sb[:, bass.ds(b * NT, NT), :]
                            nc.vector.tensor_tensor(tiles, tiles,
                                                    bankO[:, :].rearrange("p (t e) -> p t e", e=D),
                                                    ALU.add).then_inc(x_done, 1)

                @block.gpsimd
                def _(pool):
                    begin(pool, *ahead.of_pool)
                    ahead.pool_rstd(pool, 0, 0)
                    with pool.Fori(0, B // 2) as pair:
                        for u in range(2):
                            ahead.pool_rstd(pool, pair * 2 + u + 1, 1 - u)

        def moe_stage(name, store):
            with ExitStack() as st:
                ahead = Ahead(name, st, LN_LN, x_sb, gamma_col, beta_col, want_y=True, want_sum=True)
                hid = sb(name + "_hid", [P, 2, FC, T], at=st)
                logit = sb(name + "_logit", [P, NT, E], at=st)
                shifted = sb(name + "_shifted", [P, NT, E], at=st)
                ex = sb(name + "_ex", [P, NT, E], at=st)
                top = sb(name + "_top", [P, NT, E], at=st)
                topid = sb(name + "_topid", [P, NT, E], u32, at=st)
                topidf = sb(name + "_topidf", [P, NT, E], at=st)
                is_k = sb(name + "_is_k", [P, 2, NT, E], at=st)
                val_k = sb(name + "_val_k", [P, 2, NT, E], at=st)
                chosen = sb(name + "_chosen", [P, NT, E], at=st)
                gate = sb(name + "_gate", [P, 2, NT, E], at=st)
                gateT = sb(name + "_gateT", [E, T], at=st)
                rmax = sb(name + "_rmax", [P, NT, 1], at=st)
                rsum = sb(name + "_rsum", [P, NT, 1], at=st)
                rrec = sb(name + "_rrec", [P, NT, 1], at=st)
                warm = sb(name + "_warm", [P, NT], at=st)
                bankR, bankH, bankM, bankC = bank[1], bank[2:5], bank[5:7], bank[7]

                xnT_ready = sem(name + "_xnT_ready", st)
                logits_ready = sem(name + "_logits_ready", st)
                shifted_ready = sem(name + "_shifted_ready", st)
                ex_ready = sem(name + "_ex_ready", st)
                route_step = sem(name + "_route_step", st)
                gate_ready = sem(name + "_gate_ready", st)
                gate_transposed = sem(name + "_gate_transposed", st)
                gateT_ready = sem(name + "_gateT_ready", st)
                hid_done = sem(name + "_hid_done", st)
                hid_ready = sem(name + "_hid_ready", st)
                expert_done = sem(name + "_expert_done", st)
                tile_added = sem(name + "_tile_added", st)
                const_done = sem(name + "_const_done", st)
                x_done = sem(name + "_x_done", st)
                NH = E * FC
                H_RING, M_RING = len(bankH), len(bankM)
                EXP_AT, GATE_AT, GATET_AT, CONST_AT, AHEAD_AT = 1, 2, 3, 4, 5

                with nc.Block() as block:
                    @block.tensor
                    def _(pe):
                        begin(pe, logits_ready, gate_transposed, hid_done, expert_done, const_done, ahead.tr)
                        ahead.pe_transpose(pe, 0, 0)

                        def up(b, u, e):
                            for c in range(FC):
                                n = e * FC + c
                                pe.wait_ge(hid_ready, START + b * NH + n + 1 - uses_ago(n, H_RING, NH))
                                nc.tensor.matmul(bankH[n % H_RING][:, :], W1_sb[:, e, c * P:(c + 1) * P],
                                                 xnT[:, u, :], start=True, stop=True).then_inc(hid_done, 1)

                        def down(b, u, e):
                            pe.wait_ge(tile_added, START + (b * E + e + 1 - M_RING) * NT)
                            pe.wait_ge(hid_ready, START + b * NH + (e + 1) * FC)
                            for t in range(NT):
                                for c in range(FC):
                                    mm = nc.tensor.matmul(bankM[e % M_RING][:, t * D:(t + 1) * D],
                                                          hid[:, e % 2, c, t * P:(t + 1) * P], W2_sb[:, e, c, :],
                                                          start=(c == 0), stop=(c == FC - 1))
                            mm.then_inc(expert_done, 1)

                        with pe.Fori(0, B // 2) as pair:
                            for u in range(2):
                                b = pair * 2 + u
                                pe.wait_ge(xnT_ready, START + b + 1)
                                pe.wait_ge(gateT_ready, START + b)
                                for t in range(NT):
                                    mm = nc.tensor.matmul(bankR[:, t * E:(t + 1) * E],
                                                          xnT[:, u, t * P:(t + 1) * P], Wr_sb[:, :],
                                                          start=True, stop=True)
                                mm.then_inc(logits_ready, 1)
                                up(b, u, 0)
                                for e in range(E):
                                    if e + 1 < E:
                                        up(b, u, e + 1)
                                    down(b, u, e)
                                    if e == GATE_AT:
                                        pe.wait_ge(gate_ready, START + b + 1)
                                        for t in range(NT):
                                            mm = nc.tensor.transpose(bankR[0:E, t * P:(t + 1) * P],
                                                                     gate[:, u, t, :], ident[:, :])
                                        mm.then_inc(gate_transposed, 1)
                                    if e == CONST_AT:
                                        pe.wait_ge(gateT_ready, START + b + 1)
                                        pe.wait_ge(x_done, START + b)
                                        for t in range(NT):
                                            mm = nc.tensor.matmul(bankC[:, t * D:(t + 1) * D],
                                                                  gateT[:, t * P:(t + 1) * P], moe_const[:, :],
                                                                  start=True, stop=True)
                                        mm.then_inc(const_done, 1)
                                    if e == AHEAD_AT:
                                        ahead.pe_transpose(pe, b + 1, 1 - u)

                    @block.scalar
                    def _(act):
                        begin(act, xnT_ready, ex_ready, gateT_ready, hid_ready)
                        nc.scalar.activation(warm[:, :], half[:, :], ACT.Exp)
                        ahead.act_evacuate(act, 0, 0, xnT_ready)
                        with act.Fori(0, B // 2) as pair:
                            for u in range(2):
                                b = pair * 2 + u
                                for e in range(E):
                                    act.wait_ge(expert_done, START + b * E + e - 1)
                                    for c in range(FC):
                                        n = e * FC + c
                                        act.wait_ge(hid_done, START + b * NH + n + 1)
                                        nc.scalar.activation(hid[:, e % 2, c, :], bankH[n % H_RING][:, :], ACT.Relu,
                                                             bias=b1_col[:, n:n + 1]).then_inc(hid_ready, 1)
                                    if e == EXP_AT:
                                        act.wait_ge(shifted_ready, START + b + 1)
                                        nc.scalar.activation(ex[:, :, :], shifted[:, :, :],
                                                             ACT.Exp).then_inc(ex_ready, 1)
                                    if e == GATET_AT:
                                        act.wait_ge(gate_transposed, START + b + 1)
                                        nc.scalar.activation(gateT[:, :], bankR[0:E, :],
                                                             ACT.Copy).then_inc(gateT_ready, 1)
                                    if e == AHEAD_AT + 1:
                                        ahead.act_evacuate(act, b + 1, 1 - u, xnT_ready)

                    @block.vector
                    def _(dve):
                        begin(dve, shifted_ready, route_step, gate_ready, tile_added, x_done, *ahead.of_dve)
                        ahead.dve_stats(dve, 0, 0)
                        ahead.dve_normalise(dve, 0, 0)
                        ROUTE_STEPS = 10 + 2 * NT

                        def route(b, u):
                            done = [0]

                            def mark(ins):
                                done[0] += 1
                                ins.then_inc(route_step, 1)

                            def settle():
                                dve.wait_ge(route_step, START + b * ROUTE_STEPS + done[0])

                            wide = [P, NT, E]
                            dve.wait_ge(logits_ready, START + b + 1)
                            mark(nc.vector.tensor_tensor(
                                logit[:, :, :], bankR[:, 0:NT * E].rearrange("p (t e) -> p t e", e=E),
                                br_sb[:, :].unsqueeze(1).to_broadcast(wide), ALU.add))
                            settle()
                            mark(nc.vector.tensor_reduce(rmax[:, :, 0], logit[:, :, :], AX.X, ALU.max))
                            settle()
                            nc.vector.tensor_tensor(shifted[:, :, :], logit[:, :, :],
                                                    rmax[:, :, :].to_broadcast(wide),
                                                    ALU.subtract).then_inc(shifted_ready, 1)
                            dve.wait_ge(ex_ready, START + b + 1)
                            mark(nc.vector.tensor_reduce(rsum[:, :, 0], ex[:, :, :], AX.X, ALU.add))
                            for t in range(NT):
                                mark(nc.vector.max(top[:, t, :], ex[:, t, :]))
                            settle()
                            mark(nc.vector.reciprocal(rrec[:, :, :], rsum[:, :, :]))
                            for t in range(NT):
                                mark(nc.vector.max_index(topid[:, t, :], top[:, t, :], ex[:, t, :]))
                            settle()
                            mark(nc.vector.tensor_copy(topidf[:, :, :], topid[:, :, :]))
                            settle()
                            for k in range(2):
                                mark(nc.vector.tensor_tensor(is_k[:, k, :, :],
                                                             expert_id[:, :].unsqueeze(1).to_broadcast(wide),
                                                             topidf[:, :, k:k + 1].to_broadcast(wide),
                                                             ALU.is_equal))
                            settle()
                            for k in range(2):
                                mark(nc.vector.tensor_tensor(val_k[:, k, :, :], is_k[:, k, :, :],
                                                             top[:, :, k:k + 1].to_broadcast(wide), ALU.mult))
                            settle()
                            mark(nc.vector.tensor_tensor(chosen[:, :, :], val_k[:, 0, :, :], val_k[:, 1, :, :],
                                                         ALU.add))
                            settle()
                            nc.vector.tensor_tensor(gate[:, u, :, :], chosen[:, :, :],
                                                    rrec[:, :, :].to_broadcast(wide),
                                                    ALU.mult).then_inc(gate_ready, 1)
                            assert done[0] == ROUTE_STEPS

                        with dve.Fori(0, B // 2) as pair:
                            for u in range(2):
                                b = pair * 2 + u
                                route(b, u)
                                dve.wait_ge(gate_ready, START + b + 1)
                                dve.wait_ge(ahead.sum, START + b + 1)
                                for e in range(E):
                                    dve.wait_ge(expert_done, START + b * E + e + 1)
                                    dve.wait_ge(tile_added, START + (b * E + e) * NT)
                                    for t in range(NT):
                                        acc = xy_sb[:, u, t, :]
                                        nc.vector.scalar_tensor_tensor(
                                            out=acc, in0=bankM[e % M_RING][:, t * D:(t + 1) * D],
                                            scalar=gate[:, u, t, e:e + 1], in1=acc,
                                            op0=ALU.mult, op1=ALU.add).then_inc(tile_added, 1)
                                    if e == 2:
                                        ahead.dve_stats(dve, b + 1, 1 - u)
                                    if e == 4:
                                        ahead.dve_normalise(dve, b + 1, 1 - u)
                                dve.wait_ge(const_done, START + b + 1)
                                dve.wait_ge(tile_added, START + (b + 1) * E * NT)
                                nc.vector.tensor_tensor(x_sb[:, bass.ds(b * NT, NT), :], xy_sb[:, u, :, :],
                                                        bankC[:, :].rearrange("p (t e) -> p t e", e=D),
                                                        ALU.add).then_inc(x_done, 1)

                    @block.gpsimd
                    def _(pool):
                        begin(pool, *ahead.of_pool)
                        ahead.pool_rstd(pool, 0, 0)
                        ahead.pool_finish(pool, 0, 0)
                        with pool.Fori(0, B // 2) as pair:
                            for u in range(2):
                                ahead.pool_rstd(pool, pair * 2 + u + 1, 1 - u)
                                ahead.pool_finish(pool, pair * 2 + u + 1, 1 - u)

                    if store:
                        @block.sync
                        def _(sp):
                            with sp.Fori(0, B) as b:
                                sp.wait_ge(x_done, START + b + 1)
                                sp.dma_start(out[bass.ds(b, 1)].rearrange("o (t p) e -> p (o t) e", p=P),
                                             x_sb[:, bass.ds(b * NT, NT), :]).then_inc(s_store, 16)
                            sp.wait_ge(s_store, 16 * B)

        def linear_attention_stage():
            with ExitStack() as st:
                ahead = Ahead("b", st, LN_LN, x_sb, attn_norm_col, None, want_y=True, want_htok=True)
                GR = 2
                NS = NT * GR
                V_sb = sb("V_sb", [P, NT, HB * DB], at=st)
                G_sb = sb("Gb_sb", [P, HB, T], at=st)
                R_sb = sb("R_sb", [P, GR, 4 * DB], at=st)
                AT_sb = sb("AT_sb", [P, 2, 4, P], at=st)
                o_sb = sb("o_sb", [P, 2, 4, DB], at=st)
                oT_sb = sb("oT_sb", [P, 2, 4 * P], at=st)
                junk = sb("junk", [P, 2, 4, DB], at=st)
                ss = sb("ss", [P, 2, 4], at=st)
                ms = sb("ms", [P, 2, 4], at=st)
                ro = sb("ro", [P, 2, 4, 1], at=st)
                bankW, bankOo, bankRr, bankZ = bank[1:3], bank[3:5], bank[5:7], bank[7]

                xnT_ready = sem("b_xnT_ready", st)
                proj_done, proj_ready = sem("b_proj_done", st), sem("b_proj_ready", st)
                att_done, att_ready = sem("b_att_done", st), sem("b_att_ready", st)
                o_done = sem("b_o_done", st)
                squares = sem("b_squares", st)
                pool_root = sem("b_pool_root", st)
                root_ready = sem("b_root_ready", st)
                o_ready = sem("b_o_ready", st)
                oT_done, oT_ready = sem("b_oT_done", st), sem("b_oT_ready", st)
                R_done = [sem(f"b_R_done{g}", st) for g in range(GR)]
                R_ready = [sem(f"b_R_ready{g}", st) for g in range(GR)]
                row_done = sem("b_row_done", st)
                z_done = sem("b_z_done", st)

                before = [("v", 0, 0), ("v", 0, 1)] + [("G", h) for h in range(4)]
                after = {0: [("G", h) for h in range(4, 8)]}
                for i in range(1, NT):
                    after[2 * i - 1] = [("v", i, 0), ("v", i, 1)]
                uses = list(before)
                for s in range(NS):
                    uses += [("att", s)] + after.get(s, [])
                NPROJ = sum(x[0] != "att" for x in uses)
                assert len(uses) % 2 == 0
                proj_index = {x: k for k, x in enumerate(x for x in uses if x[0] != "att")}
                AHEAD_AT = 5

                with nc.Block() as block:
                    @block.tensor
                    def _(pe):
                        begin(pe, proj_done, att_done, o_done, oT_done, *R_done, row_done, ahead.tr)
                        ahead.pe_transpose(pe, 0, 0)

                        def claim(b, use):
                            k = uses.index(use)
                            last = uses[k - 2]
                            if k < 2:
                                pe.wait_ge(att_ready, START + b * NS)
                            elif last[0] == "att":
                                pe.wait_ge(att_ready, START + b * NS + last[1] + 1)
                            else:
                                pe.wait_ge(proj_ready, START + b * NPROJ + proj_index[last] + 1)
                            return bankW[k % 2]

                        def project(b, u, use):
                            ps = claim(b, use)
                            if use[0] == "v":
                                _, i, g = use
                                mm = nc.tensor.matmul(ps[:, :], xnT[:, u, i * P:(i + 1) * P],
                                                      Wv_sb[:, g * 512:(g + 1) * 512], start=True, stop=True)
                            else:
                                mm = nc.tensor.matmul(ps[:, :], A_sb[:, use[1], :], xnT[:, u, :], start=True,
                                                      stop=True)
                            mm.then_inc(proj_done, 1)

                        def scores(b, u, s):
                            i, g = divmod(s, GR)
                            ps = claim(b, ("att", s))
                            pe.wait_ge(proj_ready, START + b * NPROJ + proj_index[("G", 4 * g + 3)] + 1)
                            nc.tensor.matmul(ps[:, :].rearrange("p (h i) -> p h i", i=P),
                                             xnT[:, u, i * P:(i + 1) * P],
                                             G_sb[:, 4 * g:4 * g + 4, i * P:(i + 1) * P],
                                             start=True, stop=True).then_inc(att_done, 1)

                        def outputs(b, u, s):
                            i, g = divmod(s, GR)
                            pe.wait_ge(o_ready, START + b * NS + s - 1)
                            pe.wait_ge(att_ready, START + b * NS + s + 1)
                            pe.wait_ge(proj_ready, START + b * NPROJ + proj_index[("v", i, g)] + 1)
                            if i > 0:
                                pe.wait_ge(R_ready[g], START + b * (NT - 1) + i)
                            for m in range(4):
                                h = 4 * g + m
                                o = bankOo[s % 2][:, m * DB:(m + 1) * DB]
                                mm = nc.tensor.matmul(o, AT_sb[:, s % 2, m, :], V_sb[:, i, h * DB:(h + 1) * DB],
                                                      start=True, stop=(i == 0))
                                if i > 0:
                                    mm = nc.tensor.matmul(o, G_sb[:, h, i * P:(i + 1) * P],
                                                          R_sb[:, g, m * DB:(m + 1) * DB], start=False, stop=True)
                            mm.then_inc(o_done, 1)

                        def state(b, u, s):
                            i, g = divmod(s, GR)
                            if i == NT - 1:
                                return
                            if s == 0:
                                pe.wait_ge(ahead.htok, START + b + 1)
                            pe.wait_ge(R_ready[g], START + b * (NT - 1) + i)
                            nc.tensor.matmul(bankRr[g][:, :], htok[:, u, i, :], V_sb[:, i, g * 512:(g + 1) * 512],
                                             start=(i == 0), stop=(i == NT - 2),
                                             skip_group_check=True).then_inc(R_done[g], 1)

                        def transposes(b, u, s):
                            pe.wait_ge(o_ready, START + b * NS + s + 1)
                            pe.wait_ge(oT_ready, START + b * NS + s)
                            if s == 4:
                                pe.wait_ge(xnT_ready, START + b + 2)
                            for m in range(4):
                                mm = nc.tensor.transpose(bank[0][:, m * P:(m + 1) * P], o_sb[:, s % 2, m, :],
                                                         ident[:, :])
                            mm.then_inc(oT_done, 1)

                        def project_out(b, u, s):
                            i, g = divmod(s, GR)
                            if s == 0:
                                pe.wait_ge(z_done, START + b)
                            pe.wait_ge(oT_ready, START + b * NS + s + 1)
                            for m in range(4):
                                mm = nc.tensor.matmul(bankZ[:, i * D:(i + 1) * D], oT_sb[:, s % 2, m * P:(m + 1) * P],
                                                      Wo_sb[:, 4 * g + m, :], start=(g == 0 and m == 0),
                                                      stop=(g == GR - 1 and m == 3))
                            if s == NS - 1:
                                mm.then_inc(row_done, 1)

                        with pe.Fori(0, B // 2) as pair:
                            for u in range(2):
                                b = pair * 2 + u
                                pe.wait_ge(xnT_ready, START + b + 1)
                                for use in before:
                                    project(b, u, use)
                                for s in range(NS + 3):
                                    if s < NS:
                                        scores(b, u, s)
                                        for use in after.get(s, []):
                                            project(b, u, use)
                                    if 1 <= s <= NS:
                                        outputs(b, u, s - 1)
                                        state(b, u, s - 1)
                                    if 2 <= s <= NS + 1:
                                        transposes(b, u, s - 2)
                                    if s == AHEAD_AT:
                                        pe.wait_ge(oT_ready, START + b * NS + 4)
                                        ahead.pe_transpose(pe, b + 1, 1 - u)
                                    if s >= 3:
                                        project_out(b, u, s - 3)

                    @block.scalar
                    def _(act):
                        begin(act, xnT_ready, proj_ready, squares, oT_ready, *R_ready)
                        ahead.act_evacuate(act, 0, 0, xnT_ready)

                        def copy_out(b, u, use):
                            k = uses.index(use)
                            act.wait_ge(proj_done, START + b * NPROJ + proj_index[use] + 1)
                            if use[0] == "v":
                                _, i, g = use
                                dst = V_sb[:, i, g * 512:(g + 1) * 512]
                            else:
                                dst = G_sb[:, use[1], :]
                            nc.scalar.activation(dst, bankW[k % 2][:, :], ACT.Copy).then_inc(proj_ready, 1)

                        with act.Fori(0, B // 2) as pair:
                            for u in range(2):
                                b = pair * 2 + u
                                for use in before:
                                    copy_out(b, u, use)
                                for s in range(NS + 3):
                                    for use in after.get(s, []):
                                        copy_out(b, u, use)
                                    if 1 <= s <= NS:
                                        r = s - 1
                                        i, g = divmod(r, GR)
                                        act.wait_ge(o_done, START + b * NS + r + 1)
                                        for m in range(4):
                                            ins = nc.scalar.activation(junk[:, r % 2, m, :],
                                                                       bankOo[r % 2][:, m * DB:(m + 1) * DB],
                                                                       ACT.Square, accum_out=ss[:, r % 2, m:m + 1])
                                        ins.then_inc(squares, 1)
                                        if i < NT - 1:
                                            act.wait_ge(R_done[g], START + b * (NT - 1) + i + 1)
                                            nc.scalar.activation(R_sb[:, g, :], bankRr[g][:, :],
                                                                 ACT.Copy).then_inc(R_ready[g], 1)
                                    if 2 <= s <= NS + 1:
                                        r = s - 2
                                        act.wait_ge(oT_done, START + b * NS + r + 1)
                                        nc.scalar.activation(oT_sb[:, r % 2, :], bank[0][:, :],
                                                             ACT.Copy).then_inc(oT_ready, 1)
                                    if s == AHEAD_AT:
                                        ahead.act_evacuate(act, b + 1, 1 - u, xnT_ready)

                    @block.gpsimd
                    def _(pool):
                        begin(pool, pool_root, root_ready, *ahead.of_pool)
                        ahead.pool_rstd(pool, 0, 0)
                        ahead.pool_finish(pool, 0, 0)
                        with pool.Fori(0, B // 2) as pair:
                            for u in range(2):
                                b = pair * 2 + u
                                for s in range(NS):
                                    n = b * NS + s
                                    pool.wait_ge(squares, START + n + 1)
                                    nc.gpsimd.tensor_tensor(ms[:, s % 2, :], ss[:, s % 2, :], per_dim[:, :],
                                                            ALU.mult).then_inc(pool_root, 1)
                                    pool.wait_ge(pool_root, START + 2 * n + 1)
                                    nc.gpsimd.tensor_tensor(ms[:, s % 2, :], ms[:, s % 2, :], eps[:, :],
                                                            ALU.add).then_inc(pool_root, 1)
                                    pool.wait_ge(pool_root, START + 2 * n + 2)
                                    nc.gpsimd.tensor_tensor(ro[:, s % 2, :, 0], ms[:, s % 2, :], half[:, :],
                                                            ALU.pow).then_inc(root_ready, 1)
                                    if s == 1:
                                        ahead.pool_rstd(pool, b + 1, 1 - u)
                                    if s == 3:
                                        ahead.pool_finish(pool, b + 1, 1 - u)

                    @block.vector
                    def _(dve):
                        begin(dve, att_ready, o_ready, z_done, *ahead.of_dve)
                        ahead.dve_stats(dve, 0, 0)
                        ahead.dve_normalise(dve, 0, 0)
                        with dve.Fori(0, B // 2) as pair:
                            for u in range(2):
                                b = pair * 2 + u
                                for s in range(NS + 1):
                                    if s < NS:
                                        k = uses.index(("att", s))
                                        dve.wait_ge(att_done, START + b * NS + s + 1)
                                        nc.vector.tensor_tensor(
                                            AT_sb[:, s % 2, :, :],
                                            bankW[k % 2][:, :].rearrange("p (h i) -> p h i", i=P),
                                            keep[:, :].unsqueeze(1).to_broadcast([P, 4, P]),
                                            ALU.mult).then_inc(att_ready, 1)
                                    if s == 0:
                                        ahead.dve_stats(dve, b + 1, 1 - u)
                                    if s == 3:
                                        dve.wait_ge(row_done, START + b)
                                        ahead.dve_normalise(dve, b + 1, 1 - u)
                                    if s >= 1:
                                        r = s - 1
                                        dve.wait_ge(root_ready, START + b * NS + r + 1)
                                        nc.vector.tensor_tensor(
                                            o_sb[:, r % 2, :, :],
                                            bankOo[r % 2][:, :].rearrange("p (h v) -> p h v", v=DB),
                                            ro[:, r % 2, :, :].to_broadcast([P, 4, DB]),
                                            ALU.mult).then_inc(o_ready, 1)
                                dve.wait_ge(row_done, START + b + 1)
                                nc.vector.tensor_tensor(z_sb[:, bass.ds(b * NT, NT), :], y_sb[:, u, :, :],
                                                        bankZ[:, :].rearrange("p (t e) -> p t e", e=D),
                                                        ALU.add).then_inc(z_done, 1)

        def mlp_stage():
            with ExitStack() as st:
                ahead = Ahead("m", st, RMS, z_sb, mlp_norm_col, None, want_sum=True)
                C = INTER // P
                silu = sb("silu", [P, 2, T], at=st)
                act_h = sb("act_h", [P, 2, C, T], at=st)
                warm = sb("m_warm", [P, NT], at=st)
                bankG, bankU, bankD = bank[1:3], bank[3:5], bank[5:7]
                xnT_ready = sem("m_xnT_ready", st)
                gate_done, up_done = sem("m_gate_done", st), sem("m_up_done", st)
                silu_ready, act_ready = sem("m_silu_ready", st), sem("m_act_ready", st)
                row_done = sem("m_row_done", st)
                x_done = sem("m_x_done", st)

                with nc.Block() as block:
                    @block.tensor
                    def _(pe):
                        begin(pe, gate_done, up_done, row_done, ahead.tr)
                        ahead.pe_transpose(pe, 0, 0)
                        with pe.Fori(0, B // 2) as pair:
                            for u in range(2):
                                b = pair * 2 + u
                                pe.wait_ge(xnT_ready, START + b + 1)
                                for c in range(C):
                                    n = b * C + c
                                    pe.wait_ge(silu_ready, START + n - 1)
                                    nc.tensor.matmul(bankG[c % 2][:, :], Wgate_sb[:, c * P:(c + 1) * P],
                                                     xnT[:, u, :], start=True, stop=True).then_inc(gate_done, 1)
                                    pe.wait_ge(act_ready, START + n - 1)
                                    nc.tensor.matmul(bankU[c % 2][:, :], Wup_sb[:, c * P:(c + 1) * P],
                                                     xnT[:, u, :], start=True, stop=True).then_inc(up_done, 1)
                                    if c == 2:
                                        ahead.pe_transpose(pe, b + 1, 1 - u)
                                pe.wait_ge(act_ready, START + (b + 1) * C)
                                pe.wait_ge(x_done, START + b)
                                for t in range(NT):
                                    for c in range(C):
                                        mm = nc.tensor.matmul(bankD[u][:, t * D:(t + 1) * D],
                                                              act_h[:, u, c, t * P:(t + 1) * P], Wdown_sb[:, c, :],
                                                              start=(c == 0), stop=(c == C - 1))
                                mm.then_inc(row_done, 1)

                    @block.scalar
                    def _(act):
                        begin(act, xnT_ready, silu_ready)
                        nc.scalar.activation(warm[:, :], half[:, :], ACT.Silu)
                        ahead.act_evacuate(act, 0, 0, xnT_ready)
                        with act.Fori(0, B // 2) as pair:
                            for u in range(2):
                                b = pair * 2 + u
                                for c in range(C):
                                    n = b * C + c
                                    act.wait_ge(gate_done, START + n + 1)
                                    act.wait_ge(act_ready, START + n - 1)
                                    nc.scalar.activation(silu[:, c % 2, :], bankG[c % 2][:, :],
                                                         ACT.Silu).then_inc(silu_ready, 1)
                                ahead.act_evacuate(act, b + 1, 1 - u, xnT_ready)

                    @block.vector
                    def _(dve):
                        begin(dve, act_ready, x_done, *ahead.of_dve)
                        ahead.dve_stats(dve, 0, 0)
                        ahead.dve_normalise(dve, 0, 0)
                        with dve.Fori(0, B // 2) as pair:
                            for u in range(2):
                                b = pair * 2 + u
                                ahead.dve_stats(dve, b + 1, 1 - u)
                                for c in range(C):
                                    n = b * C + c
                                    dve.wait_ge(silu_ready, START + n + 1)
                                    dve.wait_ge(up_done, START + n + 1)
                                    nc.vector.tensor_tensor(act_h[:, u, c, :], bankU[c % 2][:, :],
                                                            silu[:, c % 2, :], ALU.mult).then_inc(act_ready, 1)
                                    if c == 0:
                                        dve.wait_ge(row_done, START + b)
                                        ahead.dve_normalise(dve, b + 1, 1 - u)
                                dve.wait_ge(row_done, START + b + 1)
                                dve.wait_ge(ahead.sum, START + b + 1)
                                nc.vector.tensor_tensor(x_sb[:, bass.ds(b * NT, NT), :], xy_sb[:, u, :, :],
                                                        bankD[u][:, :].rearrange("p (t e) -> p t e", e=D),
                                                        ALU.add).then_inc(x_done, 1)

                    @block.gpsimd
                    def _(pool):
                        begin(pool, *ahead.of_pool)
                        ahead.pool_rstd(pool, 0, 0)
                        ahead.pool_finish(pool, 0, 0)
                        with pool.Fori(0, B // 2) as pair:
                            for u in range(2):
                                ahead.pool_rstd(pool, pair * 2 + u + 1, 1 - u)
                                ahead.pool_finish(pool, pair * 2 + u + 1, 1 - u)

        moe_stage("f1", store=False)
        linear_attention_stage()
        mlp_stage()
        moe_stage("f2", store=True)


_INS = ["L0_attn_a_x", "L0_attn_a_W_K", "L0_attn_a_W_Q", "L0_attn_a_W_V", "L0_attn_a_W_O",
        "L0_attn_b_attn_norm_w", "L0_attn_b_Wq", "L0_attn_b_Wk", "L0_attn_b_Wv", "L0_attn_b_Wo",
        "L0_attn_b_attn_out_norm_w", "L0_attn_b_mlp_norm_w", "L0_attn_b_Wgate", "L0_attn_b_Wup",
        "L0_attn_b_Wdown", "L0_ffn_gamma", "L0_ffn_beta", "L0_ffn_Wr", "L0_ffn_br", "L0_ffn_W1",
        "L0_ffn_b1", "L0_ffn_W2", "L0_ffn_b2"]


def kernel(**inputs):
    import numpy as _np
    import concourse.bacc as _bacc
    from concourse import mybir as _mybir
    from concourse.bass_utils import run_bass_kernel_spmd as _run

    nc = _bacc.Bacc("TRN2", target_bir_lowering=False, num_devices=1)
    arrays, args = {}, []
    for name in _INS:
        a = _np.ascontiguousarray(inputs[name])
        arrays[f"in_{name}_dram"] = a
        args.append(nc.dram_tensor(f"in_{name}_dram", a.shape, _mybir.dt.from_np(a.dtype), kind="ExternalInput").ap())
    args.append(nc.dram_tensor("out_dram", (B, T, D), f32, kind="ExternalOutput").ap())
    build_hybrid(nc, *args)
    r = _run(nc, [arrays], core_ids=[0])
    return r.results[0]["out_dram"]
```

```python
import concourse.bass as bass
from concourse import mybir
from contextlib import ExitStack, contextmanager

f32 = mybir.dt.float32
bf16 = mybir.dt.bfloat16
u32 = mybir.dt.uint32
i32 = mybir.dt.int32
ALU = mybir.AluOpType
ACT = mybir.ActivationFunctionType
AX = mybir.AxisListType

P = 128
B, T, D = 8, 512, 128
NT = T // P
EPS = 1e-5
START = 8
MASKED = -1e10

HA, DHA = 16, 64
ND = HA * NT
HB, DB = 8, 128
INTER = 512
E, F = 8, 512
FC = F // P
TOP = 2
BLK = 256
BT = BLK // P
MAX_BLOCKS = B * T // BLK
W = D + 2
REGION = B * T + BLK


def build_hybrid(nc, x, W_K, W_Q, W_V, W_O, attn_norm_w, Wq, Wk, Wv, Wo, out_norm_w, mlp_norm_w,
                 Wgate, Wup, Wdown, gamma, beta, Wr, br, W1, b1, W2, b2, out):
    root = ExitStack()
    with root:
        def sb(name, shape, dt=f32, at=root):
            return at.enter_context(nc.sbuf_tensor(name, shape, dt))

        def sem(name, at=root):
            if at is root:
                return at.enter_context(nc.semaphore(name))
            handle = nc.alloc_semaphore(name=name)
            at.semaphores.append(handle)
            return handle

        @contextmanager
        def stage():
            with ExitStack() as st:
                st.semaphores = []
                yield st
                nc.clear_and_free_semaphores(st.semaphores)
                nc.all_engine_barrier()

        bank = [root.enter_context(nc.psum_tensor(f"bank{k}", [P, 512], f32)) for k in range(8)]

        x_sb = sb("x_sb", [P, (B + 1) * NT, D])
        z_sb = sb("z_sb", [P, (B + 1) * NT, D])
        M_sb = sb("M_sb", [P, HA, D])
        U_sb = sb("U_sb", [P, HA, D])
        A_sb = sb("A_sb", [P, HB, D])
        Wv_sb = sb("Wv_sb", [P, HB * DB])
        Wo_sb = sb("Wo_sb", [P, HB, D])
        Wgate_sb = sb("Wgate_sb", [P, INTER])
        Wup_sb = sb("Wup_sb", [P, INTER])
        Wdown_sb = sb("Wdown_sb", [P, INTER // P, D])
        W1_sb = sb("W1_sb", [P, E, F])
        W2_sb = sb("W2_sb", [P, E, FC, D])
        Wr_sb = sb("Wr_sb", [P, E])
        br_sb = sb("br_sb", [P, E])
        wn_sb = sb("wn_sb", [P, D])
        cols = sb("cols", [P, E * FC + 5])
        b1_col = cols[:, 0:E * FC]
        gamma_col, beta_col, attn_norm_col, out_norm_col, mlp_norm_col = (
            cols[:, E * FC + k:E * FC + k + 1] for k in range(5))
        moe_const = sb("moe_const", [P, E, D])
        spare = sb("spare", [1, 16])
        gates = sb("gates", [P, (B + 1) * NT, TOP])
        token = sb("token", [P, (B + 1) * NT])
        fill = sb("fill", [P, BT, W])
        blocks = sb("blocks", [P, E], i32)
        fill_at = sb("fill_at", [P, E], i32)
        region_at = sb("region_at", [P, E])
        full_blocks = sb("full_blocks", [P, MAX_BLOCKS])
        run_bf = sb("run_bf", [P, E], bf16)
        ones_bf = sb("ones_bf", [P, P], bf16)
        before_bf = sb("before_bf", [P, P], bf16)
        ident = sb("ident", [P, P])
        ident_bf = sb("ident_bf", [P, P], bf16)
        mask_bf = sb("mask_bf", [P, P], bf16)
        keep = sb("keep", [P, P])
        expert_id = sb("expert_id", [P, E])
        half = sb("half", [P, NT])
        eps = sb("eps", [P, NT])
        per_dim = sb("per_dim", [P, NT])
        unit = sb("unit", [P, NT])
        xg = nc.dram_tensor("expert_in", (E * REGION, W), f32, kind="Internal").ap()
        yg = nc.dram_tensor("expert_out", (TOP * B * T + BLK, D), f32, kind="Internal").ap()

        s_xload = sem("s_xload")
        s_store = sem("s_store")

        with stage() as st:
            WK_sb = sb("WK_sb", [P, HA // 2, D], at=st)
            WQ_sb = sb("WQ_sb", [P, HA // 2, D], at=st)
            WV_sb = sb("WV_sb", [P, HA // 2, D], at=st)
            WO_sb = sb("WO_sb", [P, HA * DHA], at=st)
            WOT_sb = sb("WOT_sb", [P, HA // 2, D], at=st)
            Wq_sb = sb("Wq_sb", [P, HB * DB], at=st)
            Wk_sb = sb("Wk_sb", [P, HB * DB], at=st)
            WqT_sb = sb("WqT_sb", [P, HB, D], at=st)
            WkT_sb = sb("WkT_sb", [P, HB, D], at=st)
            Wo_raw = sb("Wo_raw", [P, HB, D], at=st)
            rows = sb("rows", [E * FC + 5, P], at=st)
            b2_sb = sb("b2_sb", [E, D], at=st)
            c_sb = sb("c_sb", [E, D], at=st)
            ones = sb("ones", [E, P], at=st)
            const_e = sb("const_e", [E, D], at=st)
            const_diag = sb("const_diag", [E, E, D], at=st)
            rb1 = sb("rb1", [P, E, FC, E], at=st)
            zero = sb("zero", [P, P], at=st)
            zero_bf = sb("zero_bf", [P, P], bf16, at=st)
            s_diag = sem("s_diag")
            s_moe = sem("s_moe")

            s_heads = sem("s_heads")
            s_lin = sem("s_lin")
            s_small = sem("s_small")
            s_big = sem("s_big")
            s_fill = sem("s_fill")
            s_const = sem("s_const")
            s_prod = sem("s_prod")
            s_evac = sem("s_evac")
            s_rows = sem("s_rows")
            s_cols = sem("s_cols")
            s_rb1 = sem("s_rb1")
            s_c = sem("s_c")
            s_csum = sem("s_csum")
            s_dve = sem("s_dve")

            CONSTS = 21

            with nc.Block() as block:
                @block.sync
                def _(sp):
                    for w_sb, w in ((WK_sb, W_K), (WQ_sb, W_Q), (WV_sb, W_V)):
                        sp.dma_start(w_sb[:, :, :], w.rearrange("(t a) d e -> (a d) t e", a=2)).then_inc(s_heads, 16)
                    sp.dma_start(WO_sb[:, :], W_O).then_inc(s_heads, 16)
                    for b in range(B):
                        sp.dma_start(x_sb[:, b * NT:(b + 1) * NT, :],
                                     x[b].rearrange("(t p) e -> p t e", p=P)).then_inc(s_xload, 16)
                    sp.dma_start(W1_sb[:, :, :], W1.rearrange("e h f -> h e f")).then_inc(s_big, 16)
                    sp.dma_start(W2_sb[:, :, :, :], W2.rearrange("e (c f) h -> f e c h", f=P)).then_inc(s_big, 16)
                    sp.dma_start(Wv_sb[:, :], Wv).then_inc(s_big, 16)
                    sp.dma_start(Wgate_sb[:, :], Wgate).then_inc(s_big, 16)
                    sp.dma_start(Wup_sb[:, :], Wup).then_inc(s_big, 16)
                    sp.dma_start(Wdown_sb[:, :, :], Wdown.rearrange("(c f) d -> f c d", f=P)).then_inc(s_big, 16)

                @block.gpsimd
                def _(pool):
                    nc.gpsimd.memset(zero[:, :], 0.0).then_inc(s_fill, 1)
                    nc.gpsimd.memset(zero_bf[:, :], 0.0).then_inc(s_fill, 1)
                    nc.gpsimd.memset(half[:, :], -0.5).then_inc(s_const, 1)
                    nc.gpsimd.memset(eps[:, :], EPS).then_inc(s_const, 1)
                    nc.gpsimd.memset(per_dim[:, :], 1.0 / DB).then_inc(s_const, 1)
                    nc.gpsimd.memset(ones[:, :], 1.0).then_inc(s_const, 1)
                    nc.gpsimd.memset(unit[:, :], 1.0).then_inc(s_const, 1)
                    nc.gpsimd.memset(x_sb[:, B * NT:, :], 0.0).then_inc(s_const, 1)
                    nc.gpsimd.memset(z_sb[:, :, :], 0.0).then_inc(s_const, 1)
                    nc.gpsimd.iota(expert_id[:, :], pattern=[[1, E]], base=0, channel_multiplier=0,
                                   allow_small_or_imprecise_dtypes=True).then_inc(s_const, 1)
                    nc.gpsimd.iota(region_at[:, :], pattern=[[REGION, E]], base=0, channel_multiplier=0,
                                   allow_small_or_imprecise_dtypes=True).then_inc(s_const, 1)
                    nc.gpsimd.iota(full_blocks[:, :], pattern=[[BLK, MAX_BLOCKS]], base=0, channel_multiplier=0,
                                   allow_small_or_imprecise_dtypes=True).then_inc(s_const, 1)
                    nc.gpsimd.memset(ones_bf[:, :], 1.0).then_inc(s_const, 1)
                    nc.gpsimd.memset(gates[:, B * NT:, :], 0.0).then_inc(s_const, 1)
                    nc.gpsimd.memset(fill[:, :, 0:D], 0.0).then_inc(s_const, 1)
                    nc.gpsimd.memset(fill[:, :, D + 1], -1.0).then_inc(s_const, 1)
                    nc.gpsimd.iota(fill[:, :, D], pattern=[[P, BT]], base=(TOP - 1) * B * T, channel_multiplier=1,
                                   allow_small_or_imprecise_dtypes=True).then_inc(s_const, 1)
                    nc.gpsimd.iota(token[:, :], pattern=[[P, (B + 1) * NT]], base=0, channel_multiplier=1,
                                   allow_small_or_imprecise_dtypes=True).then_inc(s_const, 1)
                    pool.wait_ge(s_fill, 2)
                    nc.gpsimd.affine_select(out=ident[:, :], in_=zero[:, :], compare_op=ALU.not_equal, fill=1.0,
                                            base=0, pattern=[[-1, P]], channel_multiplier=1).then_inc(s_const, 1)
                    nc.gpsimd.affine_select(out=ident_bf[:, :], in_=zero_bf[:, :], compare_op=ALU.not_equal, fill=1.0,
                                            base=0, pattern=[[-1, P]], channel_multiplier=1).then_inc(s_const, 1)
                    nc.gpsimd.affine_select(out=mask_bf[:, :], in_=zero_bf[:, :], compare_op=ALU.is_ge, fill=MASKED,
                                            base=0, pattern=[[-1, P]], channel_multiplier=1).then_inc(s_const, 1)
                    nc.gpsimd.affine_select(out=before_bf[:, :], in_=zero_bf[:, :], compare_op=ALU.is_ge, fill=1.0,
                                            base=0, pattern=[[-1, P]], channel_multiplier=1).then_inc(s_const, 1)
                    nc.gpsimd.affine_select(out=keep[:, :], in_=zero[:, :], compare_op=ALU.is_gt, fill=1.0,
                                            base=0, pattern=[[-1, P]], channel_multiplier=1).then_inc(s_const, 1)

                @block.scalar
                def _(act):
                    act.dma_start(rows[0:E * FC, :], b1.rearrange("e (c f) -> (e c) f", f=P)).then_inc(s_small, 16)
                    for k, v in enumerate((gamma, beta, attn_norm_w, out_norm_w, mlp_norm_w)):
                        act.dma_start(rows[E * FC + k:E * FC + k + 1, :],
                                      v.rearrange("(a n) -> a n", a=1)).then_inc(s_small, 16)
                    act.dma_start(b2_sb[:, :], b2).then_inc(s_small, 16)
                    act.dma_start(Wr_sb[:, :], Wr).then_inc(s_small, 16)
                    act.dma_start(br_sb[:, :], br.partition_broadcast(P)).then_inc(s_small, 16)
                    act.dma_start(wn_sb[:, :], attn_norm_w.partition_broadcast(P)).then_inc(s_small, 16)
                    act.dma_start(Wq_sb[:, :], Wq).then_inc(s_lin, 16)
                    act.dma_start(Wk_sb[:, :], Wk).then_inc(s_lin, 16)
                    act.dma_start(Wo_raw[:, :, :], Wo.rearrange("(h v) d -> v h d", v=DB)).then_inc(s_lin, 16)
                    job = 0
                    for dst, step, scale in (
                            (M_sb, 2, DHA ** -0.5), (WOT_sb, 1, 1.0), (WqT_sb, 1, 1.0), (WkT_sb, 1, 1.0),
                            (U_sb, 2, 1.0), (A_sb, 1, 1.0)):
                        for k in range(2 * step):
                            first = (k // 2) + step * 4 * (k % 2)
                            act.wait_ge(s_prod, job + 1)
                            nc.scalar.activation(dst[:, first:first + 3 * step + 1:step, :],
                                                 bank[job % 7][:, :].rearrange("p (h e) -> p h e", e=D),
                                                 ACT.Copy, scale=scale).then_inc(s_evac, 1)
                            job += 1

                @block.tensor
                def _(pe):
                    job = 0

                    def next_bank():
                        if job >= 7:
                            pe.wait_ge(s_evac, job - 6)
                        return bank[job % 7]

                    pe.wait_ge(s_heads, 64)
                    for k in range(4):
                        ps = next_bank()
                        for m in range(4):
                            h = k // 2 + 2 * (4 * (k % 2) + m)
                            r = slice(DHA * (h % 2), DHA * (h % 2) + DHA)
                            mm = nc.tensor.matmul(ps[:, m * D:(m + 1) * D], WK_sb[r, h // 2, :], WQ_sb[r, h // 2, :],
                                                  start=True, stop=True)
                        mm.then_inc(s_prod, 1)
                        job += 1
                    pe.wait_ge(s_const, CONSTS)
                    pe.wait_ge(s_lin, 48)
                    for src in (WO_sb, Wq_sb, Wk_sb):
                        for k in range(2):
                            ps = next_bank()
                            for m in range(4):
                                c = 4 * k + m
                                mm = nc.tensor.transpose(ps[:, m * P:(m + 1) * P], src[:, c * P:(c + 1) * P],
                                                         ident[:, :])
                            mm.then_inc(s_prod, 1)
                            job += 1
                    for k in range(4):
                        ps = next_bank()
                        if k == 0:
                            pe.wait_ge(s_evac, 6)
                        for m in range(4):
                            h = k // 2 + 2 * (4 * (k % 2) + m)
                            r = slice(DHA * (h % 2), DHA * (h % 2) + DHA)
                            mm = nc.tensor.matmul(ps[:, m * D:(m + 1) * D], WV_sb[r, h // 2, :], WOT_sb[r, h // 2, :],
                                                  start=True, stop=True)
                        mm.then_inc(s_prod, 1)
                        job += 1
                    for k in range(2):
                        ps = next_bank()
                        if k == 0:
                            pe.wait_ge(s_evac, 10)
                        for m in range(4):
                            h = 4 * k + m
                            mm = nc.tensor.matmul(ps[:, m * D:(m + 1) * D], WqT_sb[:, h, :], WkT_sb[:, h, :],
                                                  start=True, stop=True)
                        mm.then_inc(s_prod, 1)
                        job += 1
                    pe.wait_ge(s_small, 160)
                    n = E * FC + 5
                    nc.tensor.transpose(bank[7][:, 0:n], rows[:, :], ident[0:n, 0:n]).then_inc(s_rows, 1)
                    pe.wait_ge(s_rb1, E)
                    pe.wait_ge(s_big, 96)
                    for e in range(E):
                        for c in range(FC):
                            mm = nc.tensor.matmul(bank[7][0:E, 0:D], rb1[:, e, c, :], W2_sb[:, e, c, :],
                                                  start=(e == 0 and c == 0), stop=(e == E - 1 and c == FC - 1))
                    mm.then_inc(s_c, 1)
                    pe.wait_ge(s_dve, 3)
                    nc.tensor.matmul(bank[7][0:E, 0:D], ones[:, 0:E], c_sb[:, :], start=True, stop=True).then_inc(s_csum, 1)
                    pe.wait_ge(s_diag, 1)
                    pe.wait_ge(s_evac, 16)
                    for g in range(2):
                        nc.tensor.matmul(bank[5 + g][:, :], ones[:, :], const_diag[:, 4 * g:4 * g + 4, :],
                                         start=True, stop=True).then_inc(s_moe, 1)

                @block.vector
                def _(dve):
                    nc.vector.memset(rb1[:, :, :, :], 0.0).then_inc(s_dve, 1)
                    dve.wait_ge(s_rows, 1)
                    nc.vector.tensor_copy(cols[:, :], bank[7][:, 0:E * FC + 5]).then_inc(s_cols, 1)
                    dve.wait_ge(s_cols, 1)
                    dve.wait_ge(s_dve, 1)
                    for e in range(E):
                        nc.vector.tensor_scalar(rb1[:, e, :, e], b1_col[:, e * FC:(e + 1) * FC], 0.0, None,
                                                ALU.max).then_inc(s_rb1, 1)
                    nc.vector.tensor_scalar(Wo_sb[:, :, :], Wo_raw[:, :, :], out_norm_col, None,
                                            ALU.mult).then_inc(s_dve, 1)
                    dve.wait_ge(s_c, 1)
                    nc.vector.tensor_tensor(c_sb[:, :], bank[7][0:E, 0:D], b2_sb[:, :], ALU.add).then_inc(s_dve, 1)
                    dve.wait_ge(s_dve, 3)
                    nc.vector.tensor_tensor(b2_sb[:, :], b2_sb[:, :], c_sb[:, :], ALU.subtract).then_inc(s_dve, 1)
                    dve.wait_ge(s_csum, 1)
                    dve.wait_ge(s_dve, 4)
                    nc.vector.tensor_tensor(const_e[:, :], bank[7][0:E, 0:D], b2_sb[:, :],
                                            ALU.add).then_inc(s_dve, 1)
                    dve.wait_ge(s_dve, 5)
                    dve.wait_ge(s_const, CONSTS)
                    nc.vector.tensor_tensor(const_diag[:, :, :], const_e[:, :].unsqueeze(1).to_broadcast([E, E, D]),
                                            ident[0:E, 0:E].unsqueeze(2).to_broadcast([E, E, D]),
                                            ALU.mult).then_inc(s_diag, 1)
                    for g in range(2):
                        dve.wait_ge(s_moe, g + 1)
                        nc.vector.tensor_copy(moe_const[:, 4 * g:4 * g + 4, :],
                                              bank[5 + g][:, :].rearrange("p (e d) -> p e d", d=D)).then_inc(s_dve, 1)

        def uses_ago(n, ring, per_row):
            if n >= ring:
                return ring
            return min(ring, per_row + n - max(m for m in range(per_row) if m % ring == n))

        LN, LN_LN, RMS = range(3)

        class Ahead:

            def __init__(self, name, at, kind, src, scale, bias, want_sum=False, want_htok=False,
                         in_place=False, bankT=bank[0]):
                self.bankT, self.in_place = bankT, in_place
                self.kind, self.src, self.scale, self.bias = kind, src, scale, bias
                self.want_y = kind == LN_LN and not in_place
                self.want_sum, self.want_htok = want_sum, want_htok
                self.bn = sb(name + "_bn", [P, 2, NT, 6], at=at)
                self.mv = sb(name + "_mv", [P, 2, NT, 2], at=at)
                self.power = sb(name + "_power", [P, 2, 8, NT], at=at)
                self.xn_sb = sb(name + "_xn", [P, 2, NT, W if in_place else D], at=at)
                self.xnT = sb(name + "_xnT", [P, 2, T], at=at)
                if self.want_y:
                    self.y_sb = sb(name + "_y", [P, 2, NT, D], at=at)
                if want_sum:
                    self.sum_sb = sb(name + "_xz", [P, 2, NT, D], at=at)
                if want_htok:
                    self.htok_sb = sb(name + "_htok", [P, 2, NT, D], at=at)
                self.stats = sem(name + "_stats_ready", at)
                self.counted = sem(name + "_stats_counted", at)
                self.moments = sem(name + "_moments_ready", at)
                self.pool_step = sem(name + "_pool_step", at)
                self.rstd = sem(name + "_rstd_ready", at)
                self.xn = sem(name + "_xn_ready", at)
                self.y = sem(name + "_y_ready", at)
                self.sum = sem(name + "_sum_ready", at)
                self.htok = sem(name + "_htok_ready", at)
                self.tr = sem(name + "_transposed", at)
                self.of_dve = (self.stats, self.moments, self.xn, self.y)
                self.of_pool = (self.pool_step, self.rstd, self.sum, self.htok)

            def tiles(self, b, where=None):
                return (self.src if where is None else where)[:, bass.ds(b * NT, NT), :]

            def dve_stats(self, dve, b, u):
                for t in range(NT):
                    nc.vector.bn_stats(self.bn[:, u, t, :],
                                       self.src[:, bass.ds(b * NT + t, 1), :]).then_inc(self.stats, 1)
                dve.wait_ge(self.stats, START + b * NT + NT)
                dve.sem_inc(self.counted, 1)
                for t in range(NT):
                    nc.vector.bn_aggr(self.mv[:, u, t, :], self.bn[:, u, t, :]).then_inc(self.moments, 1)

            def pool_rstd(self, pool, b, u):
                pw = [self.power[:, u, k, :] for k in range(8)]
                mean, var = self.mv[:, u, :, 0], self.mv[:, u, :, 1]
                TT = nc.gpsimd.tensor_tensor
                per_row = {LN: 1, LN_LN: 7 if self.in_place else 5, RMS: 3}[self.kind]
                done = [0]

                def then_next(ins):
                    done[0] += 1
                    ins.then_inc(self.pool_step, 1)
                    pool.wait_ge(self.pool_step, START + b * per_row + done[0])

                pool.wait_ge(self.moments, START + b * NT + NT)
                if self.kind == RMS:
                    then_next(TT(pw[1], mean, mean, ALU.mult))
                    then_next(TT(pw[2], pw[1], var, ALU.add))
                    then_next(TT(pw[3], pw[2], eps[:, :], ALU.add))
                    TT(pw[5], pw[3], half[:, :], ALU.pow).then_inc(self.rstd, 1)
                    return
                then_next(TT(pw[1], var, eps[:, :], ALU.add))
                if self.kind == LN:
                    TT(pw[5], pw[1], half[:, :], ALU.pow).then_inc(self.rstd, 1)
                    return
                then_next(TT(pw[0], pw[1], half[:, :], ALU.pow))
                if self.in_place:
                    TT(pw[6], pw[0], unit[:, :], ALU.add).then_inc(self.pool_step, 1)
                    TT(pw[7], pw[0], mean, ALU.mult).then_inc(self.pool_step, 1)
                    done[0] += 2
                then_next(TT(pw[2], pw[0], pw[0], ALU.mult))
                then_next(TT(pw[3], pw[2], var, ALU.mult))
                then_next(TT(pw[4], pw[3], eps[:, :], ALU.add))
                TT(pw[2], pw[4], half[:, :], ALU.pow).then_inc(self.rstd, 1)
                pool.wait_ge(self.rstd, START + 2 * b + 1)
                TT(pw[5], pw[0], pw[2], ALU.mult).then_inc(self.rstd, 1)

            def dve_normalise(self, dve, b, u):
                dve.wait_ge(self.rstd, START + ((2 * b + 2) if self.kind == LN_LN else (b + 1)))
                for t in range(NT):
                    tile = self.src[:, bass.ds(b * NT + t, 1), :]
                    if self.kind == RMS:
                        nc.vector.tensor_scalar(self.xn_sb[:, u, t:t + 1, 0:D], tile, self.power[:, u, 5, t:t + 1], None,
                                                ALU.mult).then_inc(self.xn, 1)
                        continue
                    mean = self.mv[:, u, t, 0:1]
                    nc.vector.tensor_scalar(self.xn_sb[:, u, t:t + 1, 0:D], tile, mean, self.power[:, u, 5, t:t + 1],
                                            ALU.subtract, ALU.mult).then_inc(self.xn, 1)
                    if self.want_y:
                        nc.vector.tensor_scalar(self.y_sb[:, u, t:t + 1, :], tile, mean, self.power[:, u, 0, t:t + 1],
                                                ALU.subtract, ALU.mult).then_inc(self.y, 1)
                if self.in_place:
                    for t in range(NT):
                        tile = self.src[:, bass.ds(b * NT + t, 1), :]
                        nc.vector.tensor_scalar(tile, tile, self.power[:, u, 6, t:t + 1], self.power[:, u, 7, t:t + 1],
                                                ALU.mult, ALU.subtract).then_inc(self.y, 1)

            def pool_finish(self, pool, b, u):
                pool.wait_ge(self.xn, START + b * NT + NT)
                if self.want_sum:
                    nc.gpsimd.tensor_tensor(self.sum_sb[:, u, :, :], self.tiles(b, x_sb), self.tiles(b),
                                            ALU.add).then_inc(self.sum, 1)
                if self.want_htok:
                    nc.gpsimd.tensor_tensor(self.htok_sb[:, u, :, :], self.xn_sb[:, u, :, :],
                                            wn_sb[:, :].unsqueeze(1).to_broadcast([P, NT, D]),
                                            ALU.mult).then_inc(self.htok, 1)

            def pe_transpose(self, pe, b, u):
                pe.wait_ge(self.xn, START + b * NT + NT)
                for t in range(NT):
                    mm = nc.tensor.transpose(self.bankT[:, t * P:(t + 1) * P], self.xn_sb[:, u, t, 0:D], ident[:, :])
                mm.then_inc(self.tr, 1)

            def act_evacuate(self, act, b, u, done):
                act.wait_ge(self.tr, START + b + 1)
                if self.bias is not None:
                    nc.scalar.activation(self.xnT[:, u, :], self.bankT[:, :], ACT.Identity, bias=self.bias,
                                         scale=self.scale).then_inc(done, 1)
                else:
                    nc.scalar.activation(self.xnT[:, u, :], self.bankT[:, :], ACT.Copy, scale=self.scale).then_inc(done, 1)

        def begin(eng, *semaphores):
            for s in semaphores:
                eng.sem_inc(s, START)

        def each_row(eng, row):
            row(0, 0)
            with eng.Fori(0, B // 2 - 1) as pair:
                row(pair * 2 + 1, 1)
                row(pair * 2 + 2, 0)
            row(B - 1, 1)

        def is_row(b, which):
            return isinstance(b, int) and b == which

        PRIMED = 16

        def prime(pool, *semaphores):
            for s in semaphores:
                col = primed[0]
                primed[0] += 1
                pool.dma_start(spare[:, col:col + 1], z_sb[0:1, B * NT, col:col + 1]).then_inc(s, PRIMED)
            for s in semaphores:
                pool.wait_ge(s, PRIMED)

        primed = [0]

        class Route:

            LOGIT, RMAX, TOPS = 1, 2, 3 + NT
            TOPID = TOPS + 1 + NT
            IDS, IS_K, ROW_SEL = TOPID + 2, TOPID + 4, TOPID + 5
            PLACE, PICKED, SLOTF = ROW_SEL + 1, ROW_SEL + 3, ROW_SEL + 4
            DVE_STEPS = SLOTF
            wide = [P, NT, E]

            def __init__(self, name, at, bankR):
                self.bankR = bankR
                self.norm = Ahead(name, at, LN_LN, x_sb, gamma_col, beta_col, in_place=True, bankT=bankR)
                self.logit = sb(name + "_logit", [P, NT, E], f32, at=at)
                self.shifted = sb(name + "_shifted", [P, NT, E], f32, at=at)
                self.ex = sb(name + "_ex", [P, NT, E], f32, at=at)
                self.top = sb(name + "_top", [P, NT, E], f32, at=at)
                self.topid = sb(name + "_topid", [P, NT, E], u32, at=at)
                self.topidf = sb(name + "_topidf", [P, NT, E], f32, at=at)
                self.rmax = sb(name + "_rmax", [P, NT, 1], f32, at=at)
                self.rsum = sb(name + "_rsum", [P, NT, 1], f32, at=at)
                self.rrec = sb(name + "_rrec", [P, NT, 1], f32, at=at)
                self.is_k = sb(name + "_is_k", [P, TOP, NT, E], at=at)
                self.picked = sb(name + "_picked", [P, TOP, NT, E], at=at)
                self.sel = sb(name + "_sel", [P, NT, E], bf16, at=at)
                self.row_sel = sb(name + "_row_sel", [P, E], at=at)
                self.run = sb(name + "_run", [P, E], at=at)
                self.place = sb(name + "_place", [P, NT, E], at=at)
                self.slotf = sb(name + "_slotf", [P, TOP, NT], at=at)
                self.slot = sb(name + "_slot", [P, 2, NT, TOP], i32, at=at)
                self.logits_ready = sem(name + "_logits_ready", at)
                self.shifted_ready = sem(name + "_shifted_ready", at)
                self.ex_ready = sem(name + "_ex_ready", at)
                self.step = sem(name + "_route_step", at)
                self.sel_ready = sem(name + "_sel_ready", at)
                self.run_ready = sem(name + "_run_ready", at)
                self.rank_ready = sem(name + "_rank_ready", at)
                self.slot_ready = sem(name + "_slot_ready", at)
                self.tagged = sem(name + "_tagged", at)
                self.xnT_ready = sem(name + "_xnT_ready", at)
                self.may_scatter = sem(name + "_may_scatter", at)
                self.scattered = [sem(f"{name}_scattered{u}", at) for u in range(2)]
                self.of_dve = (self.shifted_ready, self.step, self.sel_ready, self.run_ready, self.slot_ready,
                               self.tagged, *self.norm.of_dve)
                self.of_pe = (self.logits_ready, self.rank_ready, self.norm.tr)
                self.of_act = (self.ex_ready, self.xnT_ready)
                self.of_pool = self.norm.of_pool

            def dve_begin(self, dve):
                nc.vector.memset(self.run[:, :], 0.0).then_inc(self.run_ready, 1)
                nc.vector.memset(run_bf[:, :], 0.0).then_inc(self.run_ready, 1)

            def pe_logits(self, pe, b, u):
                pe.wait_ge(self.xnT_ready, START + b + 1)
                pe.wait_ge(self.slot_ready, START + b)
                for t in range(NT):
                    mm = nc.tensor.matmul(self.bankR[:, t * E:(t + 1) * E], self.norm.xnT[:, u, t * P:(t + 1) * P],
                                          Wr_sb[:, :], start=True, stop=True)
                mm.then_inc(self.logits_ready, 1)

            def settle(self, dve, b, count):
                dve.wait_ge(self.step, START + b * self.DVE_STEPS + count)

            def dve_logit(self, dve, b, u):
                dve.wait_ge(self.logits_ready, START + b + 1)
                nc.vector.tensor_tensor(
                    self.logit[:, :, :], self.bankR[:, 0:NT * E].rearrange("p (t e) -> p t e", e=E),
                    br_sb[:, :].unsqueeze(1).to_broadcast(self.wide), ALU.add).then_inc(self.step, 1)

            def dve_rmax(self, dve, b, u):
                self.settle(dve, b, self.LOGIT)
                nc.vector.tensor_reduce(self.rmax[:, :, 0], self.logit[:, :, :], AX.X, ALU.max).then_inc(self.step, 1)

            def dve_shift(self, dve, b, u):
                self.settle(dve, b, self.RMAX)
                nc.vector.tensor_tensor(self.shifted[:, :, :], self.logit[:, :, :],
                                        self.rmax[:, :, :].to_broadcast(self.wide),
                                        ALU.subtract).then_inc(self.shifted_ready, 1)

            def act_exp(self, act, b, u):
                act.wait_ge(self.shifted_ready, START + b + 1)
                nc.scalar.activation(self.ex[:, :, :], self.shifted[:, :, :], ACT.Exp).then_inc(self.ex_ready, 1)

            def dve_top(self, dve, b, u):
                dve.wait_ge(self.ex_ready, START + b + 1)
                nc.vector.tensor_reduce(self.rsum[:, :, 0], self.ex[:, :, :], AX.X, ALU.add).then_inc(self.step, 1)
                for t in range(NT):
                    nc.vector.max(self.top[:, t, :], self.ex[:, t, :]).then_inc(self.step, 1)

            def dve_topid(self, dve, b, u):
                self.settle(dve, b, self.TOPS)
                nc.vector.reciprocal(self.rrec[:, :, :], self.rsum[:, :, :]).then_inc(self.step, 1)
                for t in range(NT):
                    nc.vector.max_index(self.topid[:, t, :], self.top[:, t, :], self.ex[:, t, :]).then_inc(self.step, 1)

            def dve_ids(self, dve, b, u):
                self.settle(dve, b, self.TOPID)
                nc.vector.tensor_copy(self.topidf[:, :, :], self.topid[:, :, :]).then_inc(self.step, 1)
                nc.vector.tensor_tensor(gates[:, bass.ds(b * NT, NT), :], self.top[:, :, 0:TOP],
                                        self.rrec[:, :, :].to_broadcast([P, NT, TOP]), ALU.mult).then_inc(self.step, 1)

            def dve_is_k(self, dve, b, u):
                self.settle(dve, b, self.IDS)
                nc.vector.tensor_copy(self.norm.xn_sb[:, u, :, D], token[:, bass.ds(b * NT, NT)]
                                      ).then_inc(self.tagged, 1)
                nc.vector.tensor_copy(self.norm.xn_sb[:, u, :, D + 1], self.topidf[:, :, 0]).then_inc(self.tagged, 1)
                for k in range(TOP):
                    nc.vector.tensor_tensor(self.is_k[:, k, :, :],
                                            expert_id[:, :].unsqueeze(1).to_broadcast(self.wide),
                                            self.topidf[:, :, k:k + 1].to_broadcast(self.wide),
                                            ALU.is_equal).then_inc(self.step, 1)

            def dve_sel(self, dve, b, u):
                self.settle(dve, b, self.IS_K)
                nc.vector.tensor_tensor(self.sel[:, :, :], self.is_k[:, 0, :, :], self.is_k[:, 1, :, :],
                                        ALU.add).then_inc(self.sel_ready, 1)

            def dve_row_sel(self, dve, b, u):
                dve.wait_ge(self.sel_ready, START + b + 1)
                nc.vector.tensor_reduce(self.row_sel[:, :], self.sel[:, :, :].rearrange("p t e -> p e t"),
                                        AX.X, ALU.add).then_inc(self.step, 1)

            def pe_rank(self, pe, b, u):
                pe.wait_ge(self.sel_ready, START + b + 1)
                pe.wait_ge(self.run_ready, START + 2 * b + 2)
                c0 = NT * E
                nc.tensor.matmul(self.bankR[:, c0:2 * c0], before_bf[:, :], self.sel[:, :, :], start=True, stop=False)
                for d in range(1, NT):
                    nc.tensor.matmul(self.bankR[:, c0 + d * E:2 * c0], ones_bf[:, :], self.sel[:, 0:NT - d, :],
                                     start=False, stop=False, skip_group_check=True)
                nc.tensor.matmul(self.bankR[:, c0:2 * c0], ones_bf[:, :],
                                 run_bf[:, :].unsqueeze(1).to_broadcast([P, NT, E]), start=False,
                                 stop=True).then_inc(self.rank_ready, 1)

            def dve_place(self, dve, b, u):
                dve.wait_ge(self.rank_ready, START + b + 1)
                self.settle(dve, b, self.ROW_SEL)
                nc.vector.tensor_tensor(
                    self.place[:, :, :], self.bankR[:, NT * E:2 * NT * E].rearrange("p (t e) -> p t e", e=E),
                    region_at[:, :].unsqueeze(1).to_broadcast(self.wide), ALU.add).then_inc(self.step, 1)
                dve.wait_ge(self.run_ready, START + 2 * b + 2)
                nc.vector.tensor_tensor(self.run[:, :], self.run[:, :], self.row_sel[:, :],
                                        ALU.add).then_inc(self.run_ready, 1)

            def dve_picked(self, dve, b, u):
                self.settle(dve, b, self.PLACE)
                for k in range(TOP):
                    nc.vector.tensor_tensor(self.picked[:, k, :, :], self.is_k[:, k, :, :],
                                            self.place[:, :, :], ALU.mult).then_inc(self.step, 1)
                dve.wait_ge(self.run_ready, START + 2 * b + 3)
                nc.vector.tensor_copy(run_bf[:, :], self.run[:, :]).then_inc(self.run_ready, 1)

            def dve_slotf(self, dve, b, u):
                self.settle(dve, b, self.PICKED)
                nc.vector.tensor_reduce(self.slotf[:, :, :], self.picked[:, :, :, :], AX.X,
                                        ALU.add).then_inc(self.step, 1)

            def dve_slots(self, dve, b, u):
                self.settle(dve, b, self.SLOTF)
                dve.wait_ge(self.scattered[u], PRIMED + (b - u) * (8 * TOP * NT))
                by_tile = self.slotf[:, :, :].rearrange("p k t -> p t k")
                nc.vector.tensor_copy(self.slot[:, u, :, :], by_tile).then_inc(self.slot_ready, 1)

            def dve_normalise(self, dve, b, u):
                dve.wait_ge(self.scattered[u], PRIMED + (b - u) * (8 * TOP * NT))
                self.norm.dve_normalise(dve, b, u)

            def pool_scatter(self, pool, b, u, tiles=range(NT)):
                pool.wait_ge(self.slot_ready, START + b + 1)
                pool.wait_ge(self.norm.xn, START + b * NT + NT)
                pool.wait_ge(self.tagged, START + 2 * b + 2)
                pool.sem_inc(self.may_scatter, 1)
                for t in tiles:
                    for k in range(TOP):
                        pool.indirect_dma_start(
                            xg, bass.IndirectOffsetOnAxis(ap=self.slot[:, u, t, k:k + 1], axis=0),
                            self.norm.xn_sb[:, u, t, :], None).then_inc(self.scattered[u], 16)

        with stage() as st:
            ahead = Ahead("a", st, LN, x_sb, 1.0, None)
            width = [P * (i + 1) for i in range(NT)]
            start = [sum(width[:i]) for i in range(NT)]
            G_sb = sb("G_sb", [P, 2, T], at=st)
            Vraw = sb("Vraw", [P, 2, NT, 4, D], at=st)
            Vs = sb("Vs", [P, 8, D], at=st)
            prob = sb("prob", [P, 2, sum(width)], at=st)
            negmax = sb("negmax", [P, 8], at=st)
            rowsum = sb("rowsum", [P, 8], at=st)
            rinv = sb("rinv", [P, 8], at=st)
            warm = sb("warm", [P, NT], at=st)
            route = Route("f1", st, bank[0])
            bankT, bankO, bankG, bankV, bankS = bank[0], bank[1], bank[2], bank[3:5], bank[5:8]

            xnT_ready = sem("a_xnT_ready", st)
            G_done, G_ready = sem("a_G_done", st), sem("a_G_ready", st)
            V_done, V_ready = sem("a_V_done", st), sem("a_V_ready", st)
            scores_ready = sem("a_scores_ready", st)
            negmax_ready = sem("a_negmax_ready", st)
            prob_ready = sem("a_prob_ready", st)
            rinv_ready = sem("a_rinv_ready", st)
            Vs_ready = sem("a_Vs_ready", st)
            row_done = sem("a_row_done", st)
            x_done = sem("a_x_done", st)
            x_complete = sem("a_x_complete", st)
            ROUTE_STATS, ROUTE_NORM, ROUTE_TR, ROUTE_LOGITS, ROUTE_EXP, ROUTE_RANK = 1, 5, 11, 14, 20, 31
            ROUTE_DVE = {17: route.dve_logit, 18: route.dve_rmax, 19: route.dve_shift, 22: route.dve_top,
                         23: route.dve_topid, 24: route.dve_ids, 25: route.dve_is_k, 27: route.dve_sel,
                         28: route.dve_row_sel, 33: route.dve_place, 34: route.dve_picked, 35: route.dve_slotf,
                         36: route.dve_slots}
            STATS_AT, NORM_AT, TR_AT, EVAC_AT = 40, 44, 50, 51

            def step(n):
                return n // NT, NT - 1 - n % NT

            with nc.Block() as block:
                @block.tensor
                def _(pe):
                    begin(pe, G_done, V_done, scores_ready, row_done, ahead.tr, *route.of_pe)
                    pe.wait_ge(s_const, CONSTS)
                    ahead.pe_transpose(pe, 0, 0)

                    def G(b, u, h):
                        pe.wait_ge(G_ready, START + b * HA + h)
                        nc.tensor.matmul(bankG[:, :], M_sb[:, h, :], ahead.xnT[:, u, :], start=True,
                                         stop=True).then_inc(G_done, 1)

                    def V(b, u, g, i):
                        n = g * NT + i
                        pe.wait_ge(V_ready, START + b * (NT * 4) + n - 1)
                        nc.tensor.matmul(bankV[n % 2][:, :], ahead.xnT[:, u, i * P:(i + 1) * P],
                                         U_sb[:, 4 * g:4 * g + 4, :], start=True, stop=True).then_inc(V_done, 1)

                    def S(b, u, n):
                        h, i = step(n)
                        pe.wait_ge(G_ready, START + b * HA + h + 1)
                        pe.wait_ge(prob_ready, START + b * ND + n + 1 - uses_ago(n, len(bankS), ND))
                        ps = bankS[n % 3]
                        nc.tensor.matmul(ps[:, 0:width[i]], G_sb[:, h % 2, i * P:(i + 1) * P],
                                         ahead.xnT[:, u, 0:width[i]], start=True, stop=False)
                        nc.tensor.matmul(ps[:, i * P:(i + 1) * P], ident_bf[:, :], mask_bf[:, :], start=False,
                                         stop=True).then_inc(scores_ready, 1)

                    def PV(b, u, n):
                        h, i = step(n)
                        if n == 0:
                            pe.wait_ge(x_done, START + b)
                        pe.wait_ge(prob_ready, START + b * ND + n + 1)
                        pe.wait_ge(Vs_ready, START + b * ND + n + 1)
                        for j in range(i + 1):
                            mm = nc.tensor.matmul(bankO[:, j * D:(j + 1) * D],
                                                  prob[:, h % 2, start[i] + j * P:start[i] + (j + 1) * P],
                                                  Vs[:, n % 8, :], start=(n == 0 and j == 0),
                                                  stop=(h == HA - 1), skip_group_check=True)
                        if n == ND - 1:
                            mm.then_inc(row_done, 1)

                    def row(b, u):
                        pe.wait_ge(xnT_ready, START + b + 1)
                        for n in range(ND + NT):
                            if n == 0:
                                G(b, u, 0)
                                for i in range(NT):
                                    V(b, u, 0, i)
                                G(b, u, 1)
                            elif n < ND and n % NT == 0 and n // NT + 1 < HA:
                                G(b, u, n // NT + 1)
                            if n % NT == 2 and n // NT < HA - 4:
                                V(b, u, n // NT // 4 + 1, n // NT % 4)
                            if n < ND:
                                S(b, u, n)
                            if n >= NT:
                                PV(b, u, n - NT)
                            if not is_row(b, 0):
                                if n == ROUTE_TR:
                                    route.norm.pe_transpose(pe, b - 1, 1 - u)
                                if n == ROUTE_LOGITS:
                                    route.pe_logits(pe, b - 1, 1 - u)
                                if n == ROUTE_RANK:
                                    route.pe_rank(pe, b - 1, 1 - u)
                            if n == TR_AT and not is_row(b, B - 1):
                                if not is_row(b, 0):
                                    pe.wait_ge(route.slot_ready, START + b)
                                ahead.pe_transpose(pe, b + 1, 1 - u)

                    each_row(pe, row)
                    route.norm.pe_transpose(pe, B - 1, 1)
                    route.pe_logits(pe, B - 1, 1)
                    route.pe_rank(pe, B - 1, 1)

                @block.scalar
                def _(act):
                    begin(act, G_ready, V_ready, prob_ready, xnT_ready, *route.of_act)
                    act.wait_ge(s_const, CONSTS)
                    nc.scalar.activation(warm[:, :], half[:, :], ACT.Exp)
                    ahead.act_evacuate(act, 0, 0, xnT_ready)

                    def evac_G(b, u, h):
                        act.wait_ge(G_done, START + b * HA + h + 1)
                        act.wait_ge(scores_ready, START + b * ND + NT * (h - 1))
                        nc.scalar.activation(G_sb[:, h % 2, :], bankG[:, :], ACT.Copy).then_inc(G_ready, 1)

                    def evac_V(b, u, g, i):
                        n = g * NT + i
                        act.wait_ge(V_done, START + b * (NT * 4) + n + 1)
                        act.wait_ge(Vs_ready, START + b * ND + 4 * NT * max(g - 1, 0))
                        nc.scalar.activation(Vraw[:, g % 2, i, :, :],
                                             bankV[n % 2][:, :].rearrange("p (h e) -> p h e", e=D),
                                             ACT.Copy).then_inc(V_ready, 1)

                    def row(b, u):
                        for n in range(ND):
                            if n == 0:
                                evac_G(b, u, 0)
                                for i in range(NT):
                                    evac_V(b, u, 0, i)
                                evac_G(b, u, 1)
                            elif n % NT == 0 and n // NT + 1 < HA:
                                evac_G(b, u, n // NT + 1)
                            if n % NT == 2 and n // NT < HA - 4:
                                evac_V(b, u, n // NT // 4 + 1, n // NT % 4)
                            h, i = step(n)
                            act.wait_ge(negmax_ready, START + b * ND + n + 1)
                            nc.scalar.activation(prob[:, h % 2, start[i]:start[i] + width[i]],
                                                 bankS[n % 3][:, 0:width[i]], ACT.Exp,
                                                 bias=negmax[:, n % 8:n % 8 + 1],
                                                 accum_out=rowsum[:, n % 8:n % 8 + 1]).then_inc(prob_ready, 1)
                            if n == ROUTE_TR and not is_row(b, 0):
                                route.norm.act_evacuate(act, b - 1, 1 - u, route.xnT_ready)
                            if n == ROUTE_EXP and not is_row(b, 0):
                                route.act_exp(act, b - 1, 1 - u)
                            if n == EVAC_AT and not is_row(b, B - 1):
                                ahead.act_evacuate(act, b + 1, 1 - u, xnT_ready)

                    each_row(act, row)
                    route.norm.act_evacuate(act, B - 1, 1, route.xnT_ready)
                    route.act_exp(act, B - 1, 1)

                @block.vector
                def _(dve):
                    begin(dve, negmax_ready, rinv_ready, Vs_ready, x_done, *ahead.of_dve, *route.of_dve)
                    route.dve_begin(dve)
                    dve.wait_ge(s_xload, 16 * B)
                    ahead.dve_stats(dve, 0, 0)
                    ahead.dve_normalise(dve, 0, 0)
                    def route_stats(b, u):
                        dve.wait_ge(x_done, START + b + 1)
                        dve.sem_inc(x_complete, 1)
                        route.norm.dve_stats(dve, b, u)

                    def row(b, u):
                        for n in range(ND + 2):
                            if n < ND:
                                h, i = step(n)
                                dve.wait_ge(scores_ready, START + b * ND + n + 1)
                                nc.vector.tensor_reduce(negmax[:, n % 8:n % 8 + 1],
                                                        bankS[n % 3][:, 0:width[i]], AX.X, ALU.max,
                                                        negate=True).then_inc(negmax_ready, 1)
                            if 1 <= n <= ND:
                                m = n - 1
                                dve.wait_ge(prob_ready, START + b * ND + m + 1)
                                nc.vector.reciprocal(rinv[:, m % 8:m % 8 + 1],
                                                     rowsum[:, m % 8:m % 8 + 1]).then_inc(rinv_ready, 1)
                            if n >= 2:
                                m = n - 2
                                h, i = step(m)
                                dve.wait_ge(rinv_ready, START + b * ND + m + 1)
                                dve.wait_ge(V_ready, START + b * (NT * 4) + (h // 4) * NT + i + 1)
                                nc.vector.tensor_scalar(Vs[:, m % 8, :], Vraw[:, h // 4 % 2, i, h % 4, :],
                                                        rinv[:, m % 8:m % 8 + 1], None,
                                                        ALU.mult).then_inc(Vs_ready, 1)
                            if not is_row(b, 0):
                                if n == ROUTE_STATS:
                                    route_stats(b - 1, 1 - u)
                                if n == ROUTE_NORM:
                                    route.dve_normalise(dve, b - 1, 1 - u)
                                if n in ROUTE_DVE:
                                    ROUTE_DVE[n](dve, b - 1, 1 - u)
                            if n == STATS_AT and not is_row(b, B - 1):
                                ahead.dve_stats(dve, b + 1, 1 - u)
                            if n == NORM_AT and not is_row(b, B - 1):
                                dve.wait_ge(row_done, START + b)
                                ahead.dve_normalise(dve, b + 1, 1 - u)
                        dve.wait_ge(row_done, START + b + 1)
                        tiles = x_sb[:, bass.ds(b * NT, NT), :]
                        nc.vector.tensor_tensor(tiles, tiles,
                                                bankO[:, :].rearrange("p (t e) -> p t e", e=D),
                                                ALU.add).then_inc(x_done, 1)

                    each_row(dve, row)
                    route_stats(B - 1, 1)
                    route.dve_normalise(dve, B - 1, 1)
                    for step_of in ROUTE_DVE.values():
                        step_of(dve, B - 1, 1)

                @block.gpsimd
                def _(pool):
                    begin(pool, *ahead.of_pool, *route.of_pool)
                    ahead.pool_rstd(pool, 0, 0)
                    prime(pool, *route.scattered)

                    def row(b, u):
                        if not is_row(b, 0):
                            route.norm.pool_rstd(pool, b - 1, 1 - u)
                            route.pool_scatter(pool, b - 1, 1 - u)
                        if not is_row(b, B - 1):
                            ahead.pool_rstd(pool, b + 1, 1 - u)

                    each_row(pool, row)
                    route.norm.pool_rstd(pool, B - 1, 1)
                    route.pool_scatter(pool, B - 1, 1)
                    for u in range(2):
                        pool.wait_ge(route.scattered[u], PRIMED + B // 2 * 16 * TOP * NT)

        def expert_stage(name):
            with stage() as st:
                counts = sb(name + "_counts", [P, E], at=st)
                over = sb(name + "_over", [P, E, MAX_BLOCKS], at=st)
                nblocks = sb(name + "_nblocks", [P, E], at=st)
                fillf = sb(name + "_fillf", [P, E], at=st)
                counted, plan_step = sem(name + "_counted", st), sem(name + "_plan_step", st)
                plan_ready = sem(name + "_plan_ready", st)
                filled = sem(name + "_filled", st)

                with nc.Block() as block:
                    @block.tensor
                    def _(pe):
                        nc.tensor.matmul(bank[0][:, 0:E], ones_bf[:, :], run_bf[:, :], start=True,
                                         stop=True).then_inc(counted, 1)

                    @block.vector
                    def _(dve):
                        dve.wait_ge(counted, 1)
                        nc.vector.tensor_copy(counts[:, :], bank[0][:, 0:E]).then_inc(plan_step, 1)
                        dve.wait_ge(plan_step, 1)
                        nc.vector.tensor_tensor(fillf[:, :], counts[:, :], region_at[:, :],
                                                ALU.add).then_inc(plan_step, 1)
                        nc.vector.tensor_tensor(over[:, :, :],
                                                counts[:, :].unsqueeze(2).to_broadcast([P, E, MAX_BLOCKS]),
                                                full_blocks[:, :].unsqueeze(1).to_broadcast([P, E, MAX_BLOCKS]),
                                                ALU.is_gt).then_inc(plan_step, 1)
                        dve.wait_ge(plan_step, 3)
                        nc.vector.tensor_copy(fill_at[:, :], fillf[:, :]).then_inc(plan_ready, 1)
                        nc.vector.tensor_reduce(nblocks[:, :], over[:, :, :], AX.X, ALU.add).then_inc(plan_step, 1)
                        dve.wait_ge(plan_step, 4)
                        nc.vector.tensor_scalar(blocks[:, :], nblocks[:, :], 1.0, None,
                                                ALU.max).then_inc(plan_ready, 1)

                    @block.sync
                    def _(sp):
                        dve_done = 2
                        sp.wait_ge(plan_ready, dve_done)
                        for e in range(E):
                            first = sp.value_load(fill_at[0:1, e:e + 1], min_val=e * REGION,
                                                  max_val=e * REGION + B * T)
                            sp.dma_start(xg[bass.ds(first, BLK), :].rearrange("(t p) d -> p t d", p=P),
                                         fill[:, :, :]).then_inc(filled, 16)
                        sp.wait_ge(filled, 16 * E)

            with stage() as st:
                xb = sb(name + "_xb", [P, BT, W], at=st)
                second = sb(name + "_second", [P, BT], at=st)
                first = sb(name + "_first", [P, BT], at=st)
                next_token = sb(name + "_next_token", [P, BT], at=st)
                this_to = sb(name + "_this_to", [P, BT], at=st)
                to = sb(name + "_to", [P, BT], i32, at=st)
                xbT = sb(name + "_xbT", [P, BLK], at=st)
                hid = sb(name + "_hid", [P, FC, BLK], at=st)
                yb = sb(name + "_yb", [P, BT, D], at=st)
                bankX, bankH, bankY = bank[0], bank[1:1 + FC], bank[1 + FC]
                loaded = sem(name + "_block_loaded", st)
                transposed = sem(name + "_block_transposed", st)
                xbT_ready = sem(name + "_xbT_ready", st)
                up_done = [sem(f"{name}_up_done{c}", st) for c in range(FC)]
                hid_ready = [sem(f"{name}_hid_ready{c}", st) for c in range(FC)]
                down_done = sem(name + "_down_done", st)
                y_ready = [sem(f"{name}_y_ready{t}", st) for t in range(BT)]
                first_ready = sem(name + "_first_ready", st)
                next_token_ready, this_to_ready = sem(name + "_next_token_ready", st), sem(name + "_this_to_ready", st)
                second_known = sem(name + "_second_known", st)
                to_ready = [sem(f"{name}_to_ready{t}", st) for t in range(BT)]
                stored = [sem(f"{name}_tile_stored{t}", st) for t in range(BT)]
                may_store = sem(name + "_may_store", st)

                def each_block(eng, body):
                    count = eng.alloc_register(name + "_block")
                    dmas = eng.alloc_register(name + "_block_dmas")
                    eng.reg_mov(count, START)
                    eng.reg_mov(dmas, START)
                    n = [eng.value_load(blocks[0:1, e:e + 1], min_val=1, max_val=MAX_BLOCKS) for e in range(E)]
                    for e in range(E):
                        with eng.Fori(0, n[e]) as i:
                            k, k16 = eng.snap(count), eng.snap(dmas)
                            body(e, i * BLK + e * REGION, k, k16)
                            eng.reg_add(count, count, 1)
                            eng.reg_add(dmas, dmas, 16)
                    return eng.snap(count), eng.snap(dmas)

                with nc.Block() as block:
                    @block.sync
                    def _(sp):
                        begin(sp, loaded)

                        def load(row, k):
                            sp.wait_ge(transposed, k)
                            sp.wait_ge(next_token_ready, k)
                            sp.dma_start(xb[:, :, :], xg[bass.ds(row, BLK), :].rearrange("(t p) d -> p t d", p=P)
                                         ).then_inc(loaded, 16)

                        end, _ = each_block(sp, lambda e, row, k, k16: load(row, k))
                        load(0, end)

                    @block.tensor
                    def _(pe):
                        begin(pe, transposed, *up_done, down_done)

                        def transpose(k, k16):
                            pe.wait_ge(loaded, k16 + 16)
                            pe.wait_ge(xbT_ready, k)
                            for t in range(BT):
                                mm = nc.tensor.transpose(bankX[:, t * P:(t + 1) * P], xb[:, t, 0:D], ident[:, :])
                            mm.then_inc(transposed, 1)

                        def expert(e, row, k, k16):
                            pe.wait_ge(xbT_ready, k + 1)
                            for c in range(FC):
                                pe.wait_ge(hid_ready[c], k)
                                nc.tensor.matmul(bankH[c][:, 0:BLK], W1_sb[:, e, c * P:(c + 1) * P], xbT[:, :],
                                                 start=True, stop=True).then_inc(up_done[c], 1)
                            transpose(k + 1, k16 + 16)
                            pe.wait_ge(y_ready[BT - 1], k)
                            for t in range(BT):
                                for c in range(FC):
                                    if t == 0:
                                        pe.wait_ge(hid_ready[c], k + 1)
                                    mm = nc.tensor.matmul(bankY[:, t * D:(t + 1) * D], hid[:, c, t * P:(t + 1) * P],
                                                          W2_sb[:, e, c, :], start=(c == 0), stop=(c == FC - 1))
                            mm.then_inc(down_done, 1)

                        transpose(START, START)
                        each_block(pe, expert)

                    @block.gpsimd
                    def _(pool):
                        prime(pool, *stored)

                        def store(e, row, k, k16):
                            for t in range(BT):
                                pool.wait_ge(y_ready[t], k + 1)
                                pool.wait_ge(to_ready[t], k + 1)
                                pool.sem_inc(may_store, 1)
                                pool.indirect_dma_start(yg, bass.IndirectOffsetOnAxis(ap=to[:, t:t + 1], axis=0),
                                                        yb[:, t, :], None).then_inc(stored[t], 16)

                        _, end16 = each_block(pool, store)
                        for t in range(BT):
                            pool.wait_ge(stored[t], end16 + (PRIMED - START))
                            pool.sem_inc(may_store, 1)

                    @block.scalar
                    def _(act):
                        begin(act, *hid_ready)

                        def relu(e, row, k, k16):
                            act.wait_ge(down_done, k)
                            for c in range(FC):
                                act.wait_ge(up_done[c], k + 1)
                                nc.scalar.activation(hid[:, c, :], bankH[c][:, 0:BLK], ACT.Relu,
                                                     bias=b1_col[:, e * FC + c:e * FC + c + 1]
                                                     ).then_inc(hid_ready[c], 1)

                        each_block(act, relu)

                    @block.vector
                    def _(dve):
                        begin(dve, xbT_ready, first_ready, next_token_ready, this_to_ready, second_known, *to_ready, *y_ready)

                        def prepare(e, k, k16):
                            dve.wait_ge(transposed, k + 1)
                            nc.vector.tensor_scalar(xbT[:, :], bankX[:, 0:BLK], gamma_col, beta_col, ALU.mult,
                                                    ALU.add).then_inc(xbT_ready, 1)
                            dve.wait_ge(loaded, k16 + 16)
                            dve.wait_ge(this_to_ready, k)
                            nc.vector.tensor_copy(first[:, :], xb[:, :, D + 1]).then_inc(first_ready, 1)
                            nc.vector.tensor_copy(next_token[:, :], xb[:, :, D]).then_inc(next_token_ready, 1)

                        def finish(e, row, k, k16):
                            dve.wait_ge(first_ready, k + 1)
                            dve.wait_ge(next_token_ready, k + 1)
                            nc.vector.tensor_scalar(second[:, :], first[:, :], float(e), float(B * T), ALU.not_equal,
                                                    ALU.mult).then_inc(second_known, 1)
                            dve.wait_ge(second_known, k + 1)
                            for t in range(BT):
                                dve.wait_ge(to_ready[t], k)
                            nc.vector.tensor_tensor(this_to[:, :], second[:, :], next_token[:, :],
                                                    ALU.add).then_inc(this_to_ready, 1)
                            dve.wait_ge(up_done[FC - 1], k + 1)
                            prepare(e, k + 1, k16 + 16)
                            dve.wait_ge(down_done, k + 1)
                            dve.wait_ge(this_to_ready, k + 1)
                            for t in range(BT):
                                dve.wait_ge(stored[t], k16 + (PRIMED - START))
                                nc.vector.tensor_copy(to[:, t:t + 1], this_to[:, t:t + 1]).then_inc(to_ready[t], 1)
                                nc.vector.tensor_tensor(yb[:, t, :], bankY[:, t * D:(t + 1) * D], moe_const[:, e, :],
                                                        ALU.add).then_inc(y_ready[t], 1)

                        prepare(0, START, START)
                        each_block(dve, finish)

        class Combine:

            def __init__(self, name, at):
                self.rows = sb(name + "_crows", [P, 2, TOP, NT, D], at=at)
                self.loaded = [sem(f"{name}_rows_loaded{u}", at) for u in range(2)]
                self.added = sem(name + "_experts_added", at)
                self.all_added = sem(name + "_row_added", at)
                self.of_sp = self.loaded
                self.of_dve = (self.added,)

            def load(self, sp, b, u, of=None):
                sp.wait_ge(self.added, START + (b - 1) * TOP * NT)
                for k in range(TOP):
                    first = (b if of is None else of) * T + k * B * T
                    sp.dma_start(self.rows[:, u, k, :, :],
                                 yg[bass.ds(first, T), :].rearrange("(t p) d -> p t d", p=P)
                                 ).then_inc(self.loaded[u], 16)

            def dve_add(self, dve, b, u):
                dve.wait_ge(self.loaded[u], START + (b - u) * (8 * TOP) + 16 * TOP)
                for k in range(TOP):
                    if k > 0:
                        dve.wait_ge(self.added, START + b * TOP * NT + k * NT)
                    for t in range(NT):
                        tile = x_sb[:, bass.ds(b * NT + t, 1), :]
                        nc.vector.scalar_tensor_tensor(
                            out=tile, in0=self.rows[:, u, k, t:t + 1, :], scalar=gates[:, bass.ds(b * NT + t, 1), k],
                            in1=tile, op0=ALU.mult, op1=ALU.add).then_inc(self.added, 1)
                dve.wait_ge(self.added, START + (b + 1) * TOP * NT)
                dve.sem_inc(self.all_added, 1)

        def combine_stage():
            with stage() as st:
                combine = Combine("c", st)
                with nc.Block() as block:
                    @block.sync
                    def _(sp):
                        begin(sp, *combine.of_sp)
                        combine.load(sp, 0, 0)
                        combine.load(sp, 1, 1)
                        with sp.Fori(0, B // 2 - 1) as pair:
                            for u in range(2):
                                combine.load(sp, pair * 2 + 2 + u, u)

                    @block.vector
                    def _(dve):
                        begin(dve, *combine.of_dve)
                        with dve.Fori(0, B // 2) as pair:
                            for u in range(2):
                                combine.dve_add(dve, pair * 2 + u, u)

                    @block.scalar
                    def _(act):
                        with act.Fori(0, B) as b:
                            act.wait_ge(combine.added, START + (b + 1) * TOP * NT)
                            act.dma_start(out[bass.ds(b, 1)].rearrange("o (t p) e -> p (o t) e", p=P),
                                          x_sb[:, bass.ds(b * NT, NT), :]).then_inc(s_store, 16)
                        act.wait_ge(s_store, 16 * B)

        def linear_attention_stage():
            with stage() as st:
                ahead = Ahead("b", st, LN_LN, x_sb, attn_norm_col, None, want_htok=True)
                GR = 2
                NS = NT * GR
                V_sb = sb("V_sb", [P, NT, HB * DB], at=st)
                G_sb = sb("Gb_sb", [P, 2, HB, T], at=st)
                R_sb = sb("R_sb", [P, GR, 4 * DB], at=st)
                AT_sb = sb("AT_sb", [P, 2, 4, P], at=st)
                o_sb = sb("o_sb", [P, 2, 4, DB], at=st)
                oT_sb = sb("oT_sb", [P, 2, 4 * P], at=st)
                junk = sb("junk", [P, 2, 4, DB], at=st)
                ss = sb("ss", [P, 2, 4], at=st)
                ms = sb("ms", [P, 2, 4], at=st)
                ro = sb("ro", [P, 2, 4, 1], at=st)
                bankW, bankOo, bankRr, bankZ = bank[1:3], bank[3:5], bank[5:7], bank[7]

                xnT_ready = sem("b_xnT_ready", st)
                proj_done, proj_ready = sem("b_proj_done", st), sem("b_proj_ready", st)
                att_done, att_ready = sem("b_att_done", st), sem("b_att_ready", st)
                o_done = sem("b_o_done", st)
                squares = sem("b_squares", st)
                pool_root = sem("b_pool_root", st)
                root_ready = sem("b_root_ready", st)
                o_ready = sem("b_o_ready", st)
                oT_done, oT_ready = sem("b_oT_done", st), sem("b_oT_ready", st)
                R_done = [sem(f"b_R_done{g}", st) for g in range(GR)]
                R_ready = [sem(f"b_R_ready{g}", st) for g in range(GR)]
                row_done = sem("b_row_done", st)
                z_done = sem("b_z_done", st)

                early = [("v", 0, 0), ("v", 0, 1)] + [("G", h) for h in range(4)]
                after = {0: [("G", h) for h in range(4, 8)], 7: [("next", 0), ("next", 1)],
                         8: [("next", 2), ("next", 3)], 9: [("next", 4)], 10: [("next", 5)]}
                for i in range(1, NT):
                    after[2 * i - 1] = [("v", i, 0), ("v", i, 1)]
                uses = []
                for s in range(NS + 3):
                    uses += ([("att", s)] if s < NS else []) + after.get(s, [])
                late = [x for x in uses if x[0] in ("v", "G")]
                proj_index = {x: k for k, x in enumerate(early + late)}
                NPROJ = len(proj_index)
                assert len(uses) % 2 == 0 and len(early) % 2 == 0
                COMBINE_AT, RSTD_AT, NORM_AT, AHEAD_AT = 0, 1, 3, 4

                def projected(b, use):
                    if use[0] == "next":
                        return (b + 1) * NPROJ + use[1] + 1
                    return b * NPROJ + proj_index[use] + 1

                combine = Combine("b", st)

                with nc.Block() as block:
                    @block.tensor
                    def _(pe):
                        begin(pe, proj_done, att_done, o_done, oT_done, *R_done, row_done, ahead.tr)
                        ahead.pe_transpose(pe, 0, 0)

                        def claim(b, use):
                            k = uses.index(use)
                            last = uses[k - 2]
                            if last[0] == "att":
                                pe.wait_ge(att_ready, START + b * NS + last[1] + 1)
                            else:
                                pe.wait_ge(proj_ready, START + projected(b - 1 if k < 2 else b, last))
                            return bankW[k % 2]

                        def product(ps, u, use):
                            if use[0] == "v":
                                _, i, g = use
                                mm = nc.tensor.matmul(ps[:, :], ahead.xnT[:, u, i * P:(i + 1) * P],
                                                      Wv_sb[:, g * 512:(g + 1) * 512], start=True, stop=True)
                            else:
                                mm = nc.tensor.matmul(ps[:, :], A_sb[:, use[1], :], ahead.xnT[:, u, :], start=True,
                                                      stop=True)
                            mm.then_inc(proj_done, 1)

                        def project(b, u, use):
                            if use[0] == "next":
                                if use[1] == 0:
                                    pe.wait_ge(xnT_ready, START + b + 2)
                                product(claim(b, use), 1 - u, early[use[1]])
                            else:
                                product(claim(b, use), u, use)

                        def scores(b, u, s):
                            i, g = divmod(s, GR)
                            ps = claim(b, ("att", s))
                            pe.wait_ge(proj_ready, START + projected(b, ("G", 4 * g + 3)))
                            nc.tensor.matmul(ps[:, :].rearrange("p (h i) -> p h i", i=P),
                                             ahead.xnT[:, u, i * P:(i + 1) * P],
                                             G_sb[:, u, 4 * g:4 * g + 4, i * P:(i + 1) * P],
                                             start=True, stop=True).then_inc(att_done, 1)

                        def outputs(b, u, s):
                            i, g = divmod(s, GR)
                            pe.wait_ge(o_ready, START + b * NS + s - 1)
                            pe.wait_ge(att_ready, START + b * NS + s + 1)
                            pe.wait_ge(proj_ready, START + projected(b, ("v", i, g)))
                            if i > 0:
                                pe.wait_ge(R_ready[g], START + b * (NT - 1) + i)
                            for m in range(4):
                                h = 4 * g + m
                                o = bankOo[s % 2][:, m * DB:(m + 1) * DB]
                                mm = nc.tensor.matmul(o, AT_sb[:, s % 2, m, :], V_sb[:, i, h * DB:(h + 1) * DB],
                                                      start=True, stop=(i == 0))
                                if i > 0:
                                    mm = nc.tensor.matmul(o, G_sb[:, u, h, i * P:(i + 1) * P],
                                                          R_sb[:, g, m * DB:(m + 1) * DB], start=False, stop=True)
                            mm.then_inc(o_done, 1)

                        def state(b, u, s):
                            i, g = divmod(s, GR)
                            if i == NT - 1:
                                return
                            if s == 0:
                                pe.wait_ge(ahead.htok, START + b + 1)
                            pe.wait_ge(R_ready[g], START + b * (NT - 1) + i)
                            nc.tensor.matmul(bankRr[g][:, :], ahead.htok_sb[:, u, i, :], V_sb[:, i, g * 512:(g + 1) * 512],
                                             start=(i == 0), stop=(i == NT - 2),
                                             skip_group_check=True).then_inc(R_done[g], 1)

                        def transposes(b, u, s):
                            pe.wait_ge(o_ready, START + b * NS + s + 1)
                            pe.wait_ge(oT_ready, START + b * NS + s)
                            if s == AHEAD_AT - 1:
                                pe.wait_ge(xnT_ready, START + b + 2)
                            for m in range(4):
                                mm = nc.tensor.transpose(bank[0][:, m * P:(m + 1) * P], o_sb[:, s % 2, m, :],
                                                         ident[:, :])
                            mm.then_inc(oT_done, 1)

                        def project_out(b, u, s):
                            i, g = divmod(s, GR)
                            if s == 0:
                                pe.wait_ge(z_done, START + b)
                            pe.wait_ge(oT_ready, START + b * NS + s + 1)
                            for m in range(4):
                                mm = nc.tensor.matmul(bankZ[:, i * D:(i + 1) * D], oT_sb[:, s % 2, m * P:(m + 1) * P],
                                                      Wo_sb[:, 4 * g + m, :], start=(g == 0 and m == 0),
                                                      stop=(g == GR - 1 and m == 3))
                            if s == NS - 1:
                                mm.then_inc(row_done, 1)

                        pe.wait_ge(xnT_ready, START + 1)
                        for k, use in enumerate(early):
                            if k >= 2:
                                pe.wait_ge(proj_ready, START + k - 1)
                            product(bankW[k % 2], 0, use)
                        with pe.Fori(0, B // 2) as pair:
                            for u in range(2):
                                b = pair * 2 + u
                                for s in range(NS + 3):
                                    if s < NS:
                                        scores(b, u, s)
                                    for use in after.get(s, []):
                                        project(b, u, use)
                                    if 1 <= s <= NS:
                                        outputs(b, u, s - 1)
                                        state(b, u, s - 1)
                                    if 2 <= s <= NS + 1:
                                        transposes(b, u, s - 2)
                                    if s == AHEAD_AT:
                                        pe.wait_ge(oT_ready, START + b * NS + AHEAD_AT - 1)
                                        ahead.pe_transpose(pe, b + 1, 1 - u)
                                    if s >= 3:
                                        project_out(b, u, s - 3)

                    @block.scalar
                    def _(act):
                        begin(act, xnT_ready, proj_ready, squares, oT_ready, *R_ready)
                        ahead.act_evacuate(act, 0, 0, xnT_ready)

                        def copy_product(ps, u, use):
                            if use[0] == "v":
                                _, i, g = use
                                dst = V_sb[:, i, g * 512:(g + 1) * 512]
                            else:
                                dst = G_sb[:, u, use[1], :]
                            nc.scalar.activation(dst, ps[:, :], ACT.Copy).then_inc(proj_ready, 1)

                        def copy_out(b, u, use):
                            act.wait_ge(proj_done, START + projected(b, use))
                            ps = bankW[uses.index(use) % 2]
                            if use[0] == "next":
                                copy_product(ps, 1 - u, early[use[1]])
                            else:
                                copy_product(ps, u, use)

                        for k, use in enumerate(early):
                            act.wait_ge(proj_done, START + k + 1)
                            copy_product(bankW[k % 2], 0, use)
                        with act.Fori(0, B // 2) as pair:
                            for u in range(2):
                                b = pair * 2 + u
                                for s in range(NS + 3):
                                    for use in after.get(s, []):
                                        copy_out(b, u, use)
                                    if 1 <= s <= NS:
                                        r = s - 1
                                        i, g = divmod(r, GR)
                                        act.wait_ge(o_done, START + b * NS + r + 1)
                                        for m in range(4):
                                            ins = nc.scalar.activation(junk[:, r % 2, m, :],
                                                                       bankOo[r % 2][:, m * DB:(m + 1) * DB],
                                                                       ACT.Square, accum_out=ss[:, r % 2, m:m + 1])
                                        ins.then_inc(squares, 1)
                                        if i < NT - 1:
                                            act.wait_ge(R_done[g], START + b * (NT - 1) + i + 1)
                                            nc.scalar.activation(R_sb[:, g, :], bankRr[g][:, :],
                                                                 ACT.Copy).then_inc(R_ready[g], 1)
                                    if 2 <= s <= NS + 1:
                                        r = s - 2
                                        act.wait_ge(oT_done, START + b * NS + r + 1)
                                        nc.scalar.activation(oT_sb[:, r % 2, :], bank[0][:, :],
                                                             ACT.Copy).then_inc(oT_ready, 1)
                                    if s == AHEAD_AT:
                                        ahead.act_evacuate(act, b + 1, 1 - u, xnT_ready)

                    @block.sync
                    def _(sp):
                        begin(sp, *combine.of_sp)
                        combine.load(sp, 0, 0)
                        combine.load(sp, 1, 1)
                        with sp.Fori(0, B // 2 - 1) as pair:
                            for u in range(2):
                                combine.load(sp, pair * 2 + 2 + u, u)
                        combine.load(sp, B, 0, of=0)

                    @block.gpsimd
                    def _(pool):
                        begin(pool, pool_root, root_ready, *ahead.of_pool)
                        ahead.pool_rstd(pool, 0, 0)
                        ahead.pool_finish(pool, 0, 0)
                        with pool.Fori(0, B // 2) as pair:
                            for u in range(2):
                                b = pair * 2 + u
                                for s in range(NS):
                                    n = b * NS + s
                                    pool.wait_ge(squares, START + n + 1)
                                    nc.gpsimd.tensor_tensor(ms[:, s % 2, :], ss[:, s % 2, :], per_dim[:, :],
                                                            ALU.mult).then_inc(pool_root, 1)
                                    pool.wait_ge(pool_root, START + 2 * n + 1)
                                    nc.gpsimd.tensor_tensor(ms[:, s % 2, :], ms[:, s % 2, :], eps[:, :],
                                                            ALU.add).then_inc(pool_root, 1)
                                    pool.wait_ge(pool_root, START + 2 * n + 2)
                                    nc.gpsimd.tensor_tensor(ro[:, s % 2, :, 0], ms[:, s % 2, :], half[:, :],
                                                            ALU.pow).then_inc(root_ready, 1)
                                    if s == RSTD_AT:
                                        ahead.pool_rstd(pool, b + 1, 1 - u)
                                    if s == NORM_AT:
                                        ahead.pool_finish(pool, b + 1, 1 - u)

                    @block.vector
                    def _(dve):
                        begin(dve, att_ready, o_ready, z_done, *combine.of_dve, *ahead.of_dve)
                        combine.dve_add(dve, 0, 0)
                        ahead.dve_stats(dve, 0, 0)
                        ahead.dve_normalise(dve, 0, 0)
                        with dve.Fori(0, B // 2) as pair:
                            for u in range(2):
                                b = pair * 2 + u
                                for s in range(NS + 1):
                                    if s < NS:
                                        k = uses.index(("att", s))
                                        dve.wait_ge(att_done, START + b * NS + s + 1)
                                        nc.vector.tensor_tensor(
                                            AT_sb[:, s % 2, :, :],
                                            bankW[k % 2][:, :].rearrange("p (h i) -> p h i", i=P),
                                            keep[:, :].unsqueeze(1).to_broadcast([P, 4, P]),
                                            ALU.mult).then_inc(att_ready, 1)
                                    if s == COMBINE_AT:
                                        combine.dve_add(dve, b + 1, 1 - u)
                                        ahead.dve_stats(dve, b + 1, 1 - u)
                                    if s == NORM_AT:
                                        dve.wait_ge(row_done, START + b)
                                        ahead.dve_normalise(dve, b + 1, 1 - u)
                                    if s >= 1:
                                        r = s - 1
                                        dve.wait_ge(root_ready, START + b * NS + r + 1)
                                        nc.vector.tensor_tensor(
                                            o_sb[:, r % 2, :, :],
                                            bankOo[r % 2][:, :].rearrange("p (h v) -> p h v", v=DB),
                                            ro[:, r % 2, :, :].to_broadcast([P, 4, DB]),
                                            ALU.mult).then_inc(o_ready, 1)
                                dve.wait_ge(row_done, START + b + 1)
                                nc.vector.tensor_tensor(z_sb[:, bass.ds(b * NT, NT), :], ahead.y_sb[:, u, :, :],
                                                        bankZ[:, :].rearrange("p (t e) -> p t e", e=D),
                                                        ALU.add).then_inc(z_done, 1)

        def mlp_stage():
            with stage() as st:
                ahead = Ahead("m", st, RMS, z_sb, mlp_norm_col, None, want_sum=True)
                C = INTER // P
                silu = sb("silu", [P, 2, T], at=st)
                act_h = sb("act_h", [P, 2, C, T], at=st)
                warm = sb("m_warm", [P, NT], at=st)
                bankG, bankU, bankD = bank[1:3], bank[3:5], bank[5:7]
                route = Route("f2", st, bank[7])
                xnT_ready = sem("m_xnT_ready", st)
                gate_done, up_done = sem("m_gate_done", st), sem("m_up_done", st)
                silu_ready, act_ready = sem("m_silu_ready", st), sem("m_act_ready", st)
                row_done = sem("m_row_done", st)
                x_done = sem("m_x_done", st)
                x_complete = sem("m_x_complete", st)

                def each_row_of_m(eng, row):
                    row(0, 0)
                    row(1, 1)
                    with eng.Fori(0, B // 2 - 1) as pair:
                        row(pair * 2 + 2, 0)
                        row(pair * 2 + 3, 1)

                with nc.Block() as block:
                    @block.tensor
                    def _(pe):
                        begin(pe, gate_done, up_done, row_done, ahead.tr, *route.of_pe)
                        ahead.pe_transpose(pe, 0, 0)

                        def row(b, u):
                            route_too = not is_row(b, 0)
                            pe.wait_ge(xnT_ready, START + b + 1)
                            for c in range(C):
                                n = b * C + c
                                pe.wait_ge(silu_ready, START + n - 1)
                                nc.tensor.matmul(bankG[c % 2][:, :], Wgate_sb[:, c * P:(c + 1) * P],
                                                 ahead.xnT[:, u, :], start=True, stop=True).then_inc(gate_done, 1)
                                pe.wait_ge(act_ready, START + n - 1)
                                nc.tensor.matmul(bankU[c % 2][:, :], Wup_sb[:, c * P:(c + 1) * P],
                                                 ahead.xnT[:, u, :], start=True, stop=True).then_inc(up_done, 1)
                                if c == 1 and route_too:
                                    route.norm.pe_transpose(pe, b - 1, 1 - u)
                                if c == 2 and route_too:
                                    route.pe_logits(pe, b - 1, 1 - u)
                            ahead.pe_transpose(pe, b + 1, 1 - u)
                            pe.wait_ge(act_ready, START + (b + 1) * C)
                            pe.wait_ge(x_done, START + b)
                            for t in range(NT):
                                for c in range(C):
                                    mm = nc.tensor.matmul(bankD[u][:, t * D:(t + 1) * D],
                                                          act_h[:, u, c, t * P:(t + 1) * P], Wdown_sb[:, c, :],
                                                          start=(c == 0), stop=(c == C - 1))
                            mm.then_inc(row_done, 1)
                            if route_too:
                                route.pe_rank(pe, b - 1, 1 - u)

                        each_row_of_m(pe, row)
                        route.norm.pe_transpose(pe, B - 1, 1)
                        route.pe_logits(pe, B - 1, 1)
                        route.pe_rank(pe, B - 1, 1)

                    @block.scalar
                    def _(act):
                        begin(act, xnT_ready, silu_ready, *route.of_act)
                        nc.scalar.activation(warm[:, :], half[:, :], ACT.Silu)
                        ahead.act_evacuate(act, 0, 0, xnT_ready)

                        def row(b, u):
                            for c in range(C):
                                n = b * C + c
                                act.wait_ge(gate_done, START + n + 1)
                                act.wait_ge(act_ready, START + n - 1)
                                nc.scalar.activation(silu[:, c % 2, :], bankG[c % 2][:, :],
                                                     ACT.Silu).then_inc(silu_ready, 1)
                                if c == 2 and not is_row(b, 0):
                                    route.norm.act_evacuate(act, b - 1, 1 - u, route.xnT_ready)
                            ahead.act_evacuate(act, b + 1, 1 - u, xnT_ready)
                            if not is_row(b, 0):
                                route.act_exp(act, b - 1, 1 - u)

                        each_row_of_m(act, row)
                        route.norm.act_evacuate(act, B - 1, 1, route.xnT_ready)
                        route.act_exp(act, B - 1, 1)

                    @block.vector
                    def _(dve):
                        begin(dve, act_ready, x_done, *ahead.of_dve, *route.of_dve)
                        route.dve_begin(dve)
                        ahead.dve_stats(dve, 0, 0)
                        ahead.dve_normalise(dve, 0, 0)

                        def route_stats(b, u):
                            dve.wait_ge(x_done, START + b + 1)
                            dve.sem_inc(x_complete, 1)
                            route.norm.dve_stats(dve, b, u)

                        def route_select(b, u):
                            for part in (route.dve_top, route.dve_topid, route.dve_ids, route.dve_is_k, route.dve_sel,
                                         route.dve_row_sel):
                                part(dve, b, u)

                        def route_place(b, u):
                            for part in (route.dve_place, route.dve_picked, route.dve_slotf, route.dve_slots):
                                part(dve, b, u)

                        def row(b, u):
                            route_too = not is_row(b, 0)
                            if route_too:
                                route_stats(b - 1, 1 - u)
                            for c in range(C):
                                n = b * C + c
                                dve.wait_ge(silu_ready, START + n + 1)
                                dve.wait_ge(up_done, START + n + 1)
                                nc.vector.tensor_tensor(act_h[:, u, c, :], bankU[c % 2][:, :],
                                                        silu[:, c % 2, :], ALU.mult).then_inc(act_ready, 1)
                                if c == 0:
                                    if route_too:
                                        route.dve_normalise(dve, b - 1, 1 - u)
                                    ahead.dve_stats(dve, b + 1, 1 - u)
                                if c == 1:
                                    dve.wait_ge(row_done, START + b)
                                    ahead.dve_normalise(dve, b + 1, 1 - u)
                            if route_too:
                                route.dve_logit(dve, b - 1, 1 - u)
                                route.dve_rmax(dve, b - 1, 1 - u)
                                route.dve_shift(dve, b - 1, 1 - u)
                                route_select(b - 1, 1 - u)
                            dve.wait_ge(row_done, START + b + 1)
                            dve.wait_ge(ahead.sum, START + b + 1)
                            nc.vector.tensor_tensor(x_sb[:, bass.ds(b * NT, NT), :], ahead.sum_sb[:, u, :, :],
                                                    bankD[u][:, :].rearrange("p (t e) -> p t e", e=D),
                                                    ALU.add).then_inc(x_done, 1)
                            if route_too:
                                route_place(b - 1, 1 - u)

                        each_row_of_m(dve, row)
                        route_stats(B - 1, 1)
                        route.dve_normalise(dve, B - 1, 1)
                        route.dve_logit(dve, B - 1, 1)
                        route.dve_rmax(dve, B - 1, 1)
                        route.dve_shift(dve, B - 1, 1)
                        route_select(B - 1, 1)
                        route_place(B - 1, 1)

                    @block.gpsimd
                    def _(pool):
                        begin(pool, *ahead.of_pool, *route.of_pool)
                        ahead.pool_rstd(pool, 0, 0)
                        ahead.pool_finish(pool, 0, 0)
                        prime(pool, *route.scattered)

                        def row(b, u):
                            early = is_row(b, 0) or is_row(b, 1)
                            if not is_row(b, 0):
                                route.norm.pool_rstd(pool, b - 1, 1 - u)
                            if not early:
                                route.pool_scatter(pool, b - 2, u, range(NT // 2))
                            ahead.pool_rstd(pool, b + 1, 1 - u)
                            ahead.pool_finish(pool, b + 1, 1 - u)
                            if not early:
                                route.pool_scatter(pool, b - 2, u, range(NT // 2, NT))

                        each_row_of_m(pool, row)
                        route.norm.pool_rstd(pool, B - 1, 1)
                        route.pool_scatter(pool, B - 2, 0)
                        route.pool_scatter(pool, B - 1, 1)
                        for u in range(2):
                            pool.wait_ge(route.scattered[u], PRIMED + B // 2 * 16 * TOP * NT)

        expert_stage("f1x")
        linear_attention_stage()
        mlp_stage()
        expert_stage("f2x")
        combine_stage()


_INS = ["L0_attn_a_x", "L0_attn_a_W_K", "L0_attn_a_W_Q", "L0_attn_a_W_V", "L0_attn_a_W_O",
        "L0_attn_b_attn_norm_w", "L0_attn_b_Wq", "L0_attn_b_Wk", "L0_attn_b_Wv", "L0_attn_b_Wo",
        "L0_attn_b_attn_out_norm_w", "L0_attn_b_mlp_norm_w", "L0_attn_b_Wgate", "L0_attn_b_Wup",
        "L0_attn_b_Wdown", "L0_ffn_gamma", "L0_ffn_beta", "L0_ffn_Wr", "L0_ffn_br", "L0_ffn_W1",
        "L0_ffn_b1", "L0_ffn_W2", "L0_ffn_b2"]


def kernel(**inputs):
    import numpy as _np
    import concourse.bacc as _bacc
    from concourse import mybir as _mybir
    from concourse.bass_utils import run_bass_kernel_spmd as _run

    nc = _bacc.Bacc("TRN2", target_bir_lowering=False, num_devices=1)
    arrays, args = {}, []
    for name in _INS:
        a = _np.ascontiguousarray(inputs[name])
        arrays[f"in_{name}_dram"] = a
        args.append(nc.dram_tensor(f"in_{name}_dram", a.shape, _mybir.dt.from_np(a.dtype), kind="ExternalInput").ap())
    args.append(nc.dram_tensor("out_dram", (B, T, D), f32, kind="ExternalOutput").ap())
    build_hybrid(nc, *args)
    r = _run(nc, [arrays], core_ids=[0])
    return r.results[0]["out_dram"]
```

```python
import concourse.bass as bass
from concourse import mybir
from contextlib import ExitStack, contextmanager

f32 = mybir.dt.float32
bf16 = mybir.dt.bfloat16
f32r = mybir.dt.float32r
u32 = mybir.dt.uint32
i32 = mybir.dt.int32
ALU = mybir.AluOpType
ACT = mybir.ActivationFunctionType
AX = mybir.AxisListType

P = 128
B, T, D = 8, 512, 128
NT = T // P
EPS = 1e-5
START = 8
MASKED = -1e10
HUGE = 3e38

HA, DHA = 16, 64
ND = HA * NT
HB, DB = 8, 128
INTER = 512
E, F = 8, 512
FC = F // P
TOP = 2
BLK = 256
BT = BLK // P
MAX_BLOCKS = B * T // BLK
W = D + 2
REGION = B * T + BLK


def build_hybrid(nc, x, W_K, W_Q, W_V, W_O, attn_norm_w, Wq, Wk, Wv, Wo, out_norm_w, mlp_norm_w,
                 Wgate, Wup, Wdown, gamma, beta, Wr, br, W1, b1, W2, b2, out):
    root = ExitStack()
    with root:
        def sb(name, shape, dt=f32, at=root):
            return at.enter_context(nc.sbuf_tensor(name, shape, dt))

        def sem(name, at=root):
            if at is root:
                return at.enter_context(nc.semaphore(name))
            handle = nc.alloc_semaphore(name=name)
            at.semaphores.append(handle)
            return handle

        @contextmanager
        def stage():
            with ExitStack() as st:
                st.semaphores = []
                yield st
                nc.clear_and_free_semaphores(st.semaphores)
                nc.all_engine_barrier()

        bank = [root.enter_context(nc.psum_tensor(f"bank{k}", [P, 512], f32)) for k in range(8)]

        x_sb = sb("x_sb", [P, (B + 1) * NT, D])
        z_sb = sb("z_sb", [P, (B + 1) * NT, D])
        A_hi, A_lo = sb("A_hi", [P, HB, D], f32r), sb("A_lo", [P, HB, D], f32r)
        Wv_hi, Wv_lo = sb("Wv_hi", [P, HB * DB], f32r), sb("Wv_lo", [P, HB * DB], f32r)
        Wo_sb = sb("Wo_sb", [P, HB, D])
        Wgate_sb = sb("Wgate_sb", [P, INTER])
        Wup_sb = sb("Wup_sb", [P, INTER])
        Wdown_sb = sb("Wdown_sb", [P, INTER // P, D])
        W1_sb = sb("W1_sb", [P, E, F])
        W2_sb = sb("W2_sb", [P, E, FC, D])
        Wr_sb = sb("Wr_sb", [P, E])
        br_sb = sb("br_sb", [P, E])
        wn_sb = sb("wn_sb", [P, D])
        cols = sb("cols", [P, E * FC + 5])
        b1_col = cols[:, 0:E * FC]
        gamma_col, beta_col, attn_norm_col, out_norm_col, mlp_norm_col = (
            cols[:, E * FC + k:E * FC + k + 1] for k in range(5))
        moe_const = sb("moe_const", [P, E, D])
        spare = sb("spare", [1, 16])
        gates = sb("gates", [P, (B + 1) * NT, TOP])
        token = sb("token", [P, (B + 1) * NT])
        fill = sb("fill", [P, BT, W])
        blocks = sb("blocks", [P, E], i32)
        fill_at = sb("fill_at", [P, E], i32)
        region_at = sb("region_at", [P, E])
        full_blocks = sb("full_blocks", [P, MAX_BLOCKS])
        run_bf = sb("run_bf", [P, E], bf16)
        ones_bf = sb("ones_bf", [P, P], bf16)
        before_bf = sb("before_bf", [P, P], bf16)
        ident = sb("ident", [P, P])
        mask = sb("mask", [P, T])
        keep = sb("keep", [P, P])
        expert_id = sb("expert_id", [P, E])
        half = sb("half", [P, NT])
        eps = sb("eps", [P, NT])
        per_dim = sb("per_dim", [P, NT])
        unit = sb("unit", [P, NT])
        ones = sb("ones", [E, P])
        xg = nc.dram_tensor("expert_in", (E * REGION, W), f32, kind="Internal").ap()
        yg = nc.dram_tensor("expert_out", (TOP * B * T + BLK, D), f32, kind="Internal").ap()

        s_xload = sem("s_xload")
        Wq_sb, Wk_sb = z_sb[:, 0:HB, :], z_sb[:, HB:2 * HB, :]
        Wv_sb = z_sb[:, 3 * HB:4 * HB, :].rearrange("p h v -> p (h v)")
        b2_sb = sb("b2_sb", [E, D])
        s_store = sem("s_store")
        s_lin = sem("s_lin")
        s_big = sem("s_big")

        head_weights = root.enter_context(ExitStack())
        M_hi, M_lo = (sb("M_" + part, [P, HA, D], f32r, at=head_weights) for part in ("hi", "lo"))
        U_hi, U_lo = (sb("U_" + part, [P, HA, D], f32r, at=head_weights) for part in ("hi", "lo"))

        with stage() as st:
            WK_sb = sb("WK_sb", [P, HA // 2, D], at=st)
            WQ_sb = sb("WQ_sb", [P, HA // 2, D], at=st)
            WV_sb = sb("WV_sb", [P, HA // 2, D], at=st)
            WO_sb = sb("WO_sb", [P, HA * DHA], at=st)
            WOT_sb = sb("WOT_sb", [P, HA // 2, D], at=st)
            rows = sb("rows", [E * FC + 5, P], at=st)
            zero = sb("zero", [P, P], at=st)
            zero_bf = sb("zero_bf", [P, P], bf16, at=st)

            s_heads = sem("s_heads")
            s_small = sem("s_small")
            s_fill = sem("s_fill")
            s_const = sem("s_const")
            s_prod = sem("s_prod")
            s_evac = sem("s_evac")
            s_low = sem("s_low")
            s_rows = sem("s_rows")
            s_cols = sem("s_cols")

            CONSTS = 21

            with nc.Block() as block:
                @block.sync
                def _(sp):
                    for w_sb, w in ((WK_sb, W_K), (WQ_sb, W_Q), (WV_sb, W_V)):
                        sp.dma_start(w_sb[:, :, :], w.rearrange("(t a) d e -> (a d) t e", a=2)).then_inc(s_heads, 16)
                    sp.dma_start(WO_sb[:, :], W_O).then_inc(s_heads, 16)
                    for b in range(B):
                        sp.dma_start(x_sb[:, b * NT:(b + 1) * NT, :],
                                     x[b].rearrange("(t p) e -> p t e", p=P)).then_inc(s_xload, 16)
                    sp.dma_start(W1_sb[:, :, :], W1.rearrange("e h f -> h e f")).then_inc(s_big, 16)
                    sp.dma_start(W2_sb[:, :, :, :], W2.rearrange("e (c f) h -> f e c h", f=P)).then_inc(s_big, 16)
                    sp.dma_start(Wv_sb, Wv).then_inc(s_big, 16)
                    sp.dma_start(Wgate_sb[:, :], Wgate).then_inc(s_big, 16)
                    sp.dma_start(Wup_sb[:, :], Wup).then_inc(s_big, 16)
                    sp.dma_start(Wdown_sb[:, :, :], Wdown.rearrange("(c f) d -> f c d", f=P)).then_inc(s_big, 16)
                    sp.dma_start(Wq_sb, Wq.rearrange("d (h k) -> d h k", k=DB)).then_inc(s_lin, 16)
                    sp.dma_start(Wk_sb, Wk.rearrange("d (h k) -> d h k", k=DB)).then_inc(s_lin, 16)
                    sp.dma_start(Wo_sb[:, :, :], Wo.rearrange("(h v) d -> v h d", v=DB)).then_inc(s_lin, 16)

                @block.gpsimd
                def _(pool):
                    nc.gpsimd.memset(zero[:, :], 0.0).then_inc(s_fill, 1)
                    nc.gpsimd.memset(zero_bf[:, :], 0.0).then_inc(s_fill, 1)
                    pool.wait_ge(s_fill, 2)
                    nc.gpsimd.affine_select(out=ident[:, :], in_=zero[:, :], compare_op=ALU.not_equal, fill=1.0,
                                            base=0, pattern=[[-1, P]], channel_multiplier=1).then_inc(s_const, 1)
                    nc.gpsimd.memset(mask[:, 0:T - P], 0.0).then_inc(s_const, 1)
                    nc.gpsimd.affine_select(out=mask[:, T - P:], in_=zero[:, :], compare_op=ALU.is_ge, fill=MASKED,
                                            base=0, pattern=[[-1, P]], channel_multiplier=1).then_inc(s_const, 1)
                    nc.gpsimd.affine_select(out=before_bf[:, :], in_=zero_bf[:, :], compare_op=ALU.is_ge, fill=1.0,
                                            base=0, pattern=[[-1, P]], channel_multiplier=1).then_inc(s_const, 1)
                    nc.gpsimd.affine_select(out=keep[:, :], in_=zero[:, :], compare_op=ALU.is_gt, fill=1.0,
                                            base=0, pattern=[[-1, P]], channel_multiplier=1).then_inc(s_const, 1)
                    nc.gpsimd.memset(half[:, :], -0.5).then_inc(s_const, 1)
                    nc.gpsimd.memset(eps[:, :], EPS).then_inc(s_const, 1)
                    nc.gpsimd.memset(per_dim[:, :], 1.0 / DB).then_inc(s_const, 1)
                    nc.gpsimd.memset(ones[:, :], 1.0).then_inc(s_const, 1)
                    nc.gpsimd.memset(unit[:, :], 1.0).then_inc(s_const, 1)
                    nc.gpsimd.memset(x_sb[:, B * NT:, :], 0.0).then_inc(s_const, 1)
                    nc.gpsimd.memset(z_sb[:, B * NT:, :], 0.0).then_inc(s_const, 1)
                    nc.gpsimd.iota(expert_id[:, :], pattern=[[1, E]], base=0, channel_multiplier=0,
                                   allow_small_or_imprecise_dtypes=True).then_inc(s_const, 1)
                    nc.gpsimd.iota(region_at[:, :], pattern=[[REGION, E]], base=0, channel_multiplier=0,
                                   allow_small_or_imprecise_dtypes=True).then_inc(s_const, 1)
                    nc.gpsimd.iota(full_blocks[:, :], pattern=[[BLK, MAX_BLOCKS]], base=0, channel_multiplier=0,
                                   allow_small_or_imprecise_dtypes=True).then_inc(s_const, 1)
                    nc.gpsimd.memset(ones_bf[:, :], 1.0).then_inc(s_const, 1)
                    nc.gpsimd.memset(gates[:, B * NT:, :], 0.0).then_inc(s_const, 1)
                    nc.gpsimd.memset(fill[:, :, 0:D], 0.0).then_inc(s_const, 1)
                    nc.gpsimd.memset(fill[:, :, D + 1], -1.0).then_inc(s_const, 1)
                    nc.gpsimd.iota(fill[:, :, D], pattern=[[P, BT]], base=(TOP - 1) * B * T, channel_multiplier=1,
                                   allow_small_or_imprecise_dtypes=True).then_inc(s_const, 1)
                    nc.gpsimd.iota(token[:, :], pattern=[[P, (B + 1) * NT]], base=0, channel_multiplier=1,
                                   allow_small_or_imprecise_dtypes=True).then_inc(s_const, 1)

                @block.scalar
                def _(act):
                    act.dma_start(rows[0:E * FC, :], b1.rearrange("e (c f) -> (e c) f", f=P)).then_inc(s_small, 16)
                    for k, v in enumerate((gamma, beta, attn_norm_w, out_norm_w, mlp_norm_w)):
                        act.dma_start(rows[E * FC + k:E * FC + k + 1, :],
                                      v.rearrange("(a n) -> a n", a=1)).then_inc(s_small, 16)
                    act.dma_start(b2_sb[:, :], b2).then_inc(s_small, 16)
                    act.dma_start(Wr_sb[:, :], Wr).then_inc(s_small, 16)
                    act.dma_start(br_sb[:, :], br.partition_broadcast(P)).then_inc(s_small, 16)
                    act.dma_start(wn_sb[:, :], attn_norm_w.partition_broadcast(P)).then_inc(s_small, 16)
                    job = 0
                    for dst, step, scale in (
                            (M_hi, 2, DHA ** -0.5), (WOT_sb, 1, 1.0), (U_hi, 2, 1.0)):
                        for k in range(2 * step):
                            first = (k // 2) + step * 4 * (k % 2)
                            act.wait_ge(s_prod, job + 1)
                            nc.scalar.activation(dst[:, first:first + 3 * step + 1:step, :],
                                                 bank[job % 7][:, :].rearrange("p (h e) -> p h e", e=D),
                                                 ACT.Copy, scale=scale).then_inc(s_evac, 1)
                            job += 1

                @block.tensor
                def _(pe):
                    job = 0

                    def next_bank():
                        if job >= 7:
                            pe.wait_ge(s_evac, job - 6)
                            pe.wait_ge(s_low, min(job - 6, 4))
                        return bank[job % 7]

                    pe.wait_ge(s_heads, 64)
                    for k in range(4):
                        ps = next_bank()
                        for m in range(4):
                            h = k // 2 + 2 * (4 * (k % 2) + m)
                            r = slice(DHA * (h % 2), DHA * (h % 2) + DHA)
                            mm = nc.tensor.matmul(ps[:, m * D:(m + 1) * D], WK_sb[r, h // 2, :], WQ_sb[r, h // 2, :],
                                                  start=True, stop=True)
                        mm.then_inc(s_prod, 1)
                        job += 1
                    pe.wait_ge(s_const, CONSTS)
                    for k in range(2):
                        ps = next_bank()
                        for m in range(4):
                            c = 4 * k + m
                            mm = nc.tensor.transpose(ps[:, m * P:(m + 1) * P], WO_sb[:, c * P:(c + 1) * P],
                                                     ident[:, :])
                        mm.then_inc(s_prod, 1)
                        job += 1
                    for k in range(4):
                        ps = next_bank()
                        if k == 0:
                            pe.wait_ge(s_evac, 6)
                        for m in range(4):
                            h = k // 2 + 2 * (4 * (k % 2) + m)
                            r = slice(DHA * (h % 2), DHA * (h % 2) + DHA)
                            mm = nc.tensor.matmul(ps[:, m * D:(m + 1) * D], WV_sb[r, h // 2, :], WOT_sb[r, h // 2, :],
                                                  start=True, stop=True)
                        mm.then_inc(s_prod, 1)
                        job += 1
                    pe.wait_ge(s_small, 160)
                    n = E * FC + 5
                    nc.tensor.transpose(bank[7][:, 0:n], rows[:, :], ident[0:n, 0:n]).then_inc(s_rows, 1)

                @block.vector
                def _(dve):
                    for lo, hi, job, scale in ((M_lo, M_hi, 0, DHA ** -0.5), (U_lo, U_hi, 6, 1.0)):
                        for k in range(4):
                            first = (k // 2) + 8 * (k % 2)
                            heads = slice(first, first + 7, 2)
                            dve.wait_ge(s_evac, job + 1)
                            nc.vector.scalar_tensor_tensor(
                                out=lo[:, heads, :], in0=bank[job % 7][:, :].rearrange("p (h e) -> p h e", e=D),
                                scalar=scale, in1=hi[:, heads, :], op0=ALU.mult,
                                op1=ALU.subtract).then_inc(s_low, 1)
                            job += 1
                    dve.wait_ge(s_rows, 1)
                    nc.vector.tensor_copy(cols[:, :], bank[7][:, 0:E * FC + 5]).then_inc(s_cols, 1)

        def uses_ago(n, ring, per_row):
            if n >= ring:
                return ring
            return min(ring, per_row + n - max(m for m in range(per_row) if m % ring == n))

        LN, LN_LN, RMS = range(3)

        class Ahead:

            def __init__(self, name, at, kind, src, scale, bias, want_sum=False, want_htok=False,
                         in_place=False, split=False, bankT=bank[0]):
                self.bankT, self.in_place, self.split = bankT, in_place, split
                self.kind, self.src, self.scale, self.bias = kind, src, scale, bias
                self.want_y = kind == LN_LN and not in_place
                self.want_sum, self.want_htok = want_sum, want_htok
                self.bn = sb(name + "_bn", [P, 2, NT, 6], at=at)
                self.mv = sb(name + "_mv", [P, 2, NT, 2], at=at)
                self.power = sb(name + "_power", [P, 2, 8, NT], at=at)
                self.xn_sb = sb(name + "_xn", [P, 2, NT, W if in_place else D], at=at)
                self.xnT = sb(name + "_xnT", [P, 2, T], at=at)
                if split:
                    self.hi = sb(name + "_xnT_hi", [P, 2, T], f32r, at=at)
                    self.lo = sb(name + "_xnT_lo", [P, 2, T], f32r, at=at)
                if self.want_y:
                    self.y_sb = sb(name + "_y", [P, 2, NT, D], at=at)
                if want_sum:
                    self.sum_sb = sb(name + "_xz", [P, 2, NT, D], at=at)
                if want_htok:
                    self.htok_sb = sb(name + "_htok", [P, 2, NT, D], at=at)
                self.stats = sem(name + "_stats_ready", at)
                self.counted = sem(name + "_stats_counted", at)
                self.moments = sem(name + "_moments_ready", at)
                self.pool_step = sem(name + "_pool_step", at)
                self.rstd = sem(name + "_rstd_ready", at)
                self.xn = sem(name + "_xn_ready", at)
                self.y = sem(name + "_y_ready", at)
                self.sum = sem(name + "_sum_ready", at)
                self.htok = sem(name + "_htok_ready", at)
                self.tr = sem(name + "_transposed", at)
                self.lo_ready = sem(name + "_lo_ready", at)
                self.of_dve = (self.stats, self.moments, self.xn, self.y, self.lo_ready)
                self.of_pool = (self.pool_step, self.rstd, self.sum, self.htok)

            def tiles(self, b, where=None):
                return (self.src if where is None else where)[:, bass.ds(b * NT, NT), :]

            def dve_stats(self, dve, b, u):
                for t in range(NT):
                    nc.vector.bn_stats(self.bn[:, u, t, :],
                                       self.src[:, bass.ds(b * NT + t, 1), :]).then_inc(self.stats, 1)
                dve.wait_ge(self.stats, START + b * NT + NT)
                dve.sem_inc(self.counted, 1)
                for t in range(NT):
                    nc.vector.bn_aggr(self.mv[:, u, t, :], self.bn[:, u, t, :]).then_inc(self.moments, 1)

            def pool_rstd(self, pool, b, u):
                pw = [self.power[:, u, k, :] for k in range(8)]
                mean, var = self.mv[:, u, :, 0], self.mv[:, u, :, 1]
                TT = nc.gpsimd.tensor_tensor
                per_row = {LN: 1, LN_LN: 7 if self.in_place else 5, RMS: 3}[self.kind]
                done = [0]

                def then_next(ins):
                    done[0] += 1
                    ins.then_inc(self.pool_step, 1)
                    pool.wait_ge(self.pool_step, START + b * per_row + done[0])

                pool.wait_ge(self.moments, START + b * NT + NT)
                if self.kind == RMS:
                    then_next(TT(pw[1], mean, mean, ALU.mult))
                    then_next(TT(pw[2], pw[1], var, ALU.add))
                    then_next(TT(pw[3], pw[2], eps[:, :], ALU.add))
                    TT(pw[5], pw[3], half[:, :], ALU.pow).then_inc(self.rstd, 1)
                    return
                then_next(TT(pw[1], var, eps[:, :], ALU.add))
                if self.kind == LN:
                    TT(pw[5], pw[1], half[:, :], ALU.pow).then_inc(self.rstd, 1)
                    return
                then_next(TT(pw[0], pw[1], half[:, :], ALU.pow))
                if self.in_place:
                    TT(pw[6], pw[0], unit[:, :], ALU.add).then_inc(self.pool_step, 1)
                    TT(pw[7], pw[0], mean, ALU.mult).then_inc(self.pool_step, 1)
                    done[0] += 2
                then_next(TT(pw[2], pw[0], pw[0], ALU.mult))
                then_next(TT(pw[3], pw[2], var, ALU.mult))
                then_next(TT(pw[4], pw[3], eps[:, :], ALU.add))
                TT(pw[2], pw[4], half[:, :], ALU.pow).then_inc(self.rstd, 1)
                pool.wait_ge(self.rstd, START + 2 * b + 1)
                TT(pw[5], pw[0], pw[2], ALU.mult).then_inc(self.rstd, 1)

            def dve_normalise(self, dve, b, u):
                dve.wait_ge(self.rstd, START + ((2 * b + 2) if self.kind == LN_LN else (b + 1)))
                for t in range(NT):
                    tile = self.src[:, bass.ds(b * NT + t, 1), :]
                    if self.kind == RMS:
                        nc.vector.tensor_scalar(self.xn_sb[:, u, t:t + 1, 0:D], tile, self.power[:, u, 5, t:t + 1], None,
                                                ALU.mult).then_inc(self.xn, 1)
                        continue
                    mean = self.mv[:, u, t, 0:1]
                    nc.vector.tensor_scalar(self.xn_sb[:, u, t:t + 1, 0:D], tile, mean, self.power[:, u, 5, t:t + 1],
                                            ALU.subtract, ALU.mult).then_inc(self.xn, 1)
                    if self.want_y:
                        nc.vector.tensor_scalar(self.y_sb[:, u, t:t + 1, :], tile, mean, self.power[:, u, 0, t:t + 1],
                                                ALU.subtract, ALU.mult).then_inc(self.y, 1)
                if self.in_place:
                    for t in range(NT):
                        tile = self.src[:, bass.ds(b * NT + t, 1), :]
                        nc.vector.tensor_scalar(tile, tile, self.power[:, u, 6, t:t + 1], self.power[:, u, 7, t:t + 1],
                                                ALU.mult, ALU.subtract).then_inc(self.y, 1)

            def pool_finish(self, pool, b, u):
                pool.wait_ge(self.xn, START + b * NT + NT)
                if self.want_sum:
                    nc.gpsimd.tensor_tensor(self.sum_sb[:, u, :, :], self.tiles(b, x_sb), self.tiles(b),
                                            ALU.add).then_inc(self.sum, 1)
                if self.want_htok:
                    nc.gpsimd.tensor_tensor(self.htok_sb[:, u, :, :], self.xn_sb[:, u, :, :],
                                            wn_sb[:, :].unsqueeze(1).to_broadcast([P, NT, D]),
                                            ALU.mult).then_inc(self.htok, 1)

            def pe_transpose(self, pe, b, u):
                pe.wait_ge(self.xn, START + b * NT + NT)
                for t in range(NT):
                    mm = nc.tensor.transpose(self.bankT[:, t * P:(t + 1) * P], self.xn_sb[:, u, t, 0:D], ident[:, :])
                mm.then_inc(self.tr, 1)

            def act_evacuate(self, act, b, u, done):
                act.wait_ge(self.tr, START + b + 1)
                for out in ([self.hi] if self.split else []) + [self.xnT]:
                    if self.bias is not None:
                        ins = nc.scalar.activation(out[:, u, :], self.bankT[:, :], ACT.Identity, bias=self.bias,
                                                   scale=self.scale)
                    else:
                        ins = nc.scalar.activation(out[:, u, :], self.bankT[:, :], ACT.Copy, scale=self.scale)
                ins.then_inc(done, 1)

            def dve_low(self, dve, b, u, done):
                dve.wait_ge(done, START + b + 1)
                nc.vector.tensor_tensor(self.lo[:, u, :], self.xnT[:, u, :], self.hi[:, u, :],
                                        ALU.subtract).then_inc(self.lo_ready, 1)

        def matmul3(ps, lhsT_hi, lhsT_lo, rhs_hi, rhs_lo, stop=True):
            nc.tensor.matmul(ps, lhsT_hi, rhs_hi, start=True, stop=False)
            nc.tensor.matmul(ps, lhsT_hi, rhs_lo, start=False, stop=False)
            return nc.tensor.matmul(ps, lhsT_lo, rhs_hi, start=False, stop=stop)

        def begin(eng, *semaphores):
            for s in semaphores:
                eng.sem_inc(s, START)

        def each_row(eng, row):
            row(0, 0)
            with eng.Fori(0, B // 2 - 1) as pair:
                row(pair * 2 + 1, 1)
                row(pair * 2 + 2, 0)
            row(B - 1, 1)

        def is_row(b, which):
            return isinstance(b, int) and b == which

        PRIMED = 16

        def prime(pool, *semaphores):
            for s in semaphores:
                col = primed[0]
                primed[0] += 1
                pool.dma_start(spare[:, col:col + 1], z_sb[0:1, B * NT, col:col + 1]).then_inc(s, PRIMED)
            for s in semaphores:
                pool.wait_ge(s, PRIMED)

        primed = [0]

        class Route:

            LOGIT, RMAX, TOPS = 1, 2, 3 + NT
            TOPID = TOPS + 1 + NT
            IDS, IS_K, ROW_SEL = TOPID + 2, TOPID + 4, TOPID + 5
            PLACE, PICKED, SLOTF = ROW_SEL + 1, ROW_SEL + 3, ROW_SEL + 4
            DVE_STEPS = SLOTF
            wide = [P, NT, E]

            def __init__(self, name, at, bankR):
                self.bankR = bankR
                self.norm = Ahead(name, at, LN_LN, x_sb, gamma_col, beta_col, in_place=True, bankT=bankR)
                self.logit = sb(name + "_logit", [P, NT, E], f32, at=at)
                self.shifted = sb(name + "_shifted", [P, NT, E], f32, at=at)
                self.ex = sb(name + "_ex", [P, NT, E], f32, at=at)
                self.top = sb(name + "_top", [P, NT, E], f32, at=at)
                self.topid = sb(name + "_topid", [P, NT, E], u32, at=at)
                self.topidf = sb(name + "_topidf", [P, NT, E], f32, at=at)
                self.rmax = sb(name + "_rmax", [P, NT, 1], f32, at=at)
                self.rsum = sb(name + "_rsum", [P, NT, 1], f32, at=at)
                self.rrec = sb(name + "_rrec", [P, NT, 1], f32, at=at)
                self.is_k = sb(name + "_is_k", [P, TOP, NT, E], at=at)
                self.picked = sb(name + "_picked", [P, TOP, NT, E], at=at)
                self.sel = sb(name + "_sel", [P, NT, E], bf16, at=at)
                self.row_sel = sb(name + "_row_sel", [P, E], at=at)
                self.run = sb(name + "_run", [P, E], at=at)
                self.place = sb(name + "_place", [P, NT, E], at=at)
                self.slotf = sb(name + "_slotf", [P, TOP, NT], at=at)
                self.slot = sb(name + "_slot", [P, 2, NT, TOP], i32, at=at)
                self.logits_ready = sem(name + "_logits_ready", at)
                self.shifted_ready = sem(name + "_shifted_ready", at)
                self.ex_ready = sem(name + "_ex_ready", at)
                self.step = sem(name + "_route_step", at)
                self.sel_ready = sem(name + "_sel_ready", at)
                self.run_ready = sem(name + "_run_ready", at)
                self.rank_ready = sem(name + "_rank_ready", at)
                self.slot_ready = sem(name + "_slot_ready", at)
                self.tagged = sem(name + "_tagged", at)
                self.xnT_ready = sem(name + "_xnT_ready", at)
                self.may_scatter = sem(name + "_may_scatter", at)
                self.scattered = [sem(f"{name}_scattered{u}", at) for u in range(2)]
                self.of_dve = (self.shifted_ready, self.step, self.sel_ready, self.run_ready, self.slot_ready,
                               self.tagged, *self.norm.of_dve)
                self.of_pe = (self.logits_ready, self.rank_ready, self.norm.tr)
                self.of_act = (self.ex_ready, self.xnT_ready)
                self.of_pool = self.norm.of_pool

            def dve_begin(self, dve):
                nc.vector.memset(self.run[:, :], 0.0).then_inc(self.run_ready, 1)
                nc.vector.memset(run_bf[:, :], 0.0).then_inc(self.run_ready, 1)

            def pe_logits(self, pe, b, u):
                pe.wait_ge(self.xnT_ready, START + b + 1)
                pe.wait_ge(self.slot_ready, START + b)
                for t in range(NT):
                    mm = nc.tensor.matmul(self.bankR[:, t * E:(t + 1) * E], self.norm.xnT[:, u, t * P:(t + 1) * P],
                                          Wr_sb[:, :], start=True, stop=True)
                mm.then_inc(self.logits_ready, 1)

            def settle(self, dve, b, count):
                dve.wait_ge(self.step, START + b * self.DVE_STEPS + count)

            def dve_logit(self, dve, b, u):
                dve.wait_ge(self.logits_ready, START + b + 1)
                nc.vector.tensor_tensor(
                    self.logit[:, :, :], self.bankR[:, 0:NT * E].rearrange("p (t e) -> p t e", e=E),
                    br_sb[:, :].unsqueeze(1).to_broadcast(self.wide), ALU.add).then_inc(self.step, 1)

            def dve_rmax(self, dve, b, u):
                self.settle(dve, b, self.LOGIT)
                nc.vector.tensor_reduce(self.rmax[:, :, 0], self.logit[:, :, :], AX.X, ALU.max).then_inc(self.step, 1)

            def dve_shift(self, dve, b, u):
                self.settle(dve, b, self.RMAX)
                nc.vector.tensor_tensor(self.shifted[:, :, :], self.logit[:, :, :],
                                        self.rmax[:, :, :].to_broadcast(self.wide),
                                        ALU.subtract).then_inc(self.shifted_ready, 1)

            def act_exp(self, act, b, u):
                act.wait_ge(self.shifted_ready, START + b + 1)
                nc.scalar.activation(self.ex[:, :, :], self.shifted[:, :, :], ACT.Exp).then_inc(self.ex_ready, 1)

            def dve_top(self, dve, b, u):
                dve.wait_ge(self.ex_ready, START + b + 1)
                nc.vector.tensor_reduce(self.rsum[:, :, 0], self.ex[:, :, :], AX.X, ALU.add).then_inc(self.step, 1)
                for t in range(NT):
                    nc.vector.max(self.top[:, t, :], self.ex[:, t, :]).then_inc(self.step, 1)

            def dve_topid(self, dve, b, u):
                self.settle(dve, b, self.TOPS)
                nc.vector.reciprocal(self.rrec[:, :, :], self.rsum[:, :, :]).then_inc(self.step, 1)
                for t in range(NT):
                    nc.vector.max_index(self.topid[:, t, :], self.top[:, t, :], self.ex[:, t, :]).then_inc(self.step, 1)

            def dve_ids(self, dve, b, u):
                self.settle(dve, b, self.TOPID)
                nc.vector.tensor_copy(self.topidf[:, :, :], self.topid[:, :, :]).then_inc(self.step, 1)
                nc.vector.tensor_tensor(gates[:, bass.ds(b * NT, NT), :], self.top[:, :, 0:TOP],
                                        self.rrec[:, :, :].to_broadcast([P, NT, TOP]), ALU.mult).then_inc(self.step, 1)

            def dve_is_k(self, dve, b, u):
                self.settle(dve, b, self.IDS)
                nc.vector.tensor_copy(self.norm.xn_sb[:, u, :, D], token[:, bass.ds(b * NT, NT)]
                                      ).then_inc(self.tagged, 1)
                nc.vector.tensor_copy(self.norm.xn_sb[:, u, :, D + 1], self.topidf[:, :, 0]).then_inc(self.tagged, 1)
                for k in range(TOP):
                    nc.vector.tensor_tensor(self.is_k[:, k, :, :],
                                            expert_id[:, :].unsqueeze(1).to_broadcast(self.wide),
                                            self.topidf[:, :, k:k + 1].to_broadcast(self.wide),
                                            ALU.is_equal).then_inc(self.step, 1)

            def dve_sel(self, dve, b, u):
                self.settle(dve, b, self.IS_K)
                nc.vector.tensor_tensor(self.sel[:, :, :], self.is_k[:, 0, :, :], self.is_k[:, 1, :, :],
                                        ALU.add).then_inc(self.sel_ready, 1)

            def dve_row_sel(self, dve, b, u):
                dve.wait_ge(self.sel_ready, START + b + 1)
                nc.vector.tensor_reduce(self.row_sel[:, :], self.sel[:, :, :].rearrange("p t e -> p e t"),
                                        AX.X, ALU.add).then_inc(self.step, 1)

            def pe_rank(self, pe, b, u):
                pe.wait_ge(self.sel_ready, START + b + 1)
                pe.wait_ge(self.run_ready, START + 2 * b + 2)
                c0 = NT * E
                nc.tensor.matmul(self.bankR[:, c0:2 * c0], before_bf[:, :], self.sel[:, :, :], start=True, stop=False)
                for d in range(1, NT):
                    nc.tensor.matmul(self.bankR[:, c0 + d * E:2 * c0], ones_bf[:, :], self.sel[:, 0:NT - d, :],
                                     start=False, stop=False, skip_group_check=True)
                nc.tensor.matmul(self.bankR[:, c0:2 * c0], ones_bf[:, :],
                                 run_bf[:, :].unsqueeze(1).to_broadcast([P, NT, E]), start=False,
                                 stop=True).then_inc(self.rank_ready, 1)

            def dve_place(self, dve, b, u):
                dve.wait_ge(self.rank_ready, START + b + 1)
                self.settle(dve, b, self.ROW_SEL)
                nc.vector.tensor_tensor(
                    self.place[:, :, :], self.bankR[:, NT * E:2 * NT * E].rearrange("p (t e) -> p t e", e=E),
                    region_at[:, :].unsqueeze(1).to_broadcast(self.wide), ALU.add).then_inc(self.step, 1)
                dve.wait_ge(self.run_ready, START + 2 * b + 2)
                nc.vector.tensor_tensor(self.run[:, :], self.run[:, :], self.row_sel[:, :],
                                        ALU.add).then_inc(self.run_ready, 1)

            def dve_picked(self, dve, b, u):
                self.settle(dve, b, self.PLACE)
                for k in range(TOP):
                    nc.vector.tensor_tensor(self.picked[:, k, :, :], self.is_k[:, k, :, :],
                                            self.place[:, :, :], ALU.mult).then_inc(self.step, 1)
                dve.wait_ge(self.run_ready, START + 2 * b + 3)
                nc.vector.tensor_copy(run_bf[:, :], self.run[:, :]).then_inc(self.run_ready, 1)

            def dve_slotf(self, dve, b, u):
                self.settle(dve, b, self.PICKED)
                nc.vector.tensor_reduce(self.slotf[:, :, :], self.picked[:, :, :, :], AX.X,
                                        ALU.add).then_inc(self.step, 1)

            def dve_slots(self, dve, b, u):
                self.settle(dve, b, self.SLOTF)
                dve.wait_ge(self.scattered[u], PRIMED + (b - u) * (8 * TOP * NT))
                by_tile = self.slotf[:, :, :].rearrange("p k t -> p t k")
                nc.vector.tensor_copy(self.slot[:, u, :, :], by_tile).then_inc(self.slot_ready, 1)

            def dve_normalise(self, dve, b, u):
                dve.wait_ge(self.scattered[u], PRIMED + (b - u) * (8 * TOP * NT))
                self.norm.dve_normalise(dve, b, u)

            def pool_scatter(self, pool, b, u, tiles=range(NT)):
                pool.wait_ge(self.slot_ready, START + b + 1)
                pool.wait_ge(self.norm.xn, START + b * NT + NT)
                pool.wait_ge(self.tagged, START + 2 * b + 2)
                pool.sem_inc(self.may_scatter, 1)
                for t in tiles:
                    for k in range(TOP):
                        pool.indirect_dma_start(
                            xg, bass.IndirectOffsetOnAxis(ap=self.slot[:, u, t, k:k + 1], axis=0),
                            self.norm.xn_sb[:, u, t, :], None).then_inc(self.scattered[u], 16)

        class Folding:

            def __init__(self, at, Vraw):
                free = Vraw[:, 0, :, :, :].rearrange("p t h d -> p (t h) d")
                self.WqT, self.WkT = free[:, 0:HB, :], free[:, HB:2 * HB, :]
                self.rb1 = sb("rb1", [P, E, FC, E], at=at)
                self.c = sb("c_sb", [E, D], at=at)
                self.b2_c = sb("b2_c", [E, D], at=at)
                self.const = sb("const_e", [E, D], at=at)
                self.diag = z_sb[0:E, 2 * HB:2 * HB + E, :]
                self.product, self.copied = sem("fold_product", at), sem("fold_copied", at)
                self.rb1_clear, self.rb1_ready = sem("rb1_clear", at), sem("rb1_ready", at)
                self.c_done, self.c_ready, self.csum_done = sem("c_done", at), sem("c_ready", at), sem("csum_done", at)
                self.b2_c_ready, self.const_ready = sem("b2_c_ready", at), sem("const_ready", at)
                self.diag_ready = sem("diag_ready", at)
                self.moe_done, self.moe_copied = sem("moe_const_done", at), sem("moe_const_copied", at)
                self.scaled = sem("Wo_scaled", at)
                self.Wv_hi_ready, self.low = sem("Wv_hi_ready", at), sem("fold_low", at)

            def pe(self, pe, experts):
                pe.wait_ge(s_lin, 48)
                job = 1
                for src in (Wq_sb, Wk_sb):
                    for k in range(2):
                        for m in range(4):
                            mm = nc.tensor.transpose(bank[job][:, m * P:(m + 1) * P], src[:, 4 * k + m, :], ident[:, :])
                        mm.then_inc(self.product, 1)
                        job += 1
                pe.wait_ge(self.rb1_ready, E)
                pe.wait_ge(s_big, 96)
                pe.wait_ge(experts.plan_step, 1)
                for e in range(E):
                    for c in range(FC):
                        mm = nc.tensor.matmul(bank[7][0:E, 0:D], self.rb1[:, e, c, :], W2_sb[:, e, c, :],
                                              start=(e == 0 and c == 0), stop=(e == E - 1 and c == FC - 1))
                mm.then_inc(self.c_done, 1)
                pe.wait_ge(self.copied, 4)
                for k in range(2):
                    for m in range(4):
                        h = 4 * k + m
                        mm = nc.tensor.matmul(bank[job][:, m * D:(m + 1) * D], self.WqT[:, h, :], self.WkT[:, h, :],
                                              start=True, stop=True)
                    mm.then_inc(self.product, 1)
                    job += 1
                pe.wait_ge(self.c_ready, 1)
                pe.wait_ge(self.b2_c_ready, 1)
                nc.tensor.matmul(bank[7][0:E, 0:D], ones[:, 0:E], self.c[:, :], start=True,
                                 stop=True).then_inc(self.csum_done, 1)
                pe.wait_ge(self.diag_ready, 1)
                pe.wait_ge(self.copied, 6)
                pe.wait_ge(self.low, 2)
                for g in range(2):
                    nc.tensor.matmul(bank[5 + g][:, :], ones[:, :], self.diag[:, 4 * g:4 * g + 4, :],
                                     start=True, stop=True).then_inc(self.moe_done, 1)
                pe.wait_ge(self.moe_copied, 2)

            def act(self, act):
                job = 0
                for dst in (self.WqT, self.WkT, A_hi):
                    for k in range(2):
                        act.wait_ge(self.product, job + 1)
                        nc.scalar.activation(dst[:, 4 * k:4 * k + 4, :],
                                             bank[1 + job][:, :].rearrange("p (h e) -> p h e", e=D),
                                             ACT.Copy).then_inc(self.copied, 1)
                        job += 1
                nc.scalar.activation(Wv_hi[:, :], Wv_sb, ACT.Copy).then_inc(self.Wv_hi_ready, 1)

            def dve_early(self, dve):
                nc.vector.memset(self.rb1[:, :, :, :], 0.0).then_inc(self.rb1_clear, 1)
                dve.wait_ge(self.rb1_clear, 1)
                for e in range(E):
                    nc.vector.tensor_scalar(self.rb1[:, e, :, e], b1_col[:, e * FC:(e + 1) * FC], 0.0, None,
                                            ALU.max).then_inc(self.rb1_ready, 1)

            def dve(self, dve):
                dve.wait_ge(self.c_done, 1)
                nc.vector.tensor_tensor(self.c[:, :], bank[7][0:E, 0:D], b2_sb[:, :],
                                        ALU.add).then_inc(self.c_ready, 1)
                dve.wait_ge(self.c_ready, 1)
                nc.vector.tensor_tensor(self.b2_c[:, :], b2_sb[:, :], self.c[:, :],
                                        ALU.subtract).then_inc(self.b2_c_ready, 1)
                dve.wait_ge(s_lin, 48)
                nc.vector.tensor_scalar(Wo_sb[:, :, :], Wo_sb[:, :, :], out_norm_col, None,
                                        ALU.mult).then_inc(self.scaled, 1)
                for k in range(2):
                    four = slice(4 * k, 4 * k + 4)
                    dve.wait_ge(self.copied, 5 + k)
                    nc.vector.tensor_tensor(A_lo[:, four, :], bank[5 + k][:, :].rearrange("p (h e) -> p h e", e=D),
                                            A_hi[:, four, :], ALU.subtract).then_inc(self.low, 1)
                dve.wait_ge(self.csum_done, 1)
                dve.wait_ge(self.b2_c_ready, 1)
                nc.vector.tensor_tensor(self.const[:, :], bank[7][0:E, 0:D], self.b2_c[:, :],
                                        ALU.add).then_inc(self.const_ready, 1)
                dve.wait_ge(self.const_ready, 1)
                nc.vector.tensor_tensor(self.diag[:, :, :], self.const[:, :].unsqueeze(1).to_broadcast([E, E, D]),
                                        ident[0:E, 0:E].unsqueeze(2).to_broadcast([E, E, D]),
                                        ALU.mult).then_inc(self.diag_ready, 1)
                dve.wait_ge(self.Wv_hi_ready, 1)
                nc.vector.tensor_tensor(Wv_lo[:, :], Wv_sb, Wv_hi[:, :], ALU.subtract).then_inc(self.low, 1)
                for g in range(2):
                    dve.wait_ge(self.moe_done, g + 1)
                    nc.vector.tensor_copy(moe_const[:, 4 * g:4 * g + 4, :],
                                          bank[5 + g][:, :].rearrange("p (e d) -> p e d", d=D)
                                          ).then_inc(self.moe_copied, 1)

        class Experts:

            def __init__(self, name, at, hid=None):
                self.counts = sb(name + "_x_counts", [P, E], at=at)
                self.over = sb(name + "_x_over", [P, E, MAX_BLOCKS], at=at)
                self.nblocks = sb(name + "_x_nblocks", [P, E], at=at)
                self.fillf = sb(name + "_x_fillf", [P, E], at=at)
                self.counted, self.plan_step = sem(name + "_x_counted", at), sem(name + "_x_plan_step", at)
                self.plan_ready = sem(name + "_x_plan_ready", at)
                self.filled = [sem(f"{name}_x_filled_{of}", at) for of in ("sp", "act")]

                self.xb = sb(name + "_x_xb", [P, BT, W], at=at)
                self.second = sb(name + "_x_second", [P, BT], at=at)
                self.first = sb(name + "_x_first", [P, BT], at=at)
                self.next_token = sb(name + "_x_next_token", [P, BT], at=at)
                self.this_to = sb(name + "_x_this_to", [P, BT], at=at)
                self.to = sb(name + "_x_to", [P, BT], i32, at=at)
                self.xbT = sb(name + "_x_xbT", [P, BLK], at=at)
                self.hid = sb(name + "_x_hid", [P, FC, BLK], at=at) if hid is None else hid
                self.yb = sb(name + "_x_yb", [P, BT, D], at=at)
                self.bankX, self.bankH, self.bankY = bank[0], bank[1:1 + FC], bank[1 + FC]
                self.loaded = sem(name + "_x_block_loaded", at)
                self.transposed = sem(name + "_x_block_transposed", at)
                self.xbT_ready = sem(name + "_x_xbT_ready", at)
                self.up_done = [sem(f"{name}_x_up_done{c}", at) for c in range(FC)]
                self.hid_ready = [sem(f"{name}_x_hid_ready{c}", at) for c in range(FC)]
                self.down_done = sem(name + "_x_down_done", at)
                self.y_ready = [sem(f"{name}_x_y_ready{t}", at) for t in range(BT)]
                self.first_ready = sem(name + "_x_first_ready", at)
                self.next_token_ready = sem(name + "_x_next_token_ready", at)
                self.this_to_ready = sem(name + "_x_this_to_ready", at)
                self.second_known = sem(name + "_x_second_known", at)
                self.to_ready = [sem(f"{name}_x_to_ready{t}", at) for t in range(BT)]
                self.stored = [sem(f"{name}_x_tile_stored{t}", at) for t in range(BT)]
                self.may_store = sem(name + "_x_may_store", at)
                self.name = name

            def each_block(self, eng, body, before=None):
                count = eng.alloc_register(self.name + "_block")
                dmas = eng.alloc_register(self.name + "_block_dmas")
                eng.reg_mov(count, START)
                eng.reg_mov(dmas, START)
                n = [eng.value_load(blocks[0:1, e:e + 1], min_val=1, max_val=MAX_BLOCKS) for e in range(E)]
                if before is not None:
                    before()
                for e in range(E):
                    with eng.Fori(0, n[e]) as i:
                        k, k16 = eng.snap(count), eng.snap(dmas)
                        body(e, i * BLK + e * REGION, k, k16)
                        eng.reg_add(count, count, 1)
                        eng.reg_add(dmas, dmas, 16)
                return eng.snap(count), eng.snap(dmas)

            def pe_count(self, pe, route):
                pe.wait_ge(route.run_ready, START + 2 * B + 2)
                pe.wait_ge(route.slot_ready, START + B)
                nc.tensor.matmul(bank[7][:, 0:E], ones_bf[:, :], run_bf[:, :], start=True,
                                 stop=True).then_inc(self.counted, 1)

            def dve_plan(self, dve):
                dve.wait_ge(self.counted, 1)
                nc.vector.tensor_copy(self.counts[:, :], bank[7][:, 0:E]).then_inc(self.plan_step, 1)
                dve.wait_ge(self.plan_step, 1)
                nc.vector.tensor_tensor(self.fillf[:, :], self.counts[:, :], region_at[:, :],
                                        ALU.add).then_inc(self.plan_step, 1)
                nc.vector.tensor_tensor(self.over[:, :, :],
                                        self.counts[:, :].unsqueeze(2).to_broadcast([P, E, MAX_BLOCKS]),
                                        full_blocks[:, :].unsqueeze(1).to_broadcast([P, E, MAX_BLOCKS]),
                                        ALU.is_gt).then_inc(self.plan_step, 1)
                dve.wait_ge(self.plan_step, 3)
                nc.vector.tensor_copy(fill_at[:, :], self.fillf[:, :]).then_inc(self.plan_ready, 1)
                nc.vector.tensor_reduce(self.nblocks[:, :], self.over[:, :, :], AX.X,
                                        ALU.add).then_inc(self.plan_step, 1)
                dve.wait_ge(self.plan_step, 4)
                nc.vector.tensor_scalar(blocks[:, :], self.nblocks[:, :], 1.0, None,
                                        ALU.max).then_inc(self.plan_ready, 1)

            def fill(self, eng, some, filled):
                eng.wait_ge(self.plan_ready, 2)
                for e in some:
                    first = eng.value_load(fill_at[0:1, e:e + 1], min_val=e * REGION, max_val=e * REGION + B * T)
                    eng.dma_start(xg[bass.ds(first, BLK), :].rearrange("(t p) d -> p t d", p=P),
                                  fill[:, :, :]).then_inc(filled, 16)

            def sp_work(self, sp, route):
                begin(sp, self.loaded)

                def load(row, k):
                    sp.wait_ge(self.transposed, k)
                    sp.wait_ge(self.next_token_ready, k)
                    sp.dma_start(self.xb[:, :, :], xg[bass.ds(row, BLK), :].rearrange("(t p) d -> p t d", p=P)
                                 ).then_inc(self.loaded, 16)

                def rows_written():
                    for filled in self.filled:
                        sp.wait_ge(filled, 16 * (E // 2))
                    for u in range(2):
                        sp.wait_ge(route.scattered[u], PRIMED + B // 2 * 16 * TOP * NT)

                end, _ = self.each_block(sp, lambda e, row, k, k16: load(row, k), rows_written)
                load(0, end)

            def pe_work(self, pe):
                begin(pe, self.transposed, *self.up_done, self.down_done)
                pe.wait_ge(self.plan_ready, 2)

                def transpose(k, k16):
                    pe.wait_ge(self.loaded, k16 + 16)
                    pe.wait_ge(self.xbT_ready, k)
                    for t in range(BT):
                        mm = nc.tensor.transpose(self.bankX[:, t * P:(t + 1) * P], self.xb[:, t, 0:D], ident[:, :])
                    mm.then_inc(self.transposed, 1)

                def expert(e, row, k, k16):
                    pe.wait_ge(self.xbT_ready, k + 1)
                    for c in range(FC):
                        pe.wait_ge(self.hid_ready[c], k)
                        nc.tensor.matmul(self.bankH[c][:, 0:BLK], W1_sb[:, e, c * P:(c + 1) * P], self.xbT[:, :],
                                         start=True, stop=True).then_inc(self.up_done[c], 1)
                    transpose(k + 1, k16 + 16)
                    pe.wait_ge(self.y_ready[BT - 1], k)
                    for t in range(BT):
                        for c in range(FC):
                            if t == 0:
                                pe.wait_ge(self.hid_ready[c], k + 1)
                            mm = nc.tensor.matmul(self.bankY[:, t * D:(t + 1) * D], self.hid[:, c, t * P:(t + 1) * P],
                                                  W2_sb[:, e, c, :], start=(c == 0), stop=(c == FC - 1))
                    mm.then_inc(self.down_done, 1)

                self.each_block(pe, expert, lambda: transpose(START, START))

            def act_work(self, act):
                begin(act, *self.hid_ready)
                act.wait_ge(self.plan_ready, 2)

                def relu(e, row, k, k16):
                    act.wait_ge(self.down_done, k)
                    for c in range(FC):
                        act.wait_ge(self.up_done[c], k + 1)
                        nc.scalar.activation(self.hid[:, c, :], self.bankH[c][:, 0:BLK], ACT.Relu,
                                             bias=b1_col[:, e * FC + c:e * FC + c + 1]
                                             ).then_inc(self.hid_ready[c], 1)

                self.each_block(act, relu)

            def dve_work(self, dve):
                begin(dve, self.xbT_ready, self.first_ready, self.next_token_ready, self.this_to_ready,
                      self.second_known, *self.to_ready, *self.y_ready)
                dve.wait_ge(self.plan_ready, 2)

                def prepare(e, k, k16):
                    dve.wait_ge(self.transposed, k + 1)
                    nc.vector.tensor_scalar(self.xbT[:, :], self.bankX[:, 0:BLK], gamma_col, beta_col, ALU.mult,
                                            ALU.add).then_inc(self.xbT_ready, 1)
                    dve.wait_ge(self.loaded, k16 + 16)
                    dve.wait_ge(self.this_to_ready, k)
                    nc.vector.tensor_copy(self.first[:, :], self.xb[:, :, D + 1]).then_inc(self.first_ready, 1)
                    nc.vector.tensor_copy(self.next_token[:, :], self.xb[:, :, D]).then_inc(self.next_token_ready, 1)

                def finish(e, row, k, k16):
                    dve.wait_ge(self.first_ready, k + 1)
                    dve.wait_ge(self.next_token_ready, k + 1)
                    nc.vector.tensor_scalar(self.second[:, :], self.first[:, :], float(e), float(B * T), ALU.not_equal,
                                            ALU.mult).then_inc(self.second_known, 1)
                    dve.wait_ge(self.second_known, k + 1)
                    for t in range(BT):
                        dve.wait_ge(self.to_ready[t], k)
                    nc.vector.tensor_tensor(self.this_to[:, :], self.second[:, :], self.next_token[:, :],
                                            ALU.add).then_inc(self.this_to_ready, 1)
                    dve.wait_ge(self.up_done[FC - 1], k + 1)
                    prepare(e, k + 1, k16 + 16)
                    dve.wait_ge(self.down_done, k + 1)
                    dve.wait_ge(self.this_to_ready, k + 1)
                    for t in range(BT):
                        dve.wait_ge(self.stored[t], k16 + (PRIMED - START))
                        nc.vector.tensor_copy(self.to[:, t:t + 1],
                                              self.this_to[:, t:t + 1]).then_inc(self.to_ready[t], 1)
                        nc.vector.tensor_tensor(self.yb[:, t, :], self.bankY[:, t * D:(t + 1) * D], moe_const[:, e, :],
                                                ALU.add).then_inc(self.y_ready[t], 1)

                self.each_block(dve, finish, lambda: prepare(0, START, START))

            def pool_work(self, pool):
                prime(pool, *self.stored)
                pool.wait_ge(self.plan_ready, 2)

                def store(e, row, k, k16):
                    for t in range(BT):
                        pool.wait_ge(self.y_ready[t], k + 1)
                        pool.wait_ge(self.to_ready[t], k + 1)
                        pool.sem_inc(self.may_store, 1)
                        pool.indirect_dma_start(yg, bass.IndirectOffsetOnAxis(ap=self.to[:, t:t + 1], axis=0),
                                                self.yb[:, t, :], None).then_inc(self.stored[t], 16)

                _, end16 = self.each_block(pool, store)
                for t in range(BT):
                    pool.wait_ge(self.stored[t], end16 + (PRIMED - START))
                    pool.sem_inc(self.may_store, 1)

        with stage() as st:
            ahead = Ahead("a", st, LN, x_sb, 1.0, None, split=True)
            width = [P * (i + 1) for i in range(NT)]
            start = [sum(width[:i]) for i in range(NT)]
            G_sb = sb("G_sb", [P, 2, T - P], at=st)
            G_hi, G_lo = sb("G_hi", [P, 2, P], f32r, at=st), sb("G_lo", [P, 2, P], f32r, at=st)
            Vraw = sb("Vraw", [P, 2, NT, 4, D], at=st)
            folding = Folding(st, Vraw)
            Vs = sb("Vs", [P, 8, D], at=st)
            prob = sb("prob", [P, 2, sum(width)], at=st)
            experts = Experts("f1", st, hid=prob[:, 0, 0:FC * BLK].rearrange("p (c s) -> p c s", s=BLK))
            negmax = sb("negmax", [P, 8], at=st)
            rowsum = sb("rowsum", [P, 8], at=st)
            rinv = sb("rinv", [P, 8], at=st)
            warm = sb("warm", [P, NT], at=st)
            route = Route("f1", st, bank[0])
            bankT, bankO, bankG, bankV, bankS = bank[0], bank[1], bank[2], bank[3:5], bank[5:8]

            xnT_ready = sem("a_xnT_ready", st)
            G_done, G_ready = sem("a_G_done", st), sem("a_G_ready", st)
            G_lo_ready = sem("a_G_lo_ready", st)
            V_done, V_ready = sem("a_V_done", st), sem("a_V_ready", st)
            scores_ready = sem("a_scores_ready", st)
            scores_seen = sem("a_scores_seen", st)
            negmax_ready = sem("a_negmax_ready", st)
            prob_ready = sem("a_prob_ready", st)
            rinv_ready = sem("a_rinv_ready", st)
            Vs_ready = sem("a_Vs_ready", st)
            row_done = sem("a_row_done", st)
            x_done = sem("a_x_done", st)
            x_complete = sem("a_x_complete", st)
            ROUTE_STATS, ROUTE_NORM, ROUTE_TR, ROUTE_LOGITS, ROUTE_EXP, ROUTE_RANK = 5, 10, 14, 16, 21, 31
            ROUTE_DVE = {17: route.dve_logit, 18: route.dve_rmax, 19: route.dve_shift, 22: route.dve_top,
                         23: route.dve_topid, 24: route.dve_ids, 25: route.dve_is_k, 27: route.dve_sel,
                         28: route.dve_row_sel, 33: route.dve_place, 34: route.dve_picked, 35: route.dve_slotf,
                         36: route.dve_slots}
            STATS_AT, NORM_AT, TR_AT, EVAC_AT, LOW_AT = 40, 44, 50, 51, 54

            def step(n):
                return n // NT, NT - 1 - n % NT

            with nc.Block() as block:
                @block.tensor
                def _(pe):
                    begin(pe, G_done, V_done, scores_ready, row_done, ahead.tr, *route.of_pe)
                    ahead.pe_transpose(pe, 0, 0)

                    def G(b, u, h):
                        pe.wait_ge(G_ready, START + b * HA + h)
                        pe.wait_ge(G_lo_ready, START + b * HA + h)
                        matmul3(bankG[:, :], M_hi[:, h, :], M_lo[:, h, :], ahead.hi[:, u, :],
                                ahead.lo[:, u, :]).then_inc(G_done, 1)

                    def V(b, u, g, i):
                        n = g * NT + i
                        pe.wait_ge(V_ready, START + b * (NT * 4) + n - 1)
                        tile, four = slice(i * P, (i + 1) * P), slice(4 * g, 4 * g + 4)
                        matmul3(bankV[n % 2][:, :], ahead.hi[:, u, tile], ahead.lo[:, u, tile], U_hi[:, four, :],
                                U_lo[:, four, :]).then_inc(V_done, 1)

                    def S(b, u, n):
                        h, i = step(n)
                        pe.wait_ge(G_ready, START + b * HA + h + 1)
                        pe.wait_ge(prob_ready, START + b * ND + n + 1 - uses_ago(n, len(bankS), ND))
                        ps = bankS[n % 3]
                        if i == NT - 1:
                            pe.wait_ge(G_lo_ready, START + b * HA + h + 1)
                            matmul3(ps[:, :], G_hi[:, h % 2, :], G_lo[:, h % 2, :], ahead.hi[:, u, :],
                                    ahead.lo[:, u, :]).then_inc(scores_ready, 1)
                        else:
                            nc.tensor.matmul(ps[:, 0:width[i]], G_sb[:, h % 2, i * P:(i + 1) * P],
                                             ahead.xnT[:, u, 0:width[i]], start=True,
                                             stop=True).then_inc(scores_ready, 1)

                    def PV(b, u, n):
                        h, i = step(n)
                        if n == 0:
                            pe.wait_ge(x_done, START + b)
                        pe.wait_ge(prob_ready, START + b * ND + n + 1)
                        pe.wait_ge(Vs_ready, START + b * ND + n + 1)
                        for j in range(i + 1):
                            mm = nc.tensor.matmul(bankO[:, j * D:(j + 1) * D],
                                                  prob[:, h % 2, start[i] + j * P:start[i] + (j + 1) * P],
                                                  Vs[:, n % 8, :], start=(n == 0 and j == 0),
                                                  stop=(h == HA - 1), skip_group_check=True)
                        if n == ND - 1:
                            mm.then_inc(row_done, 1)

                    def row(b, u):
                        pe.wait_ge(xnT_ready, START + b + 1)
                        pe.wait_ge(ahead.lo_ready, START + b + 1)
                        for n in range(ND + NT):
                            if n == 0:
                                G(b, u, 0)
                                for i in range(NT):
                                    V(b, u, 0, i)
                                G(b, u, 1)
                            elif n < ND and n % NT == 0 and n // NT + 1 < HA:
                                G(b, u, n // NT + 1)
                            if n % NT == 2 and n // NT < HA - 4:
                                V(b, u, n // NT // 4 + 1, n // NT % 4)
                            if n < ND:
                                S(b, u, n)
                            if n >= NT:
                                PV(b, u, n - NT)
                            if not is_row(b, 0):
                                if n == ROUTE_TR:
                                    route.norm.pe_transpose(pe, b - 1, 1 - u)
                                if n == ROUTE_LOGITS:
                                    route.pe_logits(pe, b - 1, 1 - u)
                                if n == ROUTE_RANK:
                                    route.pe_rank(pe, b - 1, 1 - u)
                            if n == TR_AT and not is_row(b, B - 1):
                                if not is_row(b, 0):
                                    pe.wait_ge(route.slot_ready, START + b)
                                ahead.pe_transpose(pe, b + 1, 1 - u)

                    each_row(pe, row)
                    route.norm.pe_transpose(pe, B - 1, 1)
                    route.pe_logits(pe, B - 1, 1)
                    route.pe_rank(pe, B - 1, 1)
                    experts.pe_count(pe, route)
                    pe.wait_ge(G_ready, START + B * HA)
                    pe.wait_ge(V_ready, START + B * NT * 4)
                    folding.pe(pe, experts)
                    experts.pe_work(pe)

                @block.scalar
                def _(act):
                    begin(act, G_ready, V_ready, prob_ready, xnT_ready, *route.of_act)
                    nc.scalar.activation(warm[:, :], half[:, :], ACT.Exp)
                    ahead.act_evacuate(act, 0, 0, xnT_ready)

                    def evac_G(b, u, h):
                        act.wait_ge(G_done, START + b * HA + h + 1)
                        act.wait_ge(scores_ready, START + b * ND + NT * (h - 1))
                        nc.scalar.activation(G_hi[:, h % 2, :], bankG[:, T - P:], ACT.Copy)
                        nc.scalar.activation(G_sb[:, h % 2, :], bankG[:, 0:T - P], ACT.Copy).then_inc(G_ready, 1)

                    def evac_V(b, u, g, i):
                        n = g * NT + i
                        act.wait_ge(V_done, START + b * (NT * 4) + n + 1)
                        act.wait_ge(Vs_ready, START + b * ND + 4 * NT * max(g - 1, 0))
                        nc.scalar.activation(Vraw[:, g % 2, i, :, :],
                                             bankV[n % 2][:, :].rearrange("p (h e) -> p h e", e=D),
                                             ACT.Copy).then_inc(V_ready, 1)

                    def row(b, u):
                        for n in range(ND):
                            if n == 0:
                                evac_G(b, u, 0)
                                for i in range(NT):
                                    evac_V(b, u, 0, i)
                                evac_G(b, u, 1)
                            elif n % NT == 0 and n // NT + 1 < HA:
                                evac_G(b, u, n // NT + 1)
                            if n % NT == 2 and n // NT < HA - 4:
                                evac_V(b, u, n // NT // 4 + 1, n // NT % 4)
                            h, i = step(n)
                            act.wait_ge(negmax_ready, START + b * ND + n + 1)
                            nc.scalar.activation(prob[:, h % 2, start[i]:start[i] + width[i]],
                                                 bankS[n % 3][:, 0:width[i]], ACT.Exp, scale=-1.0,
                                                 bias=negmax[:, n % 8:n % 8 + 1],
                                                 accum_out=rowsum[:, n % 8:n % 8 + 1]).then_inc(prob_ready, 1)
                            if n == ROUTE_TR and not is_row(b, 0):
                                route.norm.act_evacuate(act, b - 1, 1 - u, route.xnT_ready)
                            if n == ROUTE_EXP and not is_row(b, 0):
                                route.act_exp(act, b - 1, 1 - u)
                            if n == EVAC_AT and not is_row(b, B - 1):
                                ahead.act_evacuate(act, b + 1, 1 - u, xnT_ready)

                    each_row(act, row)
                    route.norm.act_evacuate(act, B - 1, 1, route.xnT_ready)
                    route.act_exp(act, B - 1, 1)
                    folding.act(act)
                    experts.fill(act, range(E // 2, E), experts.filled[1])
                    experts.act_work(act)

                @block.vector
                def _(dve):
                    begin(dve, negmax_ready, G_lo_ready, rinv_ready, Vs_ready, x_done, *ahead.of_dve, *route.of_dve)
                    route.dve_begin(dve)
                    folding.dve_early(dve)
                    dve.wait_ge(s_xload, 16 * B)
                    ahead.dve_stats(dve, 0, 0)
                    ahead.dve_normalise(dve, 0, 0)
                    ahead.dve_low(dve, 0, 0, xnT_ready)

                    def low_G(b, u, h):
                        dve.wait_ge(G_ready, START + b * HA + h + 1)
                        nc.vector.tensor_tensor(G_lo[:, h % 2, :], bankG[:, T - P:], G_hi[:, h % 2, :],
                                                ALU.subtract).then_inc(G_lo_ready, 1)

                    def route_stats(b, u):
                        dve.wait_ge(x_done, START + b + 1)
                        dve.sem_inc(x_complete, 1)
                        route.norm.dve_stats(dve, b, u)

                    def row(b, u):
                        for n in range(ND + 2):
                            if n == 0:
                                low_G(b, u, 0)
                                low_G(b, u, 1)
                            elif n < ND and n % NT == 0 and n // NT + 1 < HA:
                                low_G(b, u, n // NT + 1)
                            if n < ND:
                                h, i = step(n)
                                dve.wait_ge(scores_ready, START + b * ND + n + 1)
                                dve.sem_inc(scores_seen, 1)
                                scores = bankS[n % 3][:, 0:width[i]]
                                nc.vector.tensor_tensor_reduce(
                                    out=scores, in0=scores, in1=mask[:, T - width[i]:], scale=-1.0, scalar=HUGE,
                                    op0=ALU.add, op1=ALU.min,
                                    accum_out=negmax[:, n % 8:n % 8 + 1]).then_inc(negmax_ready, 1)
                            if 1 <= n <= ND:
                                m = n - 1
                                dve.wait_ge(prob_ready, START + b * ND + m + 1)
                                nc.vector.reciprocal(rinv[:, m % 8:m % 8 + 1],
                                                     rowsum[:, m % 8:m % 8 + 1]).then_inc(rinv_ready, 1)
                            if n >= 2:
                                m = n - 2
                                h, i = step(m)
                                dve.wait_ge(rinv_ready, START + b * ND + m + 1)
                                dve.wait_ge(V_ready, START + b * (NT * 4) + (h // 4) * NT + i + 1)
                                nc.vector.tensor_scalar(Vs[:, m % 8, :], Vraw[:, h // 4 % 2, i, h % 4, :],
                                                        rinv[:, m % 8:m % 8 + 1], None,
                                                        ALU.mult).then_inc(Vs_ready, 1)
                            if not is_row(b, 0):
                                if n == ROUTE_STATS:
                                    route_stats(b - 1, 1 - u)
                                if n == ROUTE_NORM:
                                    route.dve_normalise(dve, b - 1, 1 - u)
                                if n in ROUTE_DVE:
                                    ROUTE_DVE[n](dve, b - 1, 1 - u)
                            if n == STATS_AT and not is_row(b, B - 1):
                                ahead.dve_stats(dve, b + 1, 1 - u)
                            if n == LOW_AT and not is_row(b, B - 1):
                                ahead.dve_low(dve, b + 1, 1 - u, xnT_ready)
                            if n == NORM_AT and not is_row(b, B - 1):
                                dve.wait_ge(row_done, START + b)
                                ahead.dve_normalise(dve, b + 1, 1 - u)
                        dve.wait_ge(row_done, START + b + 1)
                        tiles = x_sb[:, bass.ds(b * NT, NT), :]
                        nc.vector.tensor_tensor(tiles, tiles,
                                                bankO[:, :].rearrange("p (t e) -> p t e", e=D),
                                                ALU.add).then_inc(x_done, 1)

                    each_row(dve, row)
                    route_stats(B - 1, 1)
                    route.dve_normalise(dve, B - 1, 1)
                    for step_of in ROUTE_DVE.values():
                        step_of(dve, B - 1, 1)
                    experts.dve_plan(dve)
                    folding.dve(dve)
                    dve.wait_ge(folding.moe_copied, 2)
                    experts.dve_work(dve)

                @block.gpsimd
                def _(pool):
                    begin(pool, *ahead.of_pool, *route.of_pool)
                    ahead.pool_rstd(pool, 0, 0)
                    prime(pool, *route.scattered)

                    def row(b, u):
                        if not is_row(b, 0):
                            route.norm.pool_rstd(pool, b - 1, 1 - u)
                            route.pool_scatter(pool, b - 1, 1 - u)
                        if not is_row(b, B - 1):
                            ahead.pool_rstd(pool, b + 1, 1 - u)

                    each_row(pool, row)
                    route.norm.pool_rstd(pool, B - 1, 1)
                    route.pool_scatter(pool, B - 1, 1)
                    experts.pool_work(pool)

                @block.sync
                def _(sp):
                    experts.fill(sp, range(E // 2), experts.filled[0])
                    experts.sp_work(sp, route)

        head_weights.close()

        class Combine:

            def __init__(self, name, at, ring):
                self.ring = ring
                self.rows = sb(name + "_crows", [P, ring, TOP, NT, D], at=at)
                self.loaded = [sem(f"{name}_rows_loaded{u}", at) for u in range(ring)]
                self.added = sem(name + "_experts_added", at)
                self.all_added = sem(name + "_row_added", at)
                self.of_sp = self.loaded
                self.of_dve = (self.added,)

            def load(self, sp, b, u, of=None):
                if not isinstance(b, int) or b >= self.ring:
                    sp.wait_ge(self.added, START + (b + 1 - self.ring) * TOP * NT)
                for k in range(TOP):
                    first = (b if of is None else of) * T + k * B * T
                    sp.dma_start(self.rows[:, u, k, :, :],
                                 yg[bass.ds(first, T), :].rearrange("(t p) d -> p t d", p=P)
                                 ).then_inc(self.loaded[u], 16)

            def dve_add(self, dve, b, u, k):
                if k == 0:
                    dve.wait_ge(self.loaded[u], START + (b - u) * (16 * TOP // self.ring) + 16 * TOP)
                else:
                    dve.wait_ge(self.added, START + b * TOP * NT + k * NT)
                for t in range(NT):
                    tile = x_sb[:, bass.ds(b * NT + t, 1), :]
                    nc.vector.scalar_tensor_tensor(
                        out=tile, in0=self.rows[:, u, k, t:t + 1, :], scalar=gates[:, bass.ds(b * NT + t, 1), k],
                        in1=tile, op0=ALU.mult, op1=ALU.add).then_inc(self.added, 1)

            def dve_complete(self, dve, b):
                dve.wait_ge(self.added, START + (b + 1) * TOP * NT)
                dve.sem_inc(self.all_added, 1)

        def combine_stage():
            with stage() as st:
                RING = 4
                combine = Combine("c", st, RING)
                with nc.Block() as block:
                    @block.sync
                    def _(sp):
                        begin(sp, *combine.of_sp)
                        for b in range(RING):
                            combine.load(sp, b, b)
                        with sp.Fori(0, B // RING - 1) as pass_:
                            for u in range(RING):
                                combine.load(sp, pass_ * RING + RING + u, u)

                    @block.vector
                    def _(dve):
                        begin(dve, *combine.of_dve)
                        with dve.Fori(0, B // RING) as pass_:
                            for u in range(RING):
                                for k in range(TOP):
                                    combine.dve_add(dve, pass_ * RING + u, u, k)

                    @block.scalar
                    def _(act):
                        with act.Fori(0, B) as b:
                            act.wait_ge(combine.added, START + (b + 1) * TOP * NT)
                            act.dma_start(out[bass.ds(b, 1)].rearrange("o (t p) e -> p (o t) e", p=P),
                                          x_sb[:, bass.ds(b * NT, NT), :]).then_inc(s_store, 16)
                        act.wait_ge(s_store, 16 * B)

        def linear_attention_stage():
            with stage() as st:
                ahead = Ahead("b", st, LN_LN, x_sb, attn_norm_col, None, want_htok=True, split=True)
                GR = 2
                NS = NT * GR
                V_sb = sb("V_sb", [P, NT, HB * DB], at=st)
                G_sb = sb("Gb_sb", [P, 2, HB, T], at=st)
                R_sb = sb("R_sb", [P, GR, 4 * DB], at=st)
                AT_sb = sb("AT_sb", [P, 2, 4, P], at=st)
                o_sb = sb("o_sb", [P, 2, 4, DB], at=st)
                oT_sb = sb("oT_sb", [P, 2, 4 * P], at=st)
                junk = sb("junk", [P, 2, 4, DB], at=st)
                ss = sb("ss", [P, 2, 4], at=st)
                ms = sb("ms", [P, 2, 4], at=st)
                ro = sb("ro", [P, 2, 4, 1], at=st)
                bankW, bankOo, bankRr, bankZ = bank[1:3], bank[3:5], bank[5:7], bank[7]

                xnT_ready = sem("b_xnT_ready", st)
                proj_done = sem("b_proj_done", st)
                v_ready, G_ready = sem("b_v_ready", st), sem("b_G_ready", st)
                att_done, att_ready = sem("b_att_done", st), sem("b_att_ready", st)
                o_done = sem("b_o_done", st)
                squares = sem("b_squares", st)
                pool_root = sem("b_pool_root", st)
                root_ready = sem("b_root_ready", st)
                o_ready = sem("b_o_ready", st)
                oT_done, oT_ready = sem("b_oT_done", st), sem("b_oT_ready", st)
                R_done = [sem(f"b_R_done{g}", st) for g in range(GR)]
                R_ready = [sem(f"b_R_ready{g}", st) for g in range(GR)]
                row_done = sem("b_row_done", st)
                z_done = sem("b_z_done", st)

                early = [("v", 0, 0), ("v", 0, 1)] + [("G", h) for h in range(4)]
                after = {0: [("G", h) for h in range(4, 8)], 7: [],
                          8: [("next", 0), ("next", 1)], 9: [("next", 2), ("next", 3), ("next", 4)], 10: [("next", 5)]}
                for i in range(1, NT):
                    after[2 * i - 2] = after.get(2 * i - 2, []) + [("v", i, 0), ("v", i, 1)]
                uses = []
                for s in range(NS + 3):
                    uses += ([("att", s)] if s < NS else []) + after.get(s, [])
                late = [x for x in uses if x[0] in ("v", "G")]
                proj_index = {x: k for k, x in enumerate(early + late)}
                NPROJ = len(proj_index)
                assert len(uses) % 2 == 0 and len(early) % 2 == 0
                COMBINE_AT, RSTD_AT, NORM_AT, AHEAD_AT = 0, 2, 4, 5

                def projected(b, use):
                    if use[0] == "next":
                        return (b + 1) * NPROJ + use[1] + 1
                    return b * NPROJ + proj_index[use] + 1

                def wait_copied(eng, b, use):
                    if use[0] == "next":
                        b, use = b + 1, early[use[1]]
                    if use[0] == "v":
                        eng.wait_ge(v_ready, START + b * (NT * GR) + use[1] * GR + use[2] + 1)
                    else:
                        eng.wait_ge(G_ready, START + b * HB + use[1] + 1)

                combine = Combine("b", st, 2)

                with nc.Block() as block:
                    @block.tensor
                    def _(pe):
                        begin(pe, proj_done, att_done, o_done, oT_done, *R_done, row_done, ahead.tr)
                        ahead.pe_transpose(pe, 0, 0)

                        def claim(b, use):
                            k = uses.index(use)
                            last = uses[k - 2]
                            if last[0] == "att":
                                pe.wait_ge(att_ready, START + b * NS + last[1] + 1)
                            else:
                                wait_copied(pe, b - 1 if k < 2 else b, last)
                            return bankW[k % 2]

                        def product(ps, u, use):
                            if use[0] == "v":
                                _, i, g = use
                                tile, four = slice(i * P, (i + 1) * P), slice(g * 512, (g + 1) * 512)
                                mm = matmul3(ps[:, :], ahead.hi[:, u, tile], ahead.lo[:, u, tile], Wv_hi[:, four],
                                             Wv_lo[:, four])
                            else:
                                mm = matmul3(ps[:, :], A_hi[:, use[1], :], A_lo[:, use[1], :], ahead.hi[:, u, :],
                                             ahead.lo[:, u, :])
                            mm.then_inc(proj_done, 1)

                        def project(b, u, use):
                            if use[0] == "next":
                                if use[1] == 0:
                                    pe.wait_ge(ahead.lo_ready, START + b + 2)
                                product(claim(b, use), 1 - u, early[use[1]])
                            else:
                                product(claim(b, use), u, use)

                        def scores(b, u, s):
                            i, g = divmod(s, GR)
                            ps = claim(b, ("att", s))
                            wait_copied(pe, b, ("G", 4 * g + 3))
                            nc.tensor.matmul(ps[:, :].rearrange("p (h i) -> p h i", i=P),
                                             ahead.xnT[:, u, i * P:(i + 1) * P],
                                             G_sb[:, u, 4 * g:4 * g + 4, i * P:(i + 1) * P],
                                             start=True, stop=True).then_inc(att_done, 1)

                        def outputs(b, u, s):
                            i, g = divmod(s, GR)
                            pe.wait_ge(o_ready, START + b * NS + s - 1)
                            pe.wait_ge(att_ready, START + b * NS + s + 1)
                            wait_copied(pe, b, ("v", i, g))
                            if i > 0:
                                pe.wait_ge(R_ready[g], START + b * (NT - 1) + i)
                            for m in range(4):
                                h = 4 * g + m
                                o = bankOo[s % 2][:, m * DB:(m + 1) * DB]
                                mm = nc.tensor.matmul(o, AT_sb[:, s % 2, m, :], V_sb[:, i, h * DB:(h + 1) * DB],
                                                      start=True, stop=(i == 0))
                                if i > 0:
                                    mm = nc.tensor.matmul(o, G_sb[:, u, h, i * P:(i + 1) * P],
                                                          R_sb[:, g, m * DB:(m + 1) * DB], start=False, stop=True)
                            mm.then_inc(o_done, 1)

                        def state(b, u, s):
                            i, g = divmod(s, GR)
                            if i == NT - 1:
                                return
                            if s == 0:
                                pe.wait_ge(ahead.htok, START + b + 1)
                            pe.wait_ge(R_ready[g], START + b * (NT - 1) + i)
                            nc.tensor.matmul(bankRr[g][:, :], ahead.htok_sb[:, u, i, :],
                                             V_sb[:, i, g * 512:(g + 1) * 512],
                                             start=(i == 0), stop=(i == NT - 2),
                                             skip_group_check=True).then_inc(R_done[g], 1)

                        def transposes(b, u, s):
                            pe.wait_ge(o_ready, START + b * NS + s + 1)
                            pe.wait_ge(oT_ready, START + b * NS + s)
                            if s == AHEAD_AT - 1:
                                pe.wait_ge(xnT_ready, START + b + 2)
                            for m in range(4):
                                mm = nc.tensor.transpose(bank[0][:, m * P:(m + 1) * P], o_sb[:, s % 2, m, :],
                                                         ident[:, :])
                            mm.then_inc(oT_done, 1)

                        def project_out(b, u, s):
                            i, g = divmod(s, GR)
                            if s == 0:
                                pe.wait_ge(z_done, START + b)
                            pe.wait_ge(oT_ready, START + b * NS + s + 1)
                            for m in range(4):
                                mm = nc.tensor.matmul(bankZ[:, i * D:(i + 1) * D], oT_sb[:, s % 2, m * P:(m + 1) * P],
                                                      Wo_sb[:, 4 * g + m, :], start=(g == 0 and m == 0),
                                                      stop=(g == GR - 1 and m == 3))
                            if s == NS - 1:
                                mm.then_inc(row_done, 1)

                        pe.wait_ge(ahead.lo_ready, START + 1)
                        for k, use in enumerate(early):
                            if k >= 2:
                                wait_copied(pe, 0, early[k - 2])
                            product(bankW[k % 2], 0, use)
                        with pe.Fori(0, B // 2) as pair:
                            for u in range(2):
                                b = pair * 2 + u
                                for s in range(NS + 3):
                                    if s < NS:
                                        scores(b, u, s)
                                    for use in after.get(s, []):
                                        project(b, u, use)
                                    if 1 <= s <= NS:
                                        outputs(b, u, s - 1)
                                        state(b, u, s - 1)
                                    if 2 <= s <= NS + 1:
                                        transposes(b, u, s - 2)
                                    if s == AHEAD_AT:
                                        pe.wait_ge(oT_ready, START + b * NS + AHEAD_AT - 1)
                                        ahead.pe_transpose(pe, b + 1, 1 - u)
                                    if s >= 3:
                                        project_out(b, u, s - 3)

                    @block.scalar
                    def _(act):
                        begin(act, xnT_ready, G_ready, squares, oT_ready, *R_ready)
                        ahead.act_evacuate(act, 0, 0, xnT_ready)

                        def copy_G(ps, u, use):
                            nc.scalar.activation(G_sb[:, u, use[1], :], ps[:, :], ACT.Copy).then_inc(G_ready, 1)

                        def copy_out(b, u, use):
                            mine = early[use[1]] if use[0] == "next" else use
                            if mine[0] == "G":
                                act.wait_ge(proj_done, START + projected(b, use))
                                copy_G(bankW[uses.index(use) % 2], 1 - u if use[0] == "next" else u, mine)

                        for k, use in enumerate(early):
                            if use[0] == "G":
                                act.wait_ge(proj_done, START + k + 1)
                                copy_G(bankW[k % 2], 0, use)
                        with act.Fori(0, B // 2) as pair:
                            for u in range(2):
                                b = pair * 2 + u
                                for s in range(NS + 3):
                                    for use in after.get(s, []):
                                        copy_out(b, u, use)
                                    if 1 <= s <= NS:
                                        r = s - 1
                                        i, g = divmod(r, GR)
                                        act.wait_ge(o_done, START + b * NS + r + 1)
                                        for m in range(4):
                                            ins = nc.scalar.activation(junk[:, r % 2, m, :],
                                                                       bankOo[r % 2][:, m * DB:(m + 1) * DB],
                                                                       ACT.Square, accum_out=ss[:, r % 2, m:m + 1])
                                        ins.then_inc(squares, 1)
                                        if i < NT - 1:
                                            act.wait_ge(R_done[g], START + b * (NT - 1) + i + 1)
                                            nc.scalar.activation(R_sb[:, g, :], bankRr[g][:, :],
                                                                 ACT.Copy).then_inc(R_ready[g], 1)
                                    if 2 <= s <= NS + 1:
                                        r = s - 2
                                        act.wait_ge(oT_done, START + b * NS + r + 1)
                                        nc.scalar.activation(oT_sb[:, r % 2, :], bank[0][:, :],
                                                             ACT.Copy).then_inc(oT_ready, 1)
                                    if s == AHEAD_AT:
                                        ahead.act_evacuate(act, b + 1, 1 - u, xnT_ready)

                    @block.sync
                    def _(sp):
                        begin(sp, *combine.of_sp)
                        combine.load(sp, 0, 0)
                        combine.load(sp, 1, 1)
                        with sp.Fori(0, B // 2 - 1) as pair:
                            for u in range(2):
                                combine.load(sp, pair * 2 + 2 + u, u)
                        combine.load(sp, B, 0, of=0)

                    @block.gpsimd
                    def _(pool):
                        begin(pool, pool_root, root_ready, *ahead.of_pool)
                        ahead.pool_rstd(pool, 0, 0)
                        ahead.pool_finish(pool, 0, 0)
                        with pool.Fori(0, B // 2) as pair:
                            for u in range(2):
                                b = pair * 2 + u
                                for s in range(NS):
                                    n = b * NS + s
                                    pool.wait_ge(squares, START + n + 1)
                                    nc.gpsimd.tensor_tensor(ms[:, s % 2, :], ss[:, s % 2, :], per_dim[:, :],
                                                            ALU.mult).then_inc(pool_root, 1)
                                    pool.wait_ge(pool_root, START + 2 * n + 1)
                                    nc.gpsimd.tensor_tensor(ms[:, s % 2, :], ms[:, s % 2, :], eps[:, :],
                                                            ALU.add).then_inc(pool_root, 1)
                                    pool.wait_ge(pool_root, START + 2 * n + 2)
                                    nc.gpsimd.tensor_tensor(ro[:, s % 2, :, 0], ms[:, s % 2, :], half[:, :],
                                                            ALU.pow).then_inc(root_ready, 1)
                                    if s == RSTD_AT:
                                        ahead.pool_rstd(pool, b + 1, 1 - u)
                                    if s == NORM_AT:
                                        ahead.pool_finish(pool, b + 1, 1 - u)

                    @block.vector
                    def _(dve):
                        begin(dve, v_ready, att_ready, o_ready, z_done, *combine.of_dve, *ahead.of_dve)
                        for k in range(TOP):
                            combine.dve_add(dve, 0, 0, k)
                        combine.dve_complete(dve, 0)
                        ahead.dve_stats(dve, 0, 0)
                        ahead.dve_normalise(dve, 0, 0)
                        ahead.dve_low(dve, 0, 0, xnT_ready)

                        def copy_v(ps, use):
                            _, i, g = use
                            nc.vector.tensor_copy(V_sb[:, i, g * 512:(g + 1) * 512], ps[:, :]).then_inc(v_ready, 1)

                        for k, use in enumerate(early):
                            if use[0] == "v":
                                dve.wait_ge(proj_done, START + k + 1)
                                copy_v(bankW[k % 2], use)
                        with dve.Fori(0, B // 2) as pair:
                            for u in range(2):
                                b = pair * 2 + u
                                for s in range(NS + 2):
                                    if s < NS:
                                        k = uses.index(("att", s))
                                        dve.wait_ge(att_done, START + b * NS + s + 1)
                                        nc.vector.tensor_tensor(
                                            AT_sb[:, s % 2, :, :],
                                            bankW[k % 2][:, :].rearrange("p (h i) -> p h i", i=P),
                                            keep[:, :].unsqueeze(1).to_broadcast([P, 4, P]),
                                            ALU.mult).then_inc(att_ready, 1)
                                    for use in after.get(s, []):
                                        mine = early[use[1]] if use[0] == "next" else use
                                        if mine[0] == "v":
                                            dve.wait_ge(proj_done, START + projected(b, use))
                                            copy_v(bankW[uses.index(use) % 2], mine)
                                    if s >= 2:
                                        r = s - 2
                                        dve.wait_ge(root_ready, START + b * NS + r + 1)
                                        nc.vector.tensor_tensor(
                                            o_sb[:, r % 2, :, :],
                                            bankOo[r % 2][:, :].rearrange("p (h v) -> p h v", v=DB),
                                            ro[:, r % 2, :, :].to_broadcast([P, 4, DB]),
                                            ALU.mult).then_inc(o_ready, 1)
                                    if s == COMBINE_AT:
                                        combine.dve_add(dve, b + 1, 1 - u, 0)
                                    if s == COMBINE_AT + 1:
                                        combine.dve_add(dve, b + 1, 1 - u, 1)
                                    if s == COMBINE_AT + 2:
                                        combine.dve_complete(dve, b + 1)
                                        ahead.dve_stats(dve, b + 1, 1 - u)
                                    if s == NORM_AT:
                                        dve.wait_ge(row_done, START + b)
                                        ahead.dve_normalise(dve, b + 1, 1 - u)
                                    if s == AHEAD_AT + 1:
                                        ahead.dve_low(dve, b + 1, 1 - u, xnT_ready)
                                dve.wait_ge(row_done, START + b + 1)
                                nc.vector.tensor_tensor(z_sb[:, bass.ds(b * NT, NT), :], ahead.y_sb[:, u, :, :],
                                                        bankZ[:, :].rearrange("p (t e) -> p t e", e=D),
                                                        ALU.add).then_inc(z_done, 1)

        def mlp_stage():
            with stage() as st:
                ahead = Ahead("m", st, RMS, z_sb, mlp_norm_col, None, want_sum=True)
                C = INTER // P
                silu = sb("silu", [P, 2, T], at=st)
                act_h = sb("act_h", [P, 2, C, T], at=st)
                warm = sb("m_warm", [P, NT], at=st)
                bankG, bankU, bankD = bank[1:3], bank[3:5], bank[5:7]
                route = Route("f2", st, bank[7])
                experts = Experts("f2", st)
                xnT_ready = sem("m_xnT_ready", st)
                gate_done, up_done = sem("m_gate_done", st), sem("m_up_done", st)
                silu_ready, act_ready = sem("m_silu_ready", st), sem("m_act_ready", st)
                row_done = sem("m_row_done", st)
                x_done = sem("m_x_done", st)
                x_complete = sem("m_x_complete", st)

                def each_row_of_m(eng, row):
                    row(0, 0)
                    row(1, 1)
                    with eng.Fori(0, B // 2 - 1) as pair:
                        row(pair * 2 + 2, 0)
                        row(pair * 2 + 3, 1)

                with nc.Block() as block:
                    @block.tensor
                    def _(pe):
                        begin(pe, gate_done, up_done, row_done, ahead.tr, *route.of_pe)
                        ahead.pe_transpose(pe, 0, 0)

                        def row(b, u):
                            route_too = not is_row(b, 0)
                            pe.wait_ge(xnT_ready, START + b + 1)
                            for c in range(C):
                                n = b * C + c
                                pe.wait_ge(silu_ready, START + n - 1)
                                nc.tensor.matmul(bankG[c % 2][:, :], Wgate_sb[:, c * P:(c + 1) * P],
                                                 ahead.xnT[:, u, :], start=True, stop=True).then_inc(gate_done, 1)
                                pe.wait_ge(act_ready, START + n - 1)
                                nc.tensor.matmul(bankU[c % 2][:, :], Wup_sb[:, c * P:(c + 1) * P],
                                                 ahead.xnT[:, u, :], start=True, stop=True).then_inc(up_done, 1)
                                if c == 2 and route_too:
                                    route.norm.pe_transpose(pe, b - 1, 1 - u)
                            if route_too:
                                route.pe_logits(pe, b - 1, 1 - u)
                            pe.wait_ge(act_ready, START + (b + 1) * C)
                            pe.wait_ge(x_done, START + b)
                            for t in range(NT):
                                for c in range(C):
                                    mm = nc.tensor.matmul(bankD[u][:, t * D:(t + 1) * D],
                                                          act_h[:, u, c, t * P:(t + 1) * P], Wdown_sb[:, c, :],
                                                          start=(c == 0), stop=(c == C - 1))
                            mm.then_inc(row_done, 1)
                            ahead.pe_transpose(pe, b + 1, 1 - u)
                            if route_too:
                                route.pe_rank(pe, b - 1, 1 - u)

                        each_row_of_m(pe, row)
                        route.norm.pe_transpose(pe, B - 1, 1)
                        route.pe_logits(pe, B - 1, 1)
                        route.pe_rank(pe, B - 1, 1)
                        experts.pe_count(pe, route)
                        pe.wait_ge(silu_ready, START + B * C)
                        pe.wait_ge(act_ready, START + B * C)
                        experts.pe_work(pe)

                    @block.scalar
                    def _(act):
                        begin(act, xnT_ready, silu_ready, *route.of_act)
                        nc.scalar.activation(warm[:, :], half[:, :], ACT.Silu)
                        ahead.act_evacuate(act, 0, 0, xnT_ready)

                        def row(b, u):
                            for c in range(C):
                                n = b * C + c
                                act.wait_ge(gate_done, START + n + 1)
                                act.wait_ge(act_ready, START + n - 1)
                                nc.scalar.activation(silu[:, c % 2, :], bankG[c % 2][:, :],
                                                     ACT.Silu).then_inc(silu_ready, 1)
                            if not is_row(b, 0):
                                route.norm.act_evacuate(act, b - 1, 1 - u, route.xnT_ready)
                                route.act_exp(act, b - 1, 1 - u)
                            nc.scalar.activation(warm[:, :], half[:, :], ACT.Silu)
                            ahead.act_evacuate(act, b + 1, 1 - u, xnT_ready)

                        each_row_of_m(act, row)
                        route.norm.act_evacuate(act, B - 1, 1, route.xnT_ready)
                        route.act_exp(act, B - 1, 1)
                        experts.fill(act, range(E // 2, E), experts.filled[1])
                        experts.act_work(act)

                    @block.vector
                    def _(dve):
                        begin(dve, act_ready, x_done, *ahead.of_dve, *route.of_dve)
                        route.dve_begin(dve)
                        ahead.dve_stats(dve, 0, 0)
                        ahead.dve_normalise(dve, 0, 0)

                        def route_stats(b, u):
                            dve.wait_ge(x_done, START + b + 1)
                            dve.sem_inc(x_complete, 1)
                            route.norm.dve_stats(dve, b, u)

                        def route_select(b, u):
                            for part in (route.dve_top, route.dve_topid, route.dve_ids, route.dve_is_k, route.dve_sel,
                                         route.dve_row_sel):
                                part(dve, b, u)

                        def route_place(b, u):
                            for part in (route.dve_place, route.dve_picked, route.dve_slotf, route.dve_slots):
                                part(dve, b, u)

                        def row(b, u):
                            route_too = not is_row(b, 0)
                            if route_too:
                                route_stats(b - 1, 1 - u)
                            for c in range(C):
                                n = b * C + c
                                dve.wait_ge(silu_ready, START + n + 1)
                                dve.wait_ge(up_done, START + n + 1)
                                nc.vector.tensor_tensor(act_h[:, u, c, :], bankU[c % 2][:, :],
                                                        silu[:, c % 2, :], ALU.mult).then_inc(act_ready, 1)
                                if c == 0:
                                    ahead.dve_stats(dve, b + 1, 1 - u)
                                if c == 1 and route_too:
                                    route.dve_normalise(dve, b - 1, 1 - u)
                                if c == 3:
                                    dve.wait_ge(row_done, START + b)
                                    ahead.dve_normalise(dve, b + 1, 1 - u)
                            if route_too:
                                route.dve_logit(dve, b - 1, 1 - u)
                                route.dve_rmax(dve, b - 1, 1 - u)
                                route.dve_shift(dve, b - 1, 1 - u)
                                route_select(b - 1, 1 - u)
                            dve.wait_ge(row_done, START + b + 1)
                            dve.wait_ge(ahead.sum, START + b + 1)
                            nc.vector.tensor_tensor(x_sb[:, bass.ds(b * NT, NT), :], ahead.sum_sb[:, u, :, :],
                                                    bankD[u][:, :].rearrange("p (t e) -> p t e", e=D),
                                                    ALU.add).then_inc(x_done, 1)
                            if route_too:
                                route_place(b - 1, 1 - u)

                        each_row_of_m(dve, row)
                        route_stats(B - 1, 1)
                        route.dve_normalise(dve, B - 1, 1)
                        route.dve_logit(dve, B - 1, 1)
                        route.dve_rmax(dve, B - 1, 1)
                        route.dve_shift(dve, B - 1, 1)
                        route_select(B - 1, 1)
                        route_place(B - 1, 1)
                        experts.dve_plan(dve)
                        experts.dve_work(dve)

                    @block.gpsimd
                    def _(pool):
                        begin(pool, *ahead.of_pool, *route.of_pool)
                        ahead.pool_rstd(pool, 0, 0)
                        ahead.pool_finish(pool, 0, 0)
                        prime(pool, *route.scattered)

                        def row(b, u):
                            early = is_row(b, 0) or is_row(b, 1)
                            if not is_row(b, 0):
                                route.norm.pool_rstd(pool, b - 1, 1 - u)
                            ahead.pool_rstd(pool, b + 1, 1 - u)
                            if not early:
                                route.pool_scatter(pool, b - 2, u)
                            ahead.pool_finish(pool, b + 1, 1 - u)

                        each_row_of_m(pool, row)
                        route.norm.pool_rstd(pool, B - 1, 1)
                        route.pool_scatter(pool, B - 2, 0)
                        route.pool_scatter(pool, B - 1, 1)
                        experts.pool_work(pool)

                    @block.sync
                    def _(sp):
                        experts.fill(sp, range(E // 2), experts.filled[0])
                        experts.sp_work(sp, route)

        linear_attention_stage()
        mlp_stage()
        combine_stage()


_INS = ["L0_attn_a_x", "L0_attn_a_W_K", "L0_attn_a_W_Q", "L0_attn_a_W_V", "L0_attn_a_W_O",
        "L0_attn_b_attn_norm_w", "L0_attn_b_Wq", "L0_attn_b_Wk", "L0_attn_b_Wv", "L0_attn_b_Wo",
        "L0_attn_b_attn_out_norm_w", "L0_attn_b_mlp_norm_w", "L0_attn_b_Wgate", "L0_attn_b_Wup",
        "L0_attn_b_Wdown", "L0_ffn_gamma", "L0_ffn_beta", "L0_ffn_Wr", "L0_ffn_br", "L0_ffn_W1",
        "L0_ffn_b1", "L0_ffn_W2", "L0_ffn_b2"]


def kernel(**inputs):
    import numpy as _np
    import concourse.bacc as _bacc
    from concourse import mybir as _mybir
    from concourse.bass_utils import run_bass_kernel_spmd as _run

    nc = _bacc.Bacc("TRN2", target_bir_lowering=False, num_devices=1)
    arrays, args = {}, []
    for name in _INS:
        a = _np.ascontiguousarray(inputs[name])
        arrays[f"in_{name}_dram"] = a
        args.append(nc.dram_tensor(f"in_{name}_dram", a.shape, _mybir.dt.from_np(a.dtype), kind="ExternalInput").ap())
    args.append(nc.dram_tensor("out_dram", (B, T, D), f32, kind="ExternalOutput").ap())
    build_hybrid(nc, *args)
    r = _run(nc, [arrays], core_ids=[0])
    return r.results[0]["out_dram"]
```
